# Optimizing a Trainium2 kernel written in Bass

```python
import numpy as np
import jax
import jax.numpy as jnp

def _softmax(x, axis=-1):
    return jax.nn.softmax(x, axis=axis)

def _gelu(x):
    return jax.nn.gelu(x, approximate=True)

def _silu(x):
    return jax.nn.silu(x)

def _sigmoid(x):
    return jax.nn.sigmoid(x)

def _layernorm(x, axis=-1, eps=1e-05):
    m = jnp.mean(x, axis=axis, keepdims=True)
    v = jnp.var(x, axis=axis, keepdims=True)
    return (x - m) / jnp.sqrt(v + eps)

def _scatter_add(tgt, idx, src, axis=0):
    return tgt.at[idx].add(src)

def _segment_sum(src, seg, n):
    return jax.ops.segment_sum(src, seg, n)
kernel_name = 'mk_adaln_attn_ffn_d1_seqx_r4_aaa5e3'

def setup_inputs(seed: int=0):
    np.random.seed(seed)
    _w = jnp.asarray

    def _rec_inputs():
        import jax
        import jax.numpy as jnp
        _rk = jax.random.key(seed)
        x = 7.22e-05 + 1 * jax.random.normal(jax.random.fold_in(_rk, 1), (64, 64, 256), jnp.float32)
        _lenS = 64 - jax.random.randint(jax.random.fold_in(_rk, 7), (64,), 0, max(1, 64 // 4) + 1, jnp.int32)
        _lenS2 = 64 - jax.random.randint(jax.random.fold_in(_rk, 8), (64,), 0, max(1, 64 // 4) + 1, jnp.int32)
        cond_64 = -0.104238 + 1.01173 * jax.random.normal(jax.random.fold_in(_rk, 11), (64, 64), jnp.float32)
        fside_16xSxS_0 = -5.72187e-05 + 0.999849 * jax.random.normal(jax.random.fold_in(_rk, 12), (16, 64, 64), jnp.float32)
        _validS = jnp.arange(64)[None, :] < _lenS[:, None]
        _validS2 = jnp.arange(64)[None, :] < _lenS2[:, None]
        _causal = jnp.tril(jnp.ones((64, 64), dtype=bool))
        mask_BxS_bk0 = jnp.logical_not(jnp.broadcast_to(_validS[:, :], (64, 64)))
        return (x, cond_64, fside_16xSxS_0, mask_BxS_bk0)
    x, cond_64, fside_16xSxS_0, mask_BxS_bk0 = _rec_inputs()

    def _L0_cond_setup():
        import jax, jax.numpy as jnp
        import numpy as np
        B, S, H = (4, 512, 256)
        E = 8
        M = 128
        K = 2
        N_SHARED = 2
        SM = M * N_SHARED
        G = 64
        GE_TEMP = 1.0
        ALPHA = 0.001
        SEQ_AUX = True
        NORM_TOPK = True
        COS_TEMP = 0.78
        CONS_ALPHA = 0.01
        LEAKY_SLOPE = 0.01
        EPS_COS = 1e-08

        def _leaky(x):
            return jnp.where(x >= 0, x, LEAKY_SLOPE * x)

        def _moe_forward(hidden_states, g, wt, wg, w_gate, w_up, w_down, sw_gate, sw_up, sw_down):
            b, s, h = hidden_states.shape
            x = hidden_states.reshape(-1, h)
            T = x.shape[0]
            logits_h = x @ wt.T
            logits_g = g @ wg.T
            logits_g = jnp.repeat(logits_g, s, axis=0)
            logits = (logits_h + logits_g / GE_TEMP) / (1.0 + 1.0 / GE_TEMP)
            scores = jax.nn.softmax(logits, axis=-1)
            topk_w, topk_idx = jax.lax.top_k(scores, K)
            if K > 1 and NORM_TOPK:
                topk_w = topk_w / (topk_w.sum(-1, keepdims=True) + 1e-20)
            onehot = jax.nn.one_hot(topk_idx.reshape(b, s * K), E, dtype=jnp.float32)
            ce = onehot.sum(1) / (s * K / E)
            aux_loss = (ce * scores.reshape(b, s, E).mean(1)).sum(1).mean() * ALPHA
            gp = _leaky(jnp.einsum('th,ehm->etm', x, w_gate))
            up = jnp.einsum('th,ehm->etm', x, w_up)
            y_all = jnp.einsum('etm,emh->eth', gp * up, w_down)
            y_sel = y_all[topk_idx, jnp.arange(T)[:, None], :]
            y = (y_sel * topk_w[..., None]).sum(1).reshape(b, s, h)
            p = _leaky(hidden_states @ sw_gate) * (hidden_states @ sw_up) @ sw_down
            y = y + p
            num = jnp.sum(y * p, -1)
            den = jnp.maximum(jnp.linalg.norm(y, axis=-1), EPS_COS) * jnp.maximum(jnp.linalg.norm(p, axis=-1), EPS_COS)
            closs = CONS_ALPHA * jnp.mean(num / den / (1.0 + COS_TEMP))
            return (y, aux_loss + closs)
        key = jax.random.key(seed)
        ks = jax.random.split(key, 12)
        sh = 1.0 / np.sqrt(H)
        sm = 1.0 / np.sqrt(M)
        ssm = 1.0 / np.sqrt(SM)
        sg = 1.0 / np.sqrt(G)
        return {'hidden_states': jax.random.normal(ks[0], (B, S, H), jnp.float32), 'g': jax.random.normal(ks[1], (B, G), jnp.float32), 'wt': jax.random.uniform(ks[2], (E, H), jnp.float32, -sh, sh), 'wg': jax.random.uniform(ks[3], (E, G), jnp.float32, -sg, sg), 'w_gate': jax.random.uniform(ks[4], (E, H, M), jnp.float32, -sh, sh), 'w_up': jax.random.uniform(ks[5], (E, H, M), jnp.float32, -sh, sh), 'w_down': jax.random.uniform(ks[6], (E, M, H), jnp.float32, -sm, sm), 'sw_gate': jax.random.uniform(ks[7], (H, SM), jnp.float32, -sh, sh), 'sw_up': jax.random.uniform(ks[8], (H, SM), jnp.float32, -sh, sh), 'sw_down': jax.random.uniform(ks[9], (SM, H), jnp.float32, -ssm, ssm)}
    _L0_cond_all = _L0_cond_setup()
    _L0_cond_in = {k: v for k, v in _L0_cond_all.items() if k in ('wt', 'wg', 'w_gate', 'w_up', 'w_down', 'sw_gate', 'sw_up', 'sw_down')}
    del _L0_cond_all

    def _L0_attn_setup():
        import jax, jax.numpy as jnp
        import numpy as np
        import math
        B, S, D, H = (2, 512, 256, 16)
        DK = D // H
        NUM_BUCKETS = 32
        MAX_DISTANCE = 128

        def _relative_position_bucket(relative_position, num_buckets=NUM_BUCKETS, max_distance=MAX_DISTANCE):
            nb = num_buckets // 2
            n = -relative_position
            ret = (n < 0).astype(jnp.int32) * nb
            n = jnp.abs(n)
            max_exact = nb // 2
            is_small = n < max_exact
            val_if_large = max_exact + (jnp.log(jnp.maximum(n, 1).astype(jnp.float32) / max_exact) / math.log(max_distance / max_exact) * (nb - max_exact)).astype(jnp.int32)
            val_if_large = jnp.minimum(val_if_large, nb - 1)
            return ret + jnp.where(is_small, n, val_if_large)
        key = jax.random.key(seed)
        ks = jax.random.split(key, 6)
        scale = 1.0 / math.sqrt(D)
        return {'hidden_states': jax.random.normal(ks[0], (B, S, D), dtype=jnp.float32), 'Wq': jax.random.normal(ks[1], (D, D), dtype=jnp.float32) * scale, 'Wk': jax.random.normal(ks[2], (D, D), dtype=jnp.float32) * scale, 'Wv': jax.random.normal(ks[3], (D, D), dtype=jnp.float32) * scale, 'Wo': jax.random.normal(ks[4], (D, D), dtype=jnp.float32) * scale, 'rel_emb': jax.random.normal(ks[5], (NUM_BUCKETS, H), dtype=jnp.float32) * 0.1}
    _L0_attn_all = _L0_attn_setup()
    _L0_attn_in = {k: v for k, v in _L0_attn_all.items() if k in ('Wq', 'Wk', 'Wv', 'Wo', 'rel_emb')}
    del _L0_attn_all

    def _L0_cond2_setup():
        import jax, jax.numpy as jnp
        import numpy as np
        B, N, DIM, H, DH = (2, 512, 256, 16, 64)
        INNER = H * DH
        EPS = 1e-05

        def layernorm(x, g):
            mean = jnp.mean(x, axis=-1, keepdims=True)
            var = jnp.var(x, axis=-1, keepdims=True)
            return (x - mean) * jax.lax.rsqrt(var + EPS) * g
        key = jax.random.key(seed)
        ks = jax.random.split(key, 10)
        x = jax.random.normal(ks[0], (B, N, DIM), dtype=jnp.float32)
        attn_bias = jax.random.normal(ks[1], (H, N, N), dtype=jnp.float32)
        mask = jax.random.randint(ks[2], (B, N), 0, 2).astype(bool)
        g_in = jnp.ones((DIM,), dtype=jnp.float32)
        null_attn_bias = jax.random.normal(ks[3], (H,), dtype=jnp.float32)
        null_kv = jax.random.normal(ks[4], (2, DH), dtype=jnp.float32)
        Wq = jax.random.normal(ks[5], (DIM, INNER), dtype=jnp.float32) * 0.02
        Wkv = jax.random.normal(ks[6], (DIM, 2 * DH), dtype=jnp.float32) * 0.02
        Wo = jax.random.normal(ks[7], (INNER, DIM), dtype=jnp.float32) * 0.02
        g_out = jnp.ones((DIM,), dtype=jnp.float32)
        return {'x': x, 'attn_bias': attn_bias, 'mask': mask, 'g_in': g_in, 'null_attn_bias': null_attn_bias, 'null_kv': null_kv, 'Wq': Wq, 'Wkv': Wkv, 'Wo': Wo, 'g_out': g_out}
    _L0_cond2_all = _L0_cond2_setup()
    _L0_cond2_in = {k: v for k, v in _L0_cond2_all.items() if k in ('g_in', 'null_attn_bias', 'Wq', 'Wkv', 'Wo', 'g_out')}
    del _L0_cond2_all

    def _L0_ffn_setup():
        import jax, jax.numpy as jnp
        import numpy as np
        H = 256
        E = 64
        K = 8
        G = 8
        TOPK_GROUP = 4
        I_MOE = 128
        I_SHARED = 512
        SCALE = 2.5

        def relu2(x):
            return jnp.square(jax.nn.relu(x))

        def _route(xf, router_w, correction_bias):
            T = xf.shape[0]
            logits = xf @ router_w.T
            scores = jax.nn.sigmoid(logits)
            sfc = scores + correction_bias[None, :]
            grp = sfc.reshape(T, G, E // G)
            top2, _ = jax.lax.top_k(grp, 2)
            group_scores = top2.sum(-1)
            _, gidx = jax.lax.top_k(group_scores, TOPK_GROUP)
            gmask = jnp.zeros((T, G), sfc.dtype).at[jnp.arange(T)[:, None], gidx].set(1.0)
            emask = jnp.repeat(gmask, E // G, axis=1)
            masked = jnp.where(emask > 0, sfc, 0.0)
            _, tidx = jax.lax.top_k(masked, K)
            tw = jnp.take_along_axis(scores, tidx, axis=1)
            tw = tw / (tw.sum(-1, keepdims=True) + 1e-20)
            return (tidx, tw * SCALE)
        key = jax.random.key(seed)
        ks = jax.random.split(key, 7)
        x = jax.random.normal(ks[0], (2, 256, H), dtype=jnp.float32)
        router_w = jax.random.normal(ks[1], (E, H), dtype=jnp.float32) * 0.02
        correction_bias = jax.random.normal(ks[2], (E,), dtype=jnp.float32) * 0.01
        up_w = jax.random.normal(ks[3], (E, H, I_MOE), dtype=jnp.float32) * 0.02
        down_w = jax.random.normal(ks[4], (E, I_MOE, H), dtype=jnp.float32) * 0.02
        shared_up_w = jax.random.normal(ks[5], (H, I_SHARED), dtype=jnp.float32) * 0.02
        shared_down_w = jax.random.normal(ks[6], (I_SHARED, H), dtype=jnp.float32) * 0.02
        return {'x': x, 'router_w': router_w, 'correction_bias': correction_bias, 'up_w': up_w, 'down_w': down_w, 'shared_up_w': shared_up_w, 'shared_down_w': shared_down_w}
    _L0_ffn_all = _L0_ffn_setup()
    _L0_ffn_in = {k: v for k, v in _L0_ffn_all.items() if k in ('router_w', 'correction_bias', 'up_w', 'down_w', 'shared_up_w', 'shared_down_w')}
    del _L0_ffn_all
    return {'x': x, 'cond_64': cond_64, 'fside_16xSxS_0': fside_16xSxS_0, 'mask_BxS_bk0': mask_BxS_bk0, 'L0_cond_wt': _L0_cond_in['wt'], 'L0_cond_wg': _L0_cond_in['wg'], 'L0_cond_w_gate': _L0_cond_in['w_gate'], 'L0_cond_w_up': _L0_cond_in['w_up'], 'L0_cond_w_down': _L0_cond_in['w_down'], 'L0_cond_sw_gate': _L0_cond_in['sw_gate'], 'L0_cond_sw_up': _L0_cond_in['sw_up'], 'L0_cond_sw_down': _L0_cond_in['sw_down'], 'L0_attn_Wq': _L0_attn_in['Wq'], 'L0_attn_Wk': _L0_attn_in['Wk'], 'L0_attn_Wv': _L0_attn_in['Wv'], 'L0_attn_Wo': _L0_attn_in['Wo'], 'L0_attn_rel_emb': _L0_attn_in['rel_emb'], 'L0_cond2_g_in': _L0_cond2_in['g_in'], 'L0_cond2_null_attn_bias': _L0_cond2_in['null_attn_bias'], 'L0_cond2_Wq': _L0_cond2_in['Wq'], 'L0_cond2_Wkv': _L0_cond2_in['Wkv'], 'L0_cond2_Wo': _L0_cond2_in['Wo'], 'L0_cond2_g_out': _L0_cond2_in['g_out'], 'L0_ffn_router_w': _L0_ffn_in['router_w'], 'L0_ffn_correction_bias': _L0_ffn_in['correction_bias'], 'L0_ffn_up_w': _L0_ffn_in['up_w'], 'L0_ffn_down_w': _L0_ffn_in['down_w'], 'L0_ffn_shared_up_w': _L0_ffn_in['shared_up_w'], 'L0_ffn_shared_down_w': _L0_ffn_in['shared_down_w']}

def reference(x, cond_64, fside_16xSxS_0, mask_BxS_bk0, L0_cond_wt, L0_cond_wg, L0_cond_w_gate, L0_cond_w_up, L0_cond_w_down, L0_cond_sw_gate, L0_cond_sw_up, L0_cond_sw_down, L0_attn_Wq, L0_attn_Wk, L0_attn_Wv, L0_attn_Wo, L0_attn_rel_emb, L0_cond2_g_in, L0_cond2_null_attn_bias, L0_cond2_Wq, L0_cond2_Wkv, L0_cond2_Wo, L0_cond2_g_out, L0_ffn_router_w, L0_ffn_correction_bias, L0_ffn_up_w, L0_ffn_down_w, L0_ffn_shared_up_w, L0_ffn_shared_down_w):
    import jax
    import jax.numpy as jnp

    def _L0_cond_ref(hidden_states, g, wt, wg, w_gate, w_up, w_down, sw_gate, sw_up, sw_down):
        import jax, jax.numpy as jnp
        import numpy as np
        B, S, H = (4, 512, 256)
        E = 8
        M = 128
        K = 2
        N_SHARED = 2
        SM = M * N_SHARED
        G = 64
        GE_TEMP = 1.0
        ALPHA = 0.001
        SEQ_AUX = True
        NORM_TOPK = True
        COS_TEMP = 0.78
        CONS_ALPHA = 0.01
        LEAKY_SLOPE = 0.01
        EPS_COS = 1e-08

        def _leaky(x):
            return jnp.where(x >= 0, x, LEAKY_SLOPE * x)

        def _moe_forward(hidden_states, g, wt, wg, w_gate, w_up, w_down, sw_gate, sw_up, sw_down):
            b, s, h = hidden_states.shape
            x = hidden_states.reshape(-1, h)
            T = x.shape[0]
            logits_h = x @ wt.T
            logits_g = g @ wg.T
            logits_g = jnp.repeat(logits_g, s, axis=0)
            logits = (logits_h + logits_g / GE_TEMP) / (1.0 + 1.0 / GE_TEMP)
            scores = jax.nn.softmax(logits, axis=-1)
            topk_w, topk_idx = jax.lax.top_k(scores, K)
            if K > 1 and NORM_TOPK:
                topk_w = topk_w / (topk_w.sum(-1, keepdims=True) + 1e-20)
            onehot = jax.nn.one_hot(topk_idx.reshape(b, s * K), E, dtype=jnp.float32)
            ce = onehot.sum(1) / (s * K / E)
            aux_loss = (ce * scores.reshape(b, s, E).mean(1)).sum(1).mean() * ALPHA
            gp = _leaky(jnp.einsum('th,ehm->etm', x, w_gate))
            up = jnp.einsum('th,ehm->etm', x, w_up)
            y_all = jnp.einsum('etm,emh->eth', gp * up, w_down)
            y_sel = y_all[topk_idx, jnp.arange(T)[:, None], :]
            y = (y_sel * topk_w[..., None]).sum(1).reshape(b, s, h)
            p = _leaky(hidden_states @ sw_gate) * (hidden_states @ sw_up) @ sw_down
            y = y + p
            num = jnp.sum(y * p, -1)
            den = jnp.maximum(jnp.linalg.norm(y, axis=-1), EPS_COS) * jnp.maximum(jnp.linalg.norm(p, axis=-1), EPS_COS)
            closs = CONS_ALPHA * jnp.mean(num / den / (1.0 + COS_TEMP))
            return (y, aux_loss + closs)
        y, _ = _moe_forward(hidden_states, g, wt, wg, w_gate, w_up, w_down, sw_gate, sw_up, sw_down)
        return y

    def _L0_attn_ref(hidden_states, Wq, Wk, Wv, Wo, rel_emb):
        import jax, jax.numpy as jnp
        import numpy as np
        import math
        B, S, D, H = (2, 512, 256, 16)
        DK = D // H
        NUM_BUCKETS = 32
        MAX_DISTANCE = 128

        def _relative_position_bucket(relative_position, num_buckets=NUM_BUCKETS, max_distance=MAX_DISTANCE):
            nb = num_buckets // 2
            n = -relative_position
            ret = (n < 0).astype(jnp.int32) * nb
            n = jnp.abs(n)
            max_exact = nb // 2
            is_small = n < max_exact
            val_if_large = max_exact + (jnp.log(jnp.maximum(n, 1).astype(jnp.float32) / max_exact) / math.log(max_distance / max_exact) * (nb - max_exact)).astype(jnp.int32)
            val_if_large = jnp.minimum(val_if_large, nb - 1)
            return ret + jnp.where(is_small, n, val_if_large)
        b, s, d = hidden_states.shape
        q = jnp.einsum('bsd,ed->bse', hidden_states, Wq).reshape(b, s, H, DK).transpose(0, 2, 1, 3)
        k = jnp.einsum('bsd,ed->bse', hidden_states, Wk).reshape(b, s, H, DK).transpose(0, 2, 1, 3)
        v = jnp.einsum('bsd,ed->bse', hidden_states, Wv).reshape(b, s, H, DK).transpose(0, 2, 1, 3)
        scores = jnp.einsum('bhqd,bhkd->bhqk', q, k) / math.sqrt(DK)
        ctx = jnp.arange(s)[:, None]
        mem = jnp.arange(s)[None, :]
        rp_bucket = _relative_position_bucket(mem - ctx)
        bias = rel_emb[rp_bucket]
        bias = bias.transpose(2, 0, 1)[None]
        scores = scores + bias
        attn = jax.nn.softmax(scores, axis=-1)
        out = jnp.einsum('bhqk,bhkd->bhqd', attn, v)
        out = out.transpose(0, 2, 1, 3).reshape(b, s, d)
        return jnp.einsum('bsd,ed->bse', out, Wo)

    def _L0_cond2_ref(x, attn_bias, mask, g_in, null_attn_bias, null_kv, Wq, Wkv, Wo, g_out):
        import jax, jax.numpy as jnp
        import numpy as np
        B, N, DIM, H, DH = (2, 512, 256, 16, 64)
        INNER = H * DH
        EPS = 1e-05

        def layernorm(x, g):
            mean = jnp.mean(x, axis=-1, keepdims=True)
            var = jnp.var(x, axis=-1, keepdims=True)
            return (x - mean) * jax.lax.rsqrt(var + EPS) * g
        b, n, _ = x.shape
        scale = DH ** (-0.5)
        xn = layernorm(x, g_in)
        q = (xn @ Wq).reshape(b, n, H, DH).transpose(0, 2, 1, 3) * scale
        kv = xn @ Wkv
        k, v = (kv[..., :DH], kv[..., DH:])
        nk = jnp.broadcast_to(null_kv[0], (b, 1, DH))
        nv = jnp.broadcast_to(null_kv[1], (b, 1, DH))
        k = jnp.concatenate([nk, k], axis=1)
        v = jnp.concatenate([nv, v], axis=1)
        sim = jnp.einsum('bhid,bjd->bhij', q, k)
        null_col = jnp.broadcast_to(null_attn_bias[:, None, None], (H, n, 1))
        bias = jnp.concatenate([null_col, attn_bias], axis=-1)
        sim = sim + bias
        neg = -jnp.finfo(sim.dtype).max
        j = n + 1
        causal_mask = jnp.triu(jnp.ones((n, j), dtype=bool), k=j - n + 1)
        sim = jnp.where(causal_mask, neg, sim)
        mask_p = jnp.pad(mask, ((0, 0), (1, 0)), constant_values=True)
        sim = jnp.where(mask_p[:, None, None, :], sim, neg)
        attn = jax.nn.softmax(sim, axis=-1)
        out = jnp.einsum('bhij,bjd->bhid', attn, v)
        out = out.transpose(0, 2, 1, 3).reshape(b, n, INNER)
        out = out @ Wo
        return layernorm(out, g_out)

    def _L0_ffn_ref(x, router_w, correction_bias, up_w, down_w, shared_up_w, shared_down_w):
        import jax, jax.numpy as jnp
        import numpy as np
        H = 256
        E = 64
        K = 8
        G = 8
        TOPK_GROUP = 4
        I_MOE = 128
        I_SHARED = 512
        SCALE = 2.5

        def relu2(x):
            return jnp.square(jax.nn.relu(x))

        def _route(xf, router_w, correction_bias):
            T = xf.shape[0]
            logits = xf @ router_w.T
            scores = jax.nn.sigmoid(logits)
            sfc = scores + correction_bias[None, :]
            grp = sfc.reshape(T, G, E // G)
            top2, _ = jax.lax.top_k(grp, 2)
            group_scores = top2.sum(-1)
            _, gidx = jax.lax.top_k(group_scores, TOPK_GROUP)
            gmask = jnp.zeros((T, G), sfc.dtype).at[jnp.arange(T)[:, None], gidx].set(1.0)
            emask = jnp.repeat(gmask, E // G, axis=1)
            masked = jnp.where(emask > 0, sfc, 0.0)
            _, tidx = jax.lax.top_k(masked, K)
            tw = jnp.take_along_axis(scores, tidx, axis=1)
            tw = tw / (tw.sum(-1, keepdims=True) + 1e-20)
            return (tidx, tw * SCALE)
        B, S, Hd = x.shape
        xf = x.reshape(-1, Hd)
        T = xf.shape[0]
        tidx, tw = _route(xf.astype(jnp.float32), router_w, correction_bias)
        combine = jnp.zeros((T, E), xf.dtype).at[jnp.arange(T)[:, None], tidx].add(tw.astype(xf.dtype))

        def body(acc, ew):
            wu, wd, c = ew
            return (acc + c[:, None] * (relu2(xf @ wu) @ wd), None)
        routed, _ = jax.lax.scan(body, jnp.zeros_like(xf), (up_w, down_w, combine.T))
        shared = relu2(xf @ shared_up_w) @ shared_down_w
        return (routed + shared).reshape(B, S, Hd)
    x = x + _L0_attn_ref(_L0_cond_ref(x, cond_64, L0_cond_wt, L0_cond_wg, L0_cond_w_gate, L0_cond_w_up, L0_cond_w_down, L0_cond_sw_gate, L0_cond_sw_up, L0_cond_sw_down), L0_attn_Wq, L0_attn_Wk, L0_attn_Wv, L0_attn_Wo, L0_attn_rel_emb)
    x = x + _L0_ffn_ref(_L0_cond2_ref(x, fside_16xSxS_0, mask_BxS_bk0, L0_cond2_g_in, L0_cond2_null_attn_bias, cond_64, L0_cond2_Wq, L0_cond2_Wkv, L0_cond2_Wo, L0_cond2_g_out), L0_ffn_router_w, L0_ffn_correction_bias, L0_ffn_up_w, L0_ffn_down_w, L0_ffn_shared_up_w, L0_ffn_shared_down_w)
    return x

_drawn_inputs = setup_inputs


def setup_inputs(seed=0):
    import zlib

    import numpy as np

    out = dict(_drawn_inputs(seed))
    spreads = {'L0_cond2_g_in': (1.0, 0.6), 'L0_cond2_g_out': (1.0, 0.6)}
    factors = {'fside_16xSxS_0': 41.328,
     'L0_cond_wt': 6.179,
     'L0_cond_wg': 6.369,
     'L0_cond_w_gate': 5.291,
     'L0_cond_w_up': 4.429,
     'L0_cond_w_down': 4.343,
     'L0_cond_sw_gate': 3.733,
     'L0_cond_sw_up': 3.151,
     'L0_cond_sw_down': 3.167,
     'L0_attn_Wq': 8.0,
     'L0_attn_Wk': 8.0,
     'L0_attn_rel_emb': 56.722,
     'L0_cond2_null_attn_bias': 32.456,
     'L0_cond2_Wq': 64.0,
     'L0_cond2_Wkv': 37.6,
     'L0_ffn_correction_bias': 64.0,
     'L0_cond2_Wo': 5.394,
     'L0_ffn_router_w': 8.0,
     'L0_ffn_up_w': 8.0,
     'L0_ffn_down_w': 8.0,
     'L0_ffn_shared_up_w': 8.0,
     'L0_ffn_shared_down_w': 8.0}
    for name, (base, spread) in spreads.items():
        noise = np.random.default_rng([zlib.crc32(name.encode()), seed]).standard_normal(out[name].shape)
        drawn = base * np.exp(spread * noise) if base else spread * noise
        out[name] = jnp.asarray(drawn.astype(out[name].dtype))
    for name, factor in factors.items():
        out[name] = (out[name] * factor).astype(out[name].dtype)
    return out
```

```python
import math
from contextlib import ExitStack

import numpy as np
import concourse.bass as bass
from concourse import mybir

F32 = mybir.dt.float32
U8 = mybir.dt.uint8
ALU = mybir.AluOpType
ACT = mybir.ActivationFunctionType
AX = mybir.AxisListType

P = 128
SEQS, S, D = 64, 64, 256
T = SEQS * S
NT = T // P
BT = 512
NB = T // BT
TPB = BT // P
SPB = BT // S
C = D // P

E1, M1 = 8, 128
SH1 = 2
N1 = E1 + SH1
K1 = 2
G = 64

H1, DK1 = 16, 16
H2, DH2 = 16, 64
J2 = H2 // 2
KN = S + 1
BUCKETS = 32
REL = 2 * S - 1

E2, M2 = 64, 128
GROUPS, TOPG, K2 = 8, 4, 8
SH2 = 4
N2 = E2 + SH2
ROUTE_SCALE = 2.5
EPS = 1e-5
MASKED = -1.0e30
TAKEN = -3.0e38
UNMATCHED = 3.0e38


def bucket_runs():
    half, exact = BUCKETS // 2, BUCKETS // 4
    rel = np.arange(-(S - 1), S)
    n = np.abs(rel)
    far = np.log(np.maximum(n, 1).astype(np.float32) / np.float32(exact)) / np.float32(math.log(128 / exact))
    far = np.minimum(exact + (far * np.float32(half - exact)).astype(np.int32), half - 1)
    bucket = np.where(n < exact, n, far) + (rel > 0) * half
    runs, at = [], 0
    for i in range(1, REL + 1):
        if i == REL or bucket[i] != bucket[at]:
            runs.append((at, i, int(bucket[at])))
            at = i
    return runs


class Steps:

    def __init__(self, eng, sem, turn=0, per=0):
        self.eng, self.sem, self.base, self.per, self.k = eng, sem, turn * per if per else 0, per, 0

    def done(self, ins):
        self.k += 1
        ins.then_inc(self.sem, 1)
        self.eng.wait_ge(self.sem, self.base + self.k)

    def close(self):
        assert self.k == self.per, (self.k, self.per)


def build(nc, x, xT, condT, cond, bias2, mask, w1gate, w1up, w1down, wtT, wgT,
          wqT, wkT, wvT, woT, relT, g_in, nbias, wq2, wkv2, wo2, g_out, rwT, cbias, up2, down2, out):
    ctx = ExitStack()
    with ctx:
        def sb(name, shape, dt=F32):
            return ctx.enter_context(nc.sbuf_tensor(name, shape, dt))

        def sem(name):
            return ctx.enter_context(nc.semaphore(name))

        rel_rows = nc.dram_tensor("rel_rows", (S, H1, REL), F32).ap()

        ctx.enter_context(nc.allow_non_contiguous_dma(reason="a few columns of constants"))
        ps = ctx.enter_context(nc.psum_tensor("ps", [P, 8, 512], F32))

        feat = sb("feat", [P, C, T])
        acc = sb("acc", [P, NT, D])
        att = sb("att", [P, NT, D])
        ident = sb("ident", [P, P])
        comb1 = sb("comb1", [P, NT, N1])
        comb2 = sb("comb2", [P, NT, N2])
        mv1 = sb("mv1", [P, NT, 2])
        rstd = sb("rstd", [P, NT])

        def make_identity(pool, seen, done):
            pool.memset(ident[:], 0.0).then_inc(seen, 1)
            pool.wait_ge(seen, 1)
            pool.affine_select(out=ident[:], in_=ident[:], compare_op=ALU.not_equal, fill=1.0, base=0,
                               pattern=[[-1, P]], channel_multiplier=1).then_inc(done, 1)

        def router1():
            ph = ExitStack()
            with ph:
                def sb(name, shape, dt=F32):
                    return ph.enter_context(nc.sbuf_tensor(name, shape, dt))

                def sem(name):
                    return ctx.enter_context(nc.semaphore("r1_" + name))

                wt = sb("wt", [P, C, P])
                wg = sb("wg", [P, P])
                cT = sb("cT", [P, SEQS])
                lT = sb("lT", [P, BT])
                s1 = sb("s1", [P, NT, E1])
                left = sb("left", [P, NT, E1])
                top8 = sb("top8", [P, NT, 8])
                stat = sb("stat", [P, NT])
                small_in, x_in = sem("small_in"), sem("x_in")
                zeroed, id_ready, padded = sem("zeroed"), sem("id_ready"), sem("padded")
                lT_ps, lT_sb, l_ps, l_sb = sem("lT_ps"), sem("lT_sb"), sem("l_ps"), sem("l_sb")
                shifted, expd, dve_step = sem("shifted"), sem("expd"), sem("dve_step")
                block = ph.enter_context(nc.Block())

                @block.sync
                def _(sp):
                    for c in range(C):
                        sp.dma_start(feat[:, c, :], xT[c * P:(c + 1) * P, :]).then_inc(x_in, 16)
                    sp.wait_ge(padded, 3)
                    sp.dma_start(wt[:, :, 0:E1], wtT.rearrange("(c p) e -> p c e", p=P)).then_inc(small_in, 16)
                    sp.dma_start(wg[0:G, 0:E1], wgT).then_inc(small_in, 16)
                    sp.dma_start(cT[0:G], condT).then_inc(small_in, 16)

                @block.gpsimd
                def _(pool):
                    for pad in (wt, wg, cT):
                        pool.memset(pad[:], 0.0).then_inc(padded, 1)
                    make_identity(pool, zeroed, id_ready)
                    pool.memset(acc[:], 0.0)

                @block.tensor
                def _(pe):
                    pe.wait_ge(small_in, 48)
                    pe.wait_ge(x_in, 16 * C)
                    pe.wait_ge(id_ready, 1)
                    with pe.Fori(0, NB) as b:
                        for c in range(C):
                            pe.matmul(ps[:, 0, :], wt[:, c, :], feat[:, c, bass.ds(b * BT, BT)],
                                      start=(c == 0), stop=False)
                        pe.matmul(ps[:, 0, :], wg[:],
                                  cT[:, bass.ds(b * SPB, SPB)].unsqueeze(2).to_broadcast([P, SPB, S]),
                                  start=False, stop=True).then_inc(lT_ps, 1)
                        pe.wait_ge(lT_sb, b + 1)
                        pe.wait_ge(l_sb, b)
                        for t in range(TPB):
                            last = pe.transpose(ps[:, 1, t * P:(t + 1) * P], lT[:, t * P:(t + 1) * P], ident[:])
                        last.then_inc(l_ps, 1)

                @block.scalar
                def _(act):
                    with act.Fori(0, NB) as b:
                        act.wait_ge(lT_ps, b + 1)
                        act.wait_ge(l_ps, b)
                        act.activation(lT[:], ps[:, 0, :], ACT.Copy, scale=0.5).then_inc(lT_sb, 1)
                    act.wait_ge(shifted, 1)
                    act.activation(s1[:], s1[:], ACT.Exp).then_inc(expd, 1)

                @block.vector
                def _(dve):
                    with dve.Fori(0, NB) as b:
                        dve.wait_ge(l_ps, b + 1)
                        dve.tensor_copy(s1[:, bass.ds(b * TPB, TPB), :],
                                        ps[:, 1, :].rearrange("p (t e) -> p t e", t=TPB)[:, :, 0:E1]).then_inc(l_sb, 1)
                    dve.wait_ge(l_sb, NB)
                    st = Steps(dve, dve_step)
                    st.done(dve.tensor_reduce(stat[:], s1[:], AX.X, ALU.max))
                    dve.tensor_tensor(s1[:], s1[:], stat[:].unsqueeze(2).to_broadcast([P, NT, E1]),
                                      ALU.subtract).then_inc(shifted, 1)
                    dve.wait_ge(expd, 1)
                    st.done(dve.tensor_reduce(stat[:], s1[:], AX.X, ALU.add))
                    st.done(dve.reciprocal(stat[:], stat[:]))
                    st.done(dve.tensor_tensor(s1[:], s1[:], stat[:].unsqueeze(2).to_broadcast([P, NT, E1]), ALU.mult))
                    for t in range(NT):
                        last = dve.max(top8[:, t, :], s1[:, t, :])
                    st.done(last)
                    st.done(dve.memset(top8[:, :, K1:8], UNMATCHED))
                    for t in range(NT):
                        last = dve.match_replace(left[:, t, :], top8[:, t, :], s1[:, t, :], -1.0)
                    st.done(last)
                    st.done(dve.tensor_scalar(left[:], left[:], -1.0, None, ALU.is_equal))
                    st.done(dve.tensor_tensor(s1[:], s1[:], left[:], ALU.mult))
                    st.done(dve.tensor_reduce(stat[:], s1[:], AX.X, ALU.add))
                    st.done(dve.tensor_scalar(stat[:], stat[:], 1e-20, None, ALU.add))
                    st.done(dve.reciprocal(stat[:], stat[:]))
                    dve.tensor_tensor(comb1[:, :, 0:E1], s1[:], stat[:].unsqueeze(2).to_broadcast([P, NT, E1]),
                                      ALU.mult)
                    dve.memset(comb1[:, :, E1:N1], 1.0)

        def experts(tag, n_exp, comb, in_ws, down_w, gated):
            ph = ExitStack()
            n_in = len(in_ws)
            TURNS = n_exp // 2
            PER = 2 * NB
            with ph:
                def sb(name, shape, dt=F32):
                    return ph.enter_context(nc.sbuf_tensor(tag + name, shape, dt))

                def sem(name):
                    return ctx.enter_context(nc.semaphore(tag + name))

                w_in = sb("w_in", [P, 2, n_in, C, P])
                w_dn = sb("w_dn", [P, 2, D])
                r = sb("r", [P, 2, BT])
                h = sb("h", [P, 2, BT])
                cexp = sb("cexp", [P, 2, NT])
                w_in_sem = [sem("weights0"), sem("weights1")]
                z_ps, y_ps, r_ready, h_ready, y_used, c_ready = (
                    sem(n) for n in ("z_ps", "y_ps", "r_ready", "h_ready", "y_used", "c_ready"))
                leaky = sem("leaky")
                block = ph.enter_context(nc.Block())

                def z_bank(i, n):
                    return ps[:, n_in * (n % 2) + i, :]

                def y_bank(n, t):
                    return ps[:, 4 + 2 * (n % 2) + t // 2, (t % 2) * D:(t % 2 + 1) * D]

                @block.sync
                def _(sp):
                    def load(e, w):
                        for i, src in enumerate(in_ws):
                            sp.dma_start(w_in[:, w, i], src[bass.ds(e, 1)].rearrange("o (c p) m -> p (o c) m", p=P)
                                         ).then_inc(w_in_sem[w], 16)
                        sp.dma_start(w_dn[:, w, :], down_w[bass.ds(e, 1)].rearrange("o p n -> p (o n)")
                                     ).then_inc(w_in_sem[w], 16)
                    load(0, 0)
                    load(1, 1)
                    with sp.Fori(0, TURNS - 1) as i:
                        for w in range(2):
                            sp.wait_ge(y_ps, (i * 2 + w + 1) * NB)
                            load(i * 2 + 2 + w, w)

                @block.tensor
                def _(pe):
                    def z(n, turn, w_ready):
                        w, b = n // NB % 2, n % NB
                        if b == 0:
                            pe.wait_ge(w_in_sem[w], w_ready)
                        for i in range(n_in):
                            for c in range(C):
                                last = pe.matmul(z_bank(i, n), w_in[:, w, i, c, :], feat[:, c, b * BT:(b + 1) * BT],
                                                 start=(c == 0), stop=(c == C - 1))
                        last.then_inc(z_ps, 1)

                    def y(n, turn, first=False):
                        w = n // NB
                        pe.wait_ge(h_ready, turn * PER + n + 1)
                        if not (first and n < 2):
                            pe.wait_ge(y_used, turn * PER + n - 1)
                        for t in range(TPB):
                            last = pe.matmul(y_bank(n, t), h[:, n % 2, t * P:(t + 1) * P], w_dn[:, w, :],
                                             start=True, stop=True)
                        last.then_inc(y_ps, 1)

                    ALL = 16 * (n_in + 1)

                    def turn_body(turn, first=False, final=False):
                        for n in range(PER):
                            if not (final and n == PER - 1):
                                nxt = n + 1
                                z(nxt, turn, (turn + (2 if nxt == PER else 1)) * ALL)
                            y(n, turn, first)

                    z(0, 0, ALL)
                    turn_body(0, first=True)
                    with pe.Fori(1, TURNS - 1) as turn:
                        turn_body(turn)
                    turn_body(TURNS - 1, final=True)

                @block.scalar
                def _(act):
                    def turn_body(turn, first=False):
                        for n in range(PER):
                            act.wait_ge(z_ps, turn * PER + n + 1)
                            if gated:
                                if not (first and n < 2):
                                    act.wait_ge(h_ready, turn * PER + n - 1)
                                act.activation(r[:, n % 2, :], z_bank(0, n), ACT.Copy, scale=0.01
                                               ).then_inc(r_ready, 1)
                            else:
                                act.activation(r[:, n % 2, :], z_bank(0, n), ACT.Relu).then_inc(r_ready, 1)
                                act.wait_ge(r_ready, turn * PER + n + 1)
                                if not (first and n < 2):
                                    act.wait_ge(y_ps, turn * PER + n - 1)
                                act.activation(h[:, n % 2, :], r[:, n % 2, :], ACT.Square).then_inc(h_ready, 1)
                    turn_body(0, first=True)
                    with act.Fori(1, TURNS) as turn:
                        turn_body(turn)

                @block.vector
                def _(dve):
                    def accumulate(n, turn, first):
                        w, b = n // NB, n % NB
                        if b == 0:
                            dve.tensor_copy(cexp[:, w, :], comb[:, :, bass.ds(turn * 2 + w, 1)].rearrange(
                                "p t o -> p (t o)")).then_inc(c_ready, 1)
                            dve.wait_ge(c_ready, turn * 2 + w + 1)
                        dve.wait_ge(y_ps, turn * PER + n + 1)
                        for t in range(TPB):
                            tile = b * TPB + t
                            last = dve.scalar_tensor_tensor(acc[:, tile, :], y_bank(n, t), cexp[:, w, tile:tile + 1],
                                                            acc[:, tile, :], ALU.mult, ALU.add)
                        last.then_inc(y_used, 1)

                    def gate(n, turn, first):
                        dve.wait_ge(r_ready, turn * PER + n + 1)
                        if not (first and n < 2):
                            dve.wait_ge(y_ps, turn * PER + n - 1)
                        dve.tensor_tensor(r[:, n % 2, :], z_bank(0, n), r[:, n % 2, :], ALU.max).then_inc(leaky, 1)
                        dve.wait_ge(leaky, turn * PER + n + 1)
                        dve.tensor_tensor(h[:, n % 2, :], r[:, n % 2, :], z_bank(1, n), ALU.mult).then_inc(h_ready, 1)

                    def turn_body(turn, first=False, final=False):
                        for n in range(PER):
                            if gated:
                                if n + 1 < PER or not final:
                                    gate(n + 1, turn, first)
                            accumulate(n, turn, first)
                    if gated:
                        gate(0, 0, True)
                    turn_body(0, first=True)
                    with dve.Fori(1, TURNS - 1) as turn:
                        turn_body(turn)
                    turn_body(TURNS - 1, final=True)

        def attention1():
            ph = ExitStack()
            with ph:
                def sb(name, shape, dt=F32):
                    return ph.enter_context(nc.sbuf_tensor("a1_" + name, shape, dt))

                def sem(name):
                    return ctx.enter_context(nc.semaphore("a1_" + name))

                wq, wk, wv, wo = (sb(n, [P, C, D]) for n in ("wq", "wk", "wv", "wo"))
                rel = sb("rel", [H1, BUCKETS])
                reld = sb("reld", [H1, REL])
                bias = sb("bias", [P, H1, S])
                own = sb("own", [P, 8])
                xb = sb("xb", [P, TPB, D])
                xres = sb("xres", [P, 2, TPB, D])
                hT = sb("hT", [P, C, BT])
                qT = sb("qT", [P, C, BT])
                kT = sb("kT", [P, C, BT])
                kbd = sb("kbd", [P, 2, C, 2, 8, S])
                vbd = sb("vbd", [P, TPB, 8, 2, 2, DK1])
                sc = sb("sc", [P, 2, H1, S])
                mx = sb("mx", [P, 2, H1])
                rs = sb("rs", [P, 2, H1])
                pT = sb("pT", [P, 8, P])
                at = sb("at", [P, D])
                atT = sb("atT", [P, C, P])
                bst = sb("bst", [P, 6])
                mv = sb("mv", [P, 2])
                w_in, rel_in, rel_sb, rel_out, bias_in, res_in = (
                    sem(n) for n in ("w_in", "rel_in", "rel_sb", "rel_out", "bias_in", "res_in0"))
                res_sem = [res_in, sem("res_in1")]
                own_step, own_ready, v_zero = sem("own_step"), sem("own_ready"), sem("v_zero")
                xb_ready, hT_ps, hT_act, hT_dve = sem("xb_ready"), sem("hT_ps"), sem("hT_act"), sem("hT_dve")
                qk_ps, qT_sb, kT_sb, v_ps, v_sb = sem("qk_ps"), sem("qT_sb"), sem("kT_sb"), sem("v_ps"), sem("v_sb")
                kbd_ready, s_ps, s_sh, e_ready, rs_ready = (
                    sem(n) for n in ("kbd_ready", "s_ps", "s_sh", "e_ready", "rs_ready"))
                pT_ps, pT_sb, o_ps, at_sb, aT_ps, aT_sb, yo_ps, tile_done, dve_step = (
                    sem(n) for n in ("pT_ps", "pT_sb", "o_ps", "at_sb", "aT_ps", "aT_sb", "yo_ps", "tile_done",
                                     "dve_step"))
                block = ph.enter_context(nc.Block())
                runs = bucket_runs()

                @block.sync
                def _(sp):
                    for dst, src in ((wq, wqT), (wk, wkT), (wv, wvT), (wo, woT)):
                        sp.dma_start(dst[:], src.rearrange("(c p) n -> p c n", p=P)).then_inc(w_in, 16)
                    sp.dma_start(rel[:], relT).then_inc(rel_in, 16)
                    sp.wait_ge(rel_sb, len(runs))
                    sp.dma_start(rel_rows.rearrange("q h r -> h q r"),
                                 reld[:].unsqueeze(1).to_broadcast([H1, S, REL])).then_inc(rel_out, 16)
                    sp.wait_ge(rel_out, 16)
                    for s in range(2):
                        diag = bass.AP(rel_rows.tensor, S - 1, [[H1 * REL - 1, S], [REL, H1], [1, S]])
                        sp.dma_start(bias[s * S:(s + 1) * S], diag).then_inc(bias_in, 16)
                    xv = x.rearrange("(t p) d -> p t d", p=P)
                    for b in range(2):
                        sp.dma_start(xres[:, b], xv[:, b * TPB:(b + 1) * TPB, :]).then_inc(res_sem[b], 16)
                    with sp.Fori(0, NB // 2 - 1) as i:
                        for w in range(2):
                            sp.wait_ge(tile_done, (i * 2 + w + 1) * TPB)
                            sp.dma_start(xres[:, w], xv[:, bass.ds((i * 2 + 2 + w) * TPB, TPB), :]
                                         ).then_inc(res_sem[w], 16)

                @block.gpsimd
                def _(pool):
                    pool.memset(own[:], 1.0).then_inc(own_step, 1)
                    pool.wait_ge(own_step, 1)
                    pool.affine_select(out=own[:], in_=own[:], compare_op=ALU.is_ge, fill=0.0, base=0,
                                       pattern=[[-DK1, 8]], channel_multiplier=1).then_inc(own_step, 1)
                    pool.wait_ge(own_step, 2)
                    pool.affine_select(out=own[:], in_=own[:], compare_op=ALU.is_ge, fill=0.0, base=DK1 - 1,
                                       pattern=[[DK1, 8]], channel_multiplier=-1).then_inc(own_ready, 1)
                    pool.wait_ge(own_ready, 1)
                    pool.memset(vbd[:], 0.0).then_inc(v_zero, 1)
                    with pool.Fori(0, NB) as b:
                        pool.wait_ge(hT_ps, b)
                        pool.tensor_copy(xb[:], acc[:, bass.ds(b * TPB, TPB), :]).then_inc(xb_ready, 1)
                        pool.wait_ge(kT_sb, b * C + C)
                        for t in range(TPB):
                            if t < 2:
                                pool.wait_ge(s_ps, b * TPB)
                            else:
                                pool.wait_ge(s_ps, b * TPB + t - 1)
                            for c in range(C):
                                kk = kT[:, c, t * P:(t + 1) * P].rearrange("p (s k) -> p s k", s=2)
                                pool.tensor_tensor(kbd[:, t % 2, c], kk.unsqueeze(2).to_broadcast([P, 2, 8, S]),
                                                   own[:].unsqueeze(1).unsqueeze(3).to_broadcast([P, 2, 8, S]),
                                                   ALU.mult).then_inc(kbd_ready, 1)

                @block.tensor
                def _(pe):
                    def scores(b, t):
                        pe.wait_ge(kbd_ready, (b * TPB + t + 1) * C)
                        if t >= 2:
                            pe.wait_ge(s_sh, b * TPB + t - 1)
                        for c in range(C):
                            for s in range(2):
                                last = pe.matmul(ps[s * S:(s + 1) * S, 2 + 2 * (t % 2) + c, :],
                                                 qT[:, c, t * P + s * S:t * P + (s + 1) * S],
                                                 kbd[:, t % 2, c, s].rearrange("p h k -> p (h k)"),
                                                 start=True, stop=True)
                        last.then_inc(s_ps, 1)

                    pe.wait_ge(w_in, 64)
                    with pe.Fori(0, NB) as b:
                        pe.wait_ge(xb_ready, b + 1)
                        pe.wait_ge(tile_done, b * TPB)
                        for c in range(C):
                            for t in range(TPB):
                                last = pe.transpose(ps[:, c, t * P:(t + 1) * P], xb[:, t, c * P:(c + 1) * P], ident[:])
                        last.then_inc(hT_ps, 1)
                        pe.wait_ge(hT_act, b + 1)
                        pe.wait_ge(hT_dve, b + 1)
                        for i, w in enumerate((wq, wk)):
                            for m in range(C):
                                for c in range(C):
                                    last = pe.matmul(ps[:, 2 + 2 * i + m, :], w[:, c, m * P:(m + 1) * P], hT[:, c, :],
                                                     start=(c == 0), stop=(c == C - 1))
                                last.then_inc(qk_ps, 1)
                        for t in range(TPB):
                            for c in range(C):
                                last = pe.matmul(ps[:, t // 2, (t % 2) * D:(t % 2 + 1) * D],
                                                 hT[:, c, t * P:(t + 1) * P], wv[:, c, :],
                                                 start=(c == 0), stop=(c == C - 1))
                        last.then_inc(v_ps, 1)
                        pe.wait_ge(qT_sb, b * C + C)
                        pe.wait_ge(kT_sb, b * C + C)
                        scores(b, 0)
                        for t in range(TPB):
                            n = b * TPB + t
                            if t + 1 < TPB:
                                scores(b, t + 1)
                            pe.wait_ge(e_ready, n + 1)
                            pe.wait_ge(pT_sb, n)
                            for j in range(8):
                                last = pe.transpose(ps[:, 6 + j // 4, (j % 4) * P:(j % 4 + 1) * P],
                                                    sc[:, t % 2, 2 * j:2 * j + 2, :].rearrange("p h k -> p (h k)"),
                                                    ident[:])
                            last.then_inc(pT_ps, 1)
                            pe.wait_ge(pT_sb, n + 1)
                            if t == 0:
                                pe.wait_ge(v_sb, b * 4 + 4)
                            for j in range(8):
                                last = pe.matmul(ps[:, 0, j * 64:(j + 1) * 64], pT[:, j, :],
                                                 vbd[:, t, j].rearrange("p s h d -> p (s h d)"),
                                                 start=True, stop=True)
                            last.then_inc(o_ps, 1)
                            pe.wait_ge(at_sb, n + 1)
                            for c in range(C):
                                last = pe.transpose(ps[:, 1, c * P:(c + 1) * P], at[:, c * P:(c + 1) * P], ident[:])
                            last.then_inc(aT_ps, 1)
                            pe.wait_ge(aT_sb, n + 1)
                            for c in range(C):
                                last = pe.matmul(ps[:, 1, D:2 * D], atT[:, c, :], wo[:, c, :],
                                                 start=(c == 0), stop=(c == C - 1))
                            last.then_inc(yo_ps, 1)

                @block.scalar
                def _(act):
                    with act.Fori(0, NB) as b:
                        act.wait_ge(hT_ps, b + 1)
                        act.copy(hT[:, 0, :], ps[:, 0, :]).then_inc(hT_act, 1)
                        for m in range(C):
                            act.wait_ge(qk_ps, b * 2 * C + m + 1)
                            act.activation(qT[:, m, :], ps[:, 2 + m, :], ACT.Copy, scale=DK1 ** -0.5).then_inc(qT_sb, 1)
                        for m in range(C):
                            act.wait_ge(qk_ps, b * 2 * C + C + m + 1)
                            act.copy(kT[:, m, :], ps[:, 4 + m, :]).then_inc(kT_sb, 1)
                        for t in range(TPB):
                            n = b * TPB + t
                            act.wait_ge(s_sh, n + 1)
                            act.activation(sc[:, t % 2], sc[:, t % 2], ACT.Exp).then_inc(e_ready, 1)
                            act.wait_ge(pT_ps, n + 1)
                            act.wait_ge(o_ps, n)
                            act.copy(pT[:].rearrange("p j q -> p (j q)"), ps[:, 6:8, :].rearrange("p a b -> p (a b)")
                                     ).then_inc(pT_sb, 1)
                            act.wait_ge(aT_ps, n + 1)
                            act.wait_ge(yo_ps, n)
                            act.copy(atT[:].rearrange("p c q -> p (c q)"), ps[:, 1, 0:C * P]).then_inc(aT_sb, 1)

                @block.vector
                def _(dve):
                    dve.wait_ge(rel_in, 16)
                    for lo, hi, bucket in runs:
                        dve.tensor_copy(reld[:, lo:hi], rel[:, bucket:bucket + 1].to_broadcast([H1, hi - lo])
                                        ).then_inc(rel_sb, 1)
                    dve.wait_ge(v_zero, 1)
                    dve.wait_ge(bias_in, 32)
                    PER = TPB * 7

                    def shift(b, t, st):
                        n = b * TPB + t
                        dve.wait_ge(s_ps, n + 1)
                        if t >= 2:
                            dve.wait_ge(pT_ps, n - 1)
                        q = sc[:, t % 2]
                        st.done(dve.tensor_tensor(q.rearrange("p h k -> p (h k)"),
                                                  ps[:, 2 + 2 * (t % 2):4 + 2 * (t % 2), :].rearrange("p a b -> p (a b)"),
                                                  bias[:].rearrange("p h k -> p (h k)"), ALU.add))
                        st.done(dve.tensor_reduce(mx[:, t % 2], q, AX.X, ALU.max))
                        dve.tensor_tensor(q, q, mx[:, t % 2].unsqueeze(2).to_broadcast([P, H1, S]), ALU.subtract
                                          ).then_inc(s_sh, 1)

                    with dve.Fori(0, NB // 2) as i:
                        for w in range(2):
                            b = i * 2 + w
                            st = Steps(dve, dve_step, b, PER)
                            dve.wait_ge(hT_ps, b + 1)
                            dve.tensor_copy(hT[:, 1, :], ps[:, 1, :]).then_inc(hT_dve, 1)
                            dve.wait_ge(v_ps, b + 1)
                            for s in range(2):
                                for h in range(2):
                                    src = ps[s * S:(s + 1) * S, 0:2, :].rearrange("p a (t j h d) -> p (a t j) h d",
                                                                                  t=2, j=8, h=2)[:, :, h, :]
                                    dst = vbd[h * S:(h + 1) * S, :, :, s, h, :].rearrange("p t j d -> p (t j) d")
                                    dve.tensor_copy(dst, src).then_inc(v_sb, 1)
                            shift(b, 0, st)
                            for t in range(TPB):
                                n = b * TPB + t
                                if t + 1 < TPB:
                                    shift(b, t + 1, st)
                                dve.wait_ge(e_ready, n + 1)
                                st.done(dve.tensor_reduce(rs[:, t % 2], sc[:, t % 2], AX.X, ALU.add))
                                st.done(dve.reciprocal(rs[:, t % 2], rs[:, t % 2]))
                                dve.wait_ge(o_ps, n + 1)
                                dve.wait_ge(aT_ps, n)
                                for s in range(2):
                                    src = ps[s * S:(s + 1) * S, 0, :].rearrange(
                                        "p (j s h d) -> p j s (h d)", j=8, s=2, h=2)[:, :, s, :]
                                    src = src.rearrange("p j (h d) -> p j h d", h=2)
                                    dst = at[s * S:(s + 1) * S, :].rearrange("p (j h d) -> p j h d", j=8, h=2)
                                    sel = rs[s * S:(s + 1) * S, t % 2, :].rearrange("p (j h) -> p j h", h=2)
                                    last = dve.tensor_tensor(dst, src, sel.unsqueeze(3).to_broadcast([S, 8, 2, DK1]),
                                                             ALU.mult)
                                last.then_inc(at_sb, 1)
                                dve.wait_ge(yo_ps, n + 1)
                                if t == 0:
                                    dve.wait_ge(res_sem[w], i * 16 + 16)
                                st.done(dve.tensor_tensor(xres[:, w, t, :], ps[:, 1, D:2 * D], xres[:, w, t, :], ALU.add))
                                dve.tensor_copy(acc[:, bass.ds(n, 1), :].rearrange("p o d -> p (o d)"), xres[:, w, t, :])
                                st.done(dve.bn_stats(bst[:], xres[:, w, t, :]))
                                dve.nop(nofuse=True)
                                st.done(dve.bn_aggr(mv[:], bst[:]))
                                dve.nop(nofuse=True)
                                dve.tensor_copy(mv1[:, bass.ds(n, 1), :].rearrange("p o d -> p (o d)"), mv[:]
                                                ).then_inc(tile_done, 1)
                            st.close()

        def deviations(tag):
            ph = ExitStack()
            with ph:
                tmp = ph.enter_context(nc.sbuf_tensor(tag + "tmp", [P, NT], F32))
                added = ctx.enter_context(nc.semaphore(tag + "added"))
                rooted = ctx.enter_context(nc.semaphore(tag + "rooted"))
                block = ph.enter_context(nc.Block())

                @block.vector
                def _(dve):
                    dve.tensor_scalar(tmp[:], mv1[:, :, 1], EPS, None, ALU.add).then_inc(added, 1)
                    dve.wait_ge(rooted, 1)
                    dve.reciprocal(rstd[:], tmp[:])

                @block.scalar
                def _(act):
                    act.wait_ge(added, 1)
                    act.activation(tmp[:], tmp[:], ACT.Sqrt).then_inc(rooted, 1)

        def attention2():
            ph = ExitStack()
            with ph:
                def sb(name, shape, dt=F32):
                    return ph.enter_context(nc.sbuf_tensor("a2_" + name, shape, dt))

                def sem(name):
                    return ctx.enter_context(nc.semaphore("a2_" + name))

                wq = sb("wq", [P, C, H2 * DH2])
                wkv = sb("wkv", [P, C, 2 * DH2])
                wkk = sb("wkk", [P, C, 2, DH2])
                wo = sb("wo", [P, J2, D])
                gin = sb("gin", [P, C])
                bias = sb("bias", [P, 2, J2, KN])
                mask8 = sb("mask8", [P, NT, S], U8)
                madd = sb("madd", [P, NT, KN])
                bm = sb("bm", [P, 2, 2, J2, KN])
                xb = sb("xb", [P, TPB, D])
                xT_ = sb("xnT", [P, C, BT])
                q = sb("q", [P, J2, BT])
                k = sb("k", [P, SPB, KN])
                v = sb("v", [P, SPB, DH2])
                sc = sb("sc", [P, 2, 2, 4, KN])
                mx = sb("mx", [P, 2, 8])
                rs = sb("rs", [P, 2, 8])
                pT = sb("pT", [KN, 2, 4, P])
                oT = sb("oT", [P, J2, P])
                bst = sb("bst", [P, 6])
                mv = sb("mv", [P, 2])
                w_in, small_in, bias_in, mask_in, bias2_in = (
                    sem(n) for n in ("w_in", "small_in", "bias_in", "mask_in", "bias2_in"))
                causal, madd_ready, kk_ready, null_ready = (
                    sem(n) for n in ("causal", "madd_ready", "kk_ready", "null_ready"))
                xb_ready, xT_ps, xT_act, xT_dve, q_ps, q_act, q_dve = (
                    sem(n) for n in ("xb_ready", "xT_ps", "xT_act", "xT_dve", "q_ps", "q_act", "q_dve"))
                kv_ps, k_sb, v_sb, bm_ready, s_ps, s_sh, s_add, e_ready, r_ready, p_ready = (
                    sem(n) for n in ("kv_ps", "k_sb", "v_sb", "bm_ready", "s_ps", "s_sh", "s_add", "e_ready",
                                     "r_ready", "p_ready"))
                pT_ps, pT_sb, o_ps, oT_sb, yo_ps, tile_done, dve_step = (
                    sem(n) for n in ("pT_ps", "pT_sb", "o_ps", "oT_sb", "yo_ps", "tile_done", "dve_step"))
                block = ph.enter_context(nc.Block())

                @block.sync
                def _(sp):
                    sp.dma_start(wq[:], wq2.rearrange("(c p) n -> p c n", p=P)).then_inc(w_in, 16)
                    sp.dma_start(wkv[:], wkv2.rearrange("(c p) n -> p c n", p=P)).then_inc(w_in, 16)
                    sp.dma_start(wo[:], wo2.rearrange("(j p) n -> p j n", p=P)).then_inc(w_in, 16)
                    sp.dma_start(gin[:], g_in).then_inc(small_in, 16)
                    for h in range(2):
                        sp.dma_start(bias[0:S, h, :, 0:S],
                                     bias2.rearrange("(j h) q k -> h q j k", h=2)[h]).then_inc(bias_in, 16)
                    for s in range(2):
                        for h in range(2):
                            sp.dma_start(bias[s * S:(s + 1) * S, h, :, S:KN],
                                         nbias.rearrange("(j h) -> h j", h=2)[h:h + 1].unsqueeze(2)
                                         .to_broadcast([S, J2, 1])).then_inc(bias2_in, 16)
                    for s in range(2):
                        sp.dma_start(mask8[s * S:(s + 1) * S],
                                     mask.rearrange("(t s) k -> s t k", s=2)[s:s + 1]
                                     .to_broadcast([S, NT, S])).then_inc(mask_in, 16)
                    for h in range(2):
                        sp.dma_start(k[h * DH2:(h + 1) * DH2, :, S:KN],
                                     cond[0, :].rearrange("(d o) -> d o", o=1).unsqueeze(1)
                                     .to_broadcast([DH2, SPB, 1])).then_inc(null_ready, 16)
                    sp.dma_start(v[S:KN, :, :], cond[1:2, :].unsqueeze(1).to_broadcast([1, SPB, DH2])
                                 ).then_inc(null_ready, 16)

                @block.gpsimd
                def _(pool):
                    pool.wait_ge(bias_in, 32)
                    for h in range(2):
                        pool.affine_select(out=bias[0:S, h, :, 0:S], in_=bias[0:S, h, :, 0:S], compare_op=ALU.is_ge,
                                           fill=MASKED, base=0, pattern=[[0, J2], [-1, S]], channel_multiplier=1
                                           ).then_inc(causal, 1)
                    pool.wait_ge(causal, 3)
                    pool.wait_ge(bias2_in, 64)
                    pool.wait_ge(madd_ready, 1)

                    def bias_mask(b, t):
                        n = b * TPB + t
                        if t < 2:
                            pool.wait_ge(s_add, b * 2 * TPB)
                        else:
                            pool.wait_ge(s_add, 2 * (n - 1))
                        pool.tensor_tensor(bm[:, t % 2].rearrange("p h j k -> p (h j) k"),
                                           bias[:].rearrange("p h j k -> p (h j) k"),
                                           madd[:, bass.ds(n, 1), :].to_broadcast([P, H2, KN]),
                                           ALU.add).then_inc(bm_ready, 1)

                    with pool.Fori(0, NB) as b:
                        bias_mask(b, 0)
                        for t in range(TPB):
                            if t + 1 < TPB:
                                bias_mask(b, t + 1)
                            for g in range(2):
                                m = (b * TPB + t) * 2 + g
                                pool.wait_ge(r_ready, m + 1)
                                p_ = sc[:, g].rearrange("p h j k -> p (h j) k")
                                pool.tensor_tensor(p_, p_, rs[:, g].unsqueeze(2).to_broadcast([P, 8, KN]),
                                                   ALU.mult).then_inc(p_ready, 1)

                @block.tensor
                def _(pe):
                    def scores(b, t, g):
                        if t > 0 or g > 0:
                            pe.wait_ge(s_add, (b * TPB + t) * 2 + g - 1)
                        pe.nop(nofuse=True)
                        for jj in range(4):
                            j = 4 * g + jj
                            for s in range(2):
                                for h in range(2):
                                    last = pe.matmul(
                                        ps[s * S:(s + 1) * S, 2 + 2 * g + h, jj * P:jj * P + KN],
                                        q[h * DH2:(h + 1) * DH2, j, t * P + s * S:t * P + (s + 1) * S],
                                        k[h * DH2:(h + 1) * DH2, 2 * t + s, :], start=True, stop=True)
                        last.then_inc(s_ps, 1)

                    pe.wait_ge(w_in, 48)
                    pe.wait_ge(kk_ready, 1)
                    with pe.Fori(0, NB) as b:
                        pe.wait_ge(xb_ready, b + 1)
                        pe.wait_ge(tile_done, b * TPB)
                        for c in range(C):
                            for t in range(TPB):
                                last = pe.transpose(ps[:, c, t * P:(t + 1) * P], xb[:, t, c * P:(c + 1) * P], ident[:])
                        last.then_inc(xT_ps, 1)
                        pe.wait_ge(xT_act, b + 1)
                        pe.wait_ge(xT_dve, b + 1)
                        for c in range(C):
                            pe.matmul(ps[:, 6, :], wkk[:, c].rearrange("p a d -> p (a d)"), xT_[:, c, :],
                                      start=(c == 0), stop=(c == C - 1))
                        for t in range(TPB):
                            for c in range(C):
                                last = pe.matmul(ps[:, 7, t * DH2:(t + 1) * DH2], xT_[:, c, t * P:(t + 1) * P],
                                                 wkv[:, c, DH2:2 * DH2], start=(c == 0), stop=(c == C - 1))
                        last.then_inc(kv_ps, 1)
                        for j in range(J2):
                            if j >= 4:
                                pe.wait_ge(q_act if j % 2 == 0 else q_dve, b * 4 + (j - 4) // 2 + 1)
                            for c in range(C):
                                last = pe.matmul(ps[:, 2 + j % 4, :], wq[:, c, j * P:(j + 1) * P], xT_[:, c, :],
                                                 start=(c == 0), stop=(c == C - 1))
                            last.then_inc(q_ps, 1)
                        pe.wait_ge(q_act, b * 4 + 4)
                        pe.wait_ge(q_dve, b * 4 + 4)
                        pe.wait_ge(k_sb, b + 1)
                        pe.wait_ge(null_ready, 48)
                        scores(b, 0, 0)
                        for t in range(TPB):
                            for g in range(2):
                                m = (b * TPB + t) * 2 + g
                                if g == 0:
                                    scores(b, t, 1)
                                elif t + 1 < TPB:
                                    scores(b, t + 1, 0)
                                pe.wait_ge(p_ready, m + 1)
                                pe.wait_ge(pT_sb, m)
                                if t == 0 and g == 0:
                                    pe.wait_ge(v_sb, b * 2 + 2)
                                for h in range(2):
                                    for jj in range(4):
                                        last = pe.transpose(ps[0:KN, 6 + h, jj * P:(jj + 1) * P], sc[:, g, h, jj, :],
                                                            ident[:])
                                last.then_inc(pT_ps, 1)
                                pe.wait_ge(pT_sb, m + 1)
                                pe.wait_ge(oT_sb, m)
                                for s in range(2):
                                    for h in range(2):
                                        last = pe.matmul(
                                            ps[h * DH2:(h + 1) * DH2, 0, :].rearrange(
                                                "p (j s q) -> p j s q", j=4, s=2)[:, :, s, :],
                                            v[0:KN, 2 * t + s, :], pT[:, h, :, s * S:(s + 1) * S],
                                            start=True, stop=True)
                                last.then_inc(o_ps, 1)
                            n = b * TPB + t
                            pe.wait_ge(oT_sb, 2 * n + 2)
                            pe.wait_ge(tile_done, n)
                            for j in range(J2):
                                last = pe.matmul(ps[:, 1, 0:D], oT[:, j, :], wo[:, j, :],
                                                 start=(j == 0), stop=(j == J2 - 1))
                            last.then_inc(yo_ps, 1)

                @block.scalar
                def _(act):
                    act.wait_ge(causal, 2)
                    act.copy(bias[S:P, :, :, 0:S].rearrange("p h j k -> p (h j) k"),
                             bias[0:S, :, :, 0:S].rearrange("p h j k -> p (h j) k")).then_inc(causal, 1)
                    act.wait_ge(w_in, 48)
                    for h in range(2):
                        last = act.copy(wkk[:, :, h, :], wkv[:, :, 0:DH2])
                    last.then_inc(kk_ready, 1)
                    act.wait_ge(small_in, 16)
                    with act.Fori(0, NB) as b:
                        act.wait_ge(xT_ps, b + 1)
                        act.activation(xT_[:, 0, :], ps[:, 0, :], ACT.Copy, scale=gin[:, 0:1]).then_inc(xT_act, 1)
                        act.wait_ge(kv_ps, b + 1)
                        act.copy(k[:, :, 0:S], ps[:, 6, :].rearrange("p (s k) -> p s k", s=SPB)).then_inc(k_sb, 1)
                        for j in range(0, J2, 2):
                            act.wait_ge(q_ps, b * J2 + j + 1)
                            act.activation(q[:, j, :], ps[:, 2 + j % 4, :], ACT.Copy, scale=DH2 ** -0.5
                                           ).then_inc(q_act, 1)
                        for t in range(TPB):
                            for g in range(2):
                                m = (b * TPB + t) * 2 + g
                                act.wait_ge(s_sh, m + 1)
                                act.activation(sc[:, g], sc[:, g], ACT.Exp).then_inc(e_ready, 1)
                                act.wait_ge(pT_ps, m + 1)
                                act.wait_ge(o_ps, m)
                                act.copy(pT[:].rearrange("p h j q -> p (h j q)"),
                                         ps[0:KN, 6:8, :].rearrange("p a b -> p (a b)")).then_inc(pT_sb, 1)

                @block.vector
                def _(dve):
                    dve.wait_ge(mask_in, 32)
                    dve.memset(madd[:, :, S:KN], 0.0)
                    dve.tensor_scalar(madd[:, :, 0:S], mask8[:], 1.0, -MASKED, ALU.subtract, ALU.mult
                                      ).then_inc(madd_ready, 1)
                    dve.wait_ge(small_in, 16)
                    PER = TPB * 6

                    def shift(b, t, g, st):
                        n = b * TPB + t
                        m = n * 2 + g
                        dve.wait_ge(s_ps, m + 1)
                        dve.wait_ge(bm_ready, n + 1)
                        if t > 0:
                            dve.wait_ge(pT_ps, m - 1)
                        dve.tensor_tensor(sc[:, g], ps[:, 2 + 2 * g:4 + 2 * g, :].rearrange(
                            "p h (j k) -> p h j k", j=4)[:, :, :, 0:KN], bm[:, t % 2, :, 4 * g:4 * g + 4, :],
                            ALU.add).then_inc(s_add, 1)
                        dve.wait_ge(s_add, m + 1)
                        s_ = sc[:, g].rearrange("p h j k -> p (h j) k")
                        st.done(dve.tensor_reduce(mx[:, g], s_, AX.X, ALU.max))
                        dve.tensor_tensor(s_, s_, mx[:, g].unsqueeze(2).to_broadcast([P, 8, KN]), ALU.subtract
                                          ).then_inc(s_sh, 1)

                    with dve.Fori(0, NB) as b:
                        st = Steps(dve, dve_step, b, PER)
                        dve.wait_ge(xT_ps, b)
                        for t in range(TPB):
                            n = b * TPB + t
                            last = dve.tensor_scalar(xb[:, t, :], acc[:, bass.ds(n, 1), :].rearrange("p o d -> p (o d)"),
                                                     mv1[:, bass.ds(n, 1), 0], rstd[:, bass.ds(n, 1)],
                                                     ALU.subtract, ALU.mult)
                        last.then_inc(xb_ready, 1)
                        dve.wait_ge(xT_ps, b + 1)
                        dve.tensor_scalar(xT_[:, 1, :], ps[:, 1, :], gin[:, 1:2], None, ALU.mult).then_inc(xT_dve, 1)
                        dve.wait_ge(kv_ps, b + 1)
                        for s in range(2):
                            dve.tensor_copy(v[0:S, :, :].rearrange("p (t s) d -> p t s d", s=2)[:, :, s, :],
                                            ps[s * S:(s + 1) * S, 7, 0:TPB * DH2].rearrange("p (t d) -> p t d", t=TPB)
                                            ).then_inc(v_sb, 1)
                        for j in range(1, J2, 2):
                            dve.wait_ge(q_ps, b * J2 + j + 1)
                            dve.tensor_scalar(q[:, j, :], ps[:, 2 + j % 4, :], DH2 ** -0.5, None, ALU.mult
                                              ).then_inc(q_dve, 1)
                        shift(b, 0, 0, st)
                        for t in range(TPB):
                            n = b * TPB + t
                            for g in range(2):
                                m = n * 2 + g
                                if g == 0:
                                    shift(b, t, 1, st)
                                elif t + 1 < TPB:
                                    shift(b, t + 1, 0, st)
                                dve.wait_ge(e_ready, m + 1)
                                st.done(dve.tensor_reduce(rs[:, g], sc[:, g].rearrange("p h j k -> p (h j) k"),
                                                          AX.X, ALU.add))
                                dve.reciprocal(rs[:, g], rs[:, g]).then_inc(r_ready, 1)
                                dve.wait_ge(o_ps, m + 1)
                                dve.wait_ge(yo_ps, n)
                                dve.tensor_copy(oT[:, 4 * g:4 * g + 4, :].rearrange("p j q -> p (j q)"), ps[:, 0, :]
                                                ).then_inc(oT_sb, 1)
                            dve.wait_ge(yo_ps, n + 1)
                            dve.tensor_copy(att[:, bass.ds(n, 1), :].rearrange("p o d -> p (o d)"), ps[:, 1, 0:D])
                            st.done(dve.bn_stats(bst[:], ps[:, 1, 0:D]))
                            dve.nop(nofuse=True)
                            st.done(dve.bn_aggr(mv[:], bst[:]))
                            dve.nop(nofuse=True)
                            dve.tensor_copy(mv1[:, bass.ds(n, 1), :].rearrange("p o d -> p (o d)"), mv[:]
                                            ).then_inc(tile_done, 1)
                        st.close()

        def router2():
            ph = ExitStack()
            with ph:
                def sb(name, shape, dt=F32):
                    return ph.enter_context(nc.sbuf_tensor("r2_" + name, shape, dt))

                def sem(name):
                    return ctx.enter_context(nc.semaphore("r2_" + name))

                gout = sb("gout", [P, C])
                rw = sb("rw", [P, C, P])
                cb = sb("cb", [P, E2])
                xb = sb("xb", [P, TPB, D])
                lT = sb("lT", [P, BT])
                score = sb("score", [P, NT, E2])
                sfc = sb("sfc", [P, NT, E2])
                left = sb("left", [P, NT, E2])
                hi = sb("hi", [P, NT * GROUPS, 4])
                lo = sb("lo", [P, NT * GROUPS, 4])
                hi2 = sb("hi2", [P, NT * GROUPS, 2])
                lo2 = sb("lo2", [P, NT * GROUPS, 2])
                t2 = sb("t2", [P, NT * GROUPS, 2])
                gs = sb("gs", [P, NT, GROUPS])
                gl = sb("gl", [P, NT, GROUPS])
                top8 = sb("top8", [P, NT, 8])
                stat = sb("stat", [P, NT])
                small_in, padded, xb_ready, xT_ps, xT_act, xT_dve = (
                    sem(n) for n in ("small_in", "padded", "xb_ready", "xT_ps", "xT_act", "xT_dve"))
                lT_ps, lT_sb, l_ps, l_sb, expd, dve_step = (
                    sem(n) for n in ("lT_ps", "lT_sb", "l_ps", "l_sb", "expd", "dve_step"))
                block = ph.enter_context(nc.Block())

                @block.sync
                def _(sp):
                    sp.dma_start(gout[:], g_out).then_inc(small_in, 16)
                    sp.wait_ge(padded, 1)
                    sp.dma_start(rw[:, :, 0:E2], rwT.rearrange("(c p) e -> p c e", p=P)).then_inc(small_in, 16)
                    sp.dma_start(cb[:], cbias.rearrange("(o e) -> o e", o=1).to_broadcast([P, E2])).then_inc(small_in, 16)

                @block.gpsimd
                def _(pool):
                    pool.memset(rw[:], 0.0).then_inc(padded, 1)

                @block.tensor
                def _(pe):
                    pe.wait_ge(small_in, 48)
                    with pe.Fori(0, NB) as b:
                        pe.wait_ge(xb_ready, b + 1)
                        for c in range(C):
                            for t in range(TPB):
                                last = pe.transpose(ps[:, c, t * P:(t + 1) * P], xb[:, t, c * P:(c + 1) * P], ident[:])
                        last.then_inc(xT_ps, 1)
                        pe.wait_ge(xT_act, b + 1)
                        pe.wait_ge(xT_dve, b + 1)
                        for c in range(C):
                            last = pe.matmul(ps[:, 2, :], rw[:, c, :], feat[:, c, bass.ds(b * BT, BT)],
                                             start=(c == 0), stop=(c == C - 1))
                        last.then_inc(lT_ps, 1)
                        pe.wait_ge(lT_sb, b + 1)
                        pe.wait_ge(l_sb, b)
                        for t in range(TPB):
                            last = pe.transpose(ps[:, 3, t * P:(t + 1) * P], lT[:, t * P:(t + 1) * P], ident[:])
                        last.then_inc(l_ps, 1)

                @block.scalar
                def _(act):
                    act.wait_ge(small_in, 48)
                    with act.Fori(0, NB) as b:
                        act.wait_ge(xT_ps, b + 1)
                        act.activation(feat[:, 0, bass.ds(b * BT, BT)], ps[:, 0, :], ACT.Copy, scale=gout[:, 0:1]
                                       ).then_inc(xT_act, 1)
                        act.wait_ge(lT_ps, b + 1)
                        act.wait_ge(l_ps, b)
                        act.copy(lT[:], ps[:, 2, :]).then_inc(lT_sb, 1)
                    act.wait_ge(l_sb, NB)
                    act.activation(score[:], score[:], ACT.Exp, scale=-1.0).then_inc(expd, 1)

                @block.vector
                def _(dve):
                    dve.wait_ge(small_in, 48)
                    with dve.Fori(0, NB) as b:
                        dve.wait_ge(xT_ps, b)
                        for t in range(TPB):
                            n = b * TPB + t
                            last = dve.tensor_scalar(xb[:, t, :], att[:, bass.ds(n, 1), :].rearrange("p o d -> p (o d)"),
                                                     mv1[:, bass.ds(n, 1), 0], rstd[:, bass.ds(n, 1)],
                                                     ALU.subtract, ALU.mult)
                        last.then_inc(xb_ready, 1)
                        dve.wait_ge(xT_ps, b + 1)
                        dve.tensor_scalar(feat[:, 1, bass.ds(b * BT, BT)], ps[:, 1, :], gout[:, 1:2], None, ALU.mult
                                          ).then_inc(xT_dve, 1)
                        dve.wait_ge(l_ps, b + 1)
                        dve.tensor_copy(score[:, bass.ds(b * TPB, TPB), :],
                                        ps[:, 3, :].rearrange("p (t e) -> p t e", t=TPB)[:, :, 0:E2]).then_inc(l_sb, 1)
                    dve.wait_ge(expd, 1)
                    st = Steps(dve, dve_step)
                    st.done(dve.tensor_scalar(score[:], score[:], 1.0, None, ALU.add))
                    st.done(dve.reciprocal(score[:], score[:]))
                    st.done(dve.tensor_tensor(sfc[:], score[:], cb[:].unsqueeze(1).to_broadcast([P, NT, E2]), ALU.add))
                    grp = sfc[:].rearrange("p t (g e) -> p (t g) e", g=GROUPS)
                    dve.tensor_tensor(hi[:], grp[:, :, 0:4], grp[:, :, 4:8], ALU.max)
                    st.done(dve.tensor_tensor(lo[:], grp[:, :, 0:4], grp[:, :, 4:8], ALU.min))

                    def merge(h, l, h_out, l_out, tmp, n):
                        dve.tensor_tensor(h_out, h[:, :, 0:n], h[:, :, n:2 * n], ALU.max)
                        dve.tensor_tensor(tmp, h[:, :, 0:n], h[:, :, n:2 * n], ALU.min)
                        st.done(dve.tensor_tensor(l_out, l[:, :, 0:n], l[:, :, n:2 * n], ALU.max))
                        st.done(dve.tensor_tensor(l_out, l_out, tmp, ALU.max))
                    merge(hi[:], lo[:], hi2[:], lo2[:], t2[:], 2)
                    merge(hi2[:], lo2[:], hi[:, :, 0:1], lo[:, :, 0:1], t2[:, :, 0:1], 1)
                    st.done(dve.tensor_tensor(gs[:].rearrange("p t (g o) -> p (t g) o", o=1), hi[:, :, 0:1],
                                              lo[:, :, 0:1], ALU.add))
                    for t in range(NT):
                        last = dve.max(top8[:, t, :], gs[:, t, :])
                    st.done(last)
                    st.done(dve.memset(top8[:, :, TOPG:8], UNMATCHED))
                    for t in range(NT):
                        last = dve.match_replace(gl[:, t, :], top8[:, t, :], gs[:, t, :], TAKEN)
                    st.done(last)
                    st.done(dve.tensor_scalar(gl[:], gl[:], TAKEN, None, ALU.is_equal))
                    st.done(dve.tensor_tensor(sfc[:].rearrange("p t (g e) -> p (t g) e", g=GROUPS),
                                              sfc[:].rearrange("p t (g e) -> p (t g) e", g=GROUPS),
                                              gl[:].rearrange("p t g -> p (t g)").unsqueeze(2)
                                              .to_broadcast([P, NT * GROUPS, 8]), ALU.mult))
                    for t in range(NT):
                        last = dve.max(top8[:, t, :], sfc[:, t, :])
                    st.done(last)
                    for t in range(NT):
                        last = dve.match_replace(left[:, t, :], top8[:, t, :], sfc[:, t, :], TAKEN)
                    st.done(last)
                    st.done(dve.tensor_scalar(left[:], left[:], TAKEN, None, ALU.is_equal))
                    st.done(dve.tensor_tensor(score[:], score[:], left[:], ALU.mult))
                    st.done(dve.tensor_reduce(stat[:], score[:], AX.X, ALU.add))
                    st.done(dve.tensor_scalar(stat[:], stat[:], 1e-20, None, ALU.add))
                    st.done(dve.reciprocal(stat[:], stat[:]))
                    st.done(dve.tensor_scalar(stat[:], stat[:], ROUTE_SCALE, None, ALU.mult))
                    dve.tensor_tensor(comb2[:, :, 0:E2], score[:], stat[:].unsqueeze(2).to_broadcast([P, NT, E2]),
                                      ALU.mult)
                    dve.memset(comb2[:, :, E2:N2], 1.0)

        def store():
            ph = ExitStack()
            with ph:
                stored = ph.enter_context(nc.semaphore("stored"))
                block = ph.enter_context(nc.Block())

                @block.sync
                def _(sp):
                    ov = out.rearrange("(t p) d -> p t d", p=P)
                    for i in range(4):
                        n = NT // 4
                        sp.dma_start(ov[:, i * n:(i + 1) * n, :], acc[:, i * n:(i + 1) * n, :]).then_inc(stored, 16)
                    sp.wait_ge(stored, 64)

        router1()
        experts("e1_", N1, comb1, [w1gate, w1up], w1down, True)
        attention1()
        deviations("ln1_")
        attention2()
        deviations("ln2_")
        router2()
        experts("e2_", N2, comb2, [up2], down2, False)
        store()


def kernel(x, cond_64, fside_16xSxS_0, mask_BxS_bk0, L0_cond_wt, L0_cond_wg, L0_cond_w_gate, L0_cond_w_up,
           L0_cond_w_down, L0_cond_sw_gate, L0_cond_sw_up, L0_cond_sw_down, L0_attn_Wq, L0_attn_Wk, L0_attn_Wv,
           L0_attn_Wo, L0_attn_rel_emb, L0_cond2_g_in, L0_cond2_null_attn_bias, L0_cond2_Wq, L0_cond2_Wkv,
           L0_cond2_Wo, L0_cond2_g_out, L0_ffn_router_w, L0_ffn_correction_bias, L0_ffn_up_w, L0_ffn_down_w,
           L0_ffn_shared_up_w, L0_ffn_shared_down_w):
    import numpy as _np
    import concourse.bacc as _bacc
    from concourse import mybir as _mybir
    from concourse.bass_utils import run_bass_kernel_spmd as _run

    def arr(a):
        return _np.asarray(a)

    def columns(w, n):
        w = arr(w)
        return w.reshape(w.shape[0], n, w.shape[1] // n).transpose(1, 0, 2)

    def rows(w, n):
        w = arr(w)
        return w.reshape(n, w.shape[0] // n, w.shape[1])

    flat = arr(x).reshape(T, D)
    laid = {
        "x": flat,
        "xT": flat.T,
        "condT": arr(cond_64).T,
        "cond": arr(cond_64),
        "bias2": arr(fside_16xSxS_0),
        "mask": arr(mask_BxS_bk0),
        "w1gate": _np.concatenate([arr(L0_cond_w_gate), columns(L0_cond_sw_gate, SH1)]),
        "w1up": _np.concatenate([arr(L0_cond_w_up), columns(L0_cond_sw_up, SH1)]),
        "w1down": _np.concatenate([arr(L0_cond_w_down), rows(L0_cond_sw_down, SH1)]),
        "wtT": arr(L0_cond_wt).T,
        "wgT": arr(L0_cond_wg).T,
        "wqT": arr(L0_attn_Wq).T,
        "wkT": arr(L0_attn_Wk).T,
        "wvT": arr(L0_attn_Wv).T,
        "woT": arr(L0_attn_Wo).T,
        "relT": arr(L0_attn_rel_emb).T,
        "g_in": arr(L0_cond2_g_in).reshape(C, P).T,
        "nbias": arr(L0_cond2_null_attn_bias),
        "wq2": arr(L0_cond2_Wq),
        "wkv2": arr(L0_cond2_Wkv),
        "wo2": arr(L0_cond2_Wo),
        "g_out": arr(L0_cond2_g_out).reshape(C, P).T,
        "rwT": arr(L0_ffn_router_w).T,
        "cbias": arr(L0_ffn_correction_bias),
        "up2": _np.concatenate([arr(L0_ffn_up_w), columns(L0_ffn_shared_up_w, SH2)]),
        "down2": _np.concatenate([arr(L0_ffn_down_w), rows(L0_ffn_shared_down_w, SH2)]),
    }
    nc = _bacc.Bacc("TRN2", target_bir_lowering=False, num_devices=1)
    arrays, args = {}, {}
    for name, a in laid.items():
        a = _np.ascontiguousarray(a)
        arrays[f"in_{name}"] = a
        args[name] = nc.dram_tensor(f"in_{name}", a.shape, _mybir.dt.from_np(a.dtype), kind="ExternalInput").ap()
    args["out"] = nc.dram_tensor("out_x", (T, D), _mybir.dt.float32, kind="ExternalOutput").ap()
    build(nc, **args)
    r = _run(nc, [arrays], core_ids=[0])
    return r.results[0]["out_x"].reshape(SEQS, S, D)
```

```python
import math
from contextlib import ExitStack

import numpy as np
import concourse.bass as bass
from concourse import mybir

F32 = mybir.dt.float32
U8 = mybir.dt.uint8
ALU = mybir.AluOpType
ACT = mybir.ActivationFunctionType
AX = mybir.AxisListType

P = 128
SEQS, S, D = 64, 64, 256
T = SEQS * S
NT = T // P
BT = 512
NB = T // BT
TPB = BT // P
SPB = BT // S
C = D // P

E1, M1 = 8, 128
SH1 = 2
N1 = E1 + SH1
K1 = 2
G = 64

H1, DK1 = 16, 16
H2, DH2 = 16, 64
J2 = H2 // 2
KN = S + 1
BUCKETS = 32
REL = 2 * S - 1

E2, M2 = 64, 128
GROUPS, TOPG, K2 = 8, 4, 8
SH2 = 4
N2 = E2 + SH2
ROUTE_SCALE = 2.5
NBLK = -(-(T * K2 // P + E2 - 1) // 8) * 8
GB = 4
NG = NBLK // GB
ROW = D + 2
I32 = mybir.dt.int32
EPS = 1e-5
MASKED = -1.0e30
TAKEN = -3.0e38
UNMATCHED = 3.0e38


def bucket_runs():
    half, exact = BUCKETS // 2, BUCKETS // 4
    rel = np.arange(-(S - 1), S)
    n = np.abs(rel)
    far = np.log(np.maximum(n, 1).astype(np.float32) / np.float32(exact)) / np.float32(math.log(128 / exact))
    far = np.minimum(exact + (far * np.float32(half - exact)).astype(np.int32), half - 1)
    bucket = np.where(n < exact, n, far) + (rel > 0) * half
    runs, at = [], 0
    for i in range(1, REL + 1):
        if i == REL or bucket[i] != bucket[at]:
            runs.append((at, i, int(bucket[at])))
            at = i
    return runs


class Steps:

    def __init__(self, eng, sem, turn=0, per=0, start=0):
        self.eng, self.sem, self.per, self.k = eng, sem, per, 0
        self.base = turn * per + start if per else start

    def done(self, ins):
        self.k += 1
        ins.then_inc(self.sem, 1)
        self.eng.wait_ge(self.sem, self.base + self.k)

    def close(self):
        assert self.k == self.per, (self.k, self.per)


def wait(eng, sem, value):
    if not (isinstance(value, int) and value <= 0):
        eng.wait_ge(sem, value)


def turns(eng, n, body):
    body(0)
    with eng.Fori(1, n) as i:
        body(i)


def blocks(eng, body):
    body(0, False)
    with eng.Fori(1, NB - 1) as b:
        body(b, False)
    body(NB - 1, True)


def build(nc, x, xT, condT, cond, bias2, mask, w1gate, w1up, w1down, wtT, wgT,
          wqT, wkT, wvT, woT, relT, g_in, nbias, wq2, wkv2, wo2, rwT, cbias, up2, down2,
          up2s, down2s, g_row, out):
    ctx = ExitStack()
    with ctx:
        def sb(name, shape, dt=F32):
            return ctx.enter_context(nc.sbuf_tensor(name, shape, dt))

        def sem(name):
            return ctx.enter_context(nc.semaphore(name))

        rel_rows = nc.dram_tensor("rel_rows", (S, H1, REL), F32).ap()
        x_slots = nc.dram_tensor("x_slots", (NBLK * P, ROW), F32).ap()
        y_rows = nc.dram_tensor("y_rows", (T * K2 + P, D), F32).ap()
        block_expert = nc.dram_tensor("block_expert", (3 * P,), I32).ap()

        ctx.enter_context(nc.allow_non_contiguous_dma(reason="a few columns of constants"))
        ps = ctx.enter_context(nc.psum_tensor("ps", [P, 8, 512], F32))

        wide = sb("wide", [P, E2 * D])
        feat = wide[:, 0:C * T].rearrange("p (c t) -> p c t", c=C)
        acc = sb("acc", [P, NT, D])
        att = wide[:, C * T:].rearrange("p (t d) -> p t d", d=D)
        ident = sb("ident", [P, P])
        comb1 = sb("comb1", [P, NT, N1])
        mv1 = sb("mv1", [P, NT, 2])
        rstd = sb("rstd", [P, NT])

        def make_identity(pool, seen, done):
            pool.memset(ident[:], 0.0).then_inc(seen, 1)
            pool.wait_ge(seen, 1)
            pool.affine_select(out=ident[:], in_=ident[:], compare_op=ALU.not_equal, fill=1.0, base=0,
                               pattern=[[-1, P]], channel_multiplier=1).then_inc(done, 1)

        def router1():
            ph = ExitStack()
            with ph:
                def sb(name, shape, dt=F32):
                    return ph.enter_context(nc.sbuf_tensor(name, shape, dt))

                def sem(name):
                    return ctx.enter_context(nc.semaphore("r1_" + name))

                wt = sb("wt", [P, C, P])
                wg = sb("wg", [P, P])
                cT = sb("cT", [P, SEQS])
                lT = sb("lT", [P, BT])
                s1 = sb("s1", [P, NT, E1])
                left = sb("left", [P, NT, E1])
                top8 = sb("top8", [P, NT, 8])
                stat = sb("stat", [P, NT])
                small_in, x_in = sem("small_in"), sem("x_in")
                zeroed, id_ready, padded = sem("zeroed"), sem("id_ready"), sem("padded")
                lT_ps, lT_sb, l_ps, l_sb = sem("lT_ps"), sem("lT_sb"), sem("l_ps"), sem("l_sb")
                shifted, expd, dve_step = sem("shifted"), sem("expd"), sem("dve_step")
                block = ph.enter_context(nc.Block())

                @block.sync
                def _(sp):
                    for c in range(C):
                        sp.dma_start(feat[:, c, :], xT[c * P:(c + 1) * P, :]).then_inc(x_in, 16)
                    sp.wait_ge(padded, 3)
                    sp.dma_start(wt[:, :, 0:E1], wtT.rearrange("(c p) e -> p c e", p=P)).then_inc(small_in, 16)
                    sp.dma_start(wg[0:G, 0:E1], wgT).then_inc(small_in, 16)
                    sp.dma_start(cT[0:G], condT).then_inc(small_in, 16)

                @block.gpsimd
                def _(pool):
                    for pad in (wt, wg, cT):
                        pool.memset(pad[:], 0.0).then_inc(padded, 1)
                    make_identity(pool, zeroed, id_ready)
                    pool.memset(acc[:], 0.0)

                @block.tensor
                def _(pe):
                    pe.wait_ge(small_in, 48)
                    pe.wait_ge(x_in, 16 * C)
                    pe.wait_ge(id_ready, 1)

                    def body(b):
                        for c in range(C):
                            pe.matmul(ps[:, 0, :], wt[:, c, :], feat[:, c, bass.ds(b * BT, BT)],
                                      start=(c == 0), stop=False)
                        pe.matmul(ps[:, 0, :], wg[:],
                                  cT[:, bass.ds(b * SPB, SPB)].unsqueeze(2).to_broadcast([P, SPB, S]),
                                  start=False, stop=True).then_inc(lT_ps, 1)
                        pe.wait_ge(lT_sb, b + 1)
                        wait(pe, l_sb, b)
                        for t in range(TPB):
                            last = pe.transpose(ps[:, 1, t * P:(t + 1) * P], lT[:, t * P:(t + 1) * P], ident[:])
                        last.then_inc(l_ps, 1)
                    turns(pe, NB, body)

                @block.scalar
                def _(act):
                    def body(b):
                        act.wait_ge(lT_ps, b + 1)
                        wait(act, l_ps, b)
                        act.activation(lT[:], ps[:, 0, :], ACT.Copy, scale=0.5).then_inc(lT_sb, 1)
                    turns(act, NB, body)
                    act.wait_ge(shifted, 1)
                    act.activation(s1[:], s1[:], ACT.Exp).then_inc(expd, 1)

                @block.vector
                def _(dve):
                    with dve.Fori(0, NB) as b:
                        dve.wait_ge(l_ps, b + 1)
                        dve.tensor_copy(s1[:, bass.ds(b * TPB, TPB), :],
                                        ps[:, 1, :].rearrange("p (t e) -> p t e", t=TPB)[:, :, 0:E1]).then_inc(l_sb, 1)
                    dve.wait_ge(l_sb, NB)
                    st = Steps(dve, dve_step)
                    st.done(dve.tensor_reduce(stat[:], s1[:], AX.X, ALU.max))
                    dve.tensor_tensor(s1[:], s1[:], stat[:].unsqueeze(2).to_broadcast([P, NT, E1]),
                                      ALU.subtract).then_inc(shifted, 1)
                    dve.wait_ge(expd, 1)
                    st.done(dve.tensor_reduce(stat[:], s1[:], AX.X, ALU.add))
                    st.done(dve.reciprocal(stat[:], stat[:]))
                    st.done(dve.tensor_tensor(s1[:], s1[:], stat[:].unsqueeze(2).to_broadcast([P, NT, E1]), ALU.mult))
                    for t in range(NT):
                        last = dve.max(top8[:, t, :], s1[:, t, :])
                    st.done(last)
                    st.done(dve.memset(top8[:, :, K1:8], UNMATCHED))
                    for t in range(NT):
                        last = dve.match_replace(left[:, t, :], top8[:, t, :], s1[:, t, :], -1.0)
                    st.done(last)
                    st.done(dve.tensor_scalar(left[:], left[:], -1.0, None, ALU.is_equal))
                    st.done(dve.tensor_tensor(s1[:], s1[:], left[:], ALU.mult))
                    st.done(dve.tensor_reduce(stat[:], s1[:], AX.X, ALU.add))
                    st.done(dve.tensor_scalar(stat[:], stat[:], 1e-20, None, ALU.add))
                    st.done(dve.reciprocal(stat[:], stat[:]))
                    dve.tensor_tensor(comb1[:, :, 0:E1], s1[:], stat[:].unsqueeze(2).to_broadcast([P, NT, E1]),
                                      ALU.mult)
                    dve.memset(comb1[:, :, E1:N1], 1.0)

        def experts(tag, n_exp, comb, comb_at, in_ws, down_w, gated):
            ph = ExitStack()
            n_in = len(in_ws)
            TURNS = n_exp // 2
            PER = 2 * NB
            with ph:
                def sb(name, shape, dt=F32):
                    return ph.enter_context(nc.sbuf_tensor(tag + name, shape, dt))

                def sem(name):
                    return ctx.enter_context(nc.semaphore(tag + name))

                w_in = sb("w_in", [P, 2, n_in, C, P])
                w_dn = sb("w_dn", [P, 2, D])
                r = sb("r", [P, 2, BT])
                h = sb("h", [P, 2, BT])
                cexp = sb("cexp", [P, 2, NT])
                w_in_sem = [sem("weights0"), sem("weights1")]
                z_ps, y_ps, r_ready, h_ready, y_used, c_ready = (
                    sem(n) for n in ("z_ps", "y_ps", "r_ready", "h_ready", "y_used", "c_ready"))
                leaky = sem("leaky")
                block = ph.enter_context(nc.Block())

                def z_bank(i, n):
                    return ps[:, n_in * (n % 2) + i, :]

                def y_bank(n, t):
                    return ps[:, 4 + 2 * (n % 2) + t // 2, (t % 2) * D:(t % 2 + 1) * D]

                @block.sync
                def _(sp):
                    def load(e, w):
                        for i, src in enumerate(in_ws):
                            sp.dma_start(w_in[:, w, i], src[bass.ds(e, 1)].rearrange("o (c p) m -> p (o c) m", p=P)
                                         ).then_inc(w_in_sem[w], 16)
                        sp.dma_start(w_dn[:, w, :], down_w[bass.ds(e, 1)].rearrange("o p n -> p (o n)")
                                     ).then_inc(w_in_sem[w], 16)
                    load(0, 0)
                    load(1, 1)
                    with sp.Fori(0, TURNS - 1) as i:
                        for w in range(2):
                            sp.wait_ge(y_ps, (i * 2 + w + 1) * NB)
                            load(i * 2 + 2 + w, w)

                @block.tensor
                def _(pe):
                    def z(n, turn, w_ready):
                        w, b = n // NB % 2, n % NB
                        if b == 0:
                            pe.wait_ge(w_in_sem[w], w_ready)
                        for i in range(n_in):
                            for c in range(C):
                                last = pe.matmul(z_bank(i, n), w_in[:, w, i, c, :], feat[:, c, b * BT:(b + 1) * BT],
                                                 start=(c == 0), stop=(c == C - 1))
                        last.then_inc(z_ps, 1)

                    def y(n, turn, first=False):
                        w = n // NB
                        pe.wait_ge(h_ready, turn * PER + n + 1)
                        if not (first and n < 2):
                            pe.wait_ge(y_used, turn * PER + n - 1)
                        for t in range(TPB):
                            last = pe.matmul(y_bank(n, t), h[:, n % 2, t * P:(t + 1) * P], w_dn[:, w, :],
                                             start=True, stop=True)
                        last.then_inc(y_ps, 1)

                    ALL = 16 * (n_in + 1)

                    def turn_body(turn, first=False, final=False):
                        for n in range(PER):
                            if not (final and n == PER - 1):
                                nxt = n + 1
                                z(nxt, turn, (turn + (2 if nxt == PER else 1)) * ALL)
                            y(n, turn, first)

                    z(0, 0, ALL)
                    turn_body(0, first=True)
                    if TURNS > 2:
                        with pe.Fori(1, TURNS - 1) as turn:
                            turn_body(turn)
                    turn_body(TURNS - 1, final=True)

                @block.scalar
                def _(act):
                    def turn_body(turn, first=False):
                        for n in range(PER):
                            act.wait_ge(z_ps, turn * PER + n + 1)
                            if gated:
                                if not (first and n < 2):
                                    act.wait_ge(h_ready, turn * PER + n - 1)
                                act.activation(r[:, n % 2, :], z_bank(0, n), ACT.Copy, scale=0.01
                                               ).then_inc(r_ready, 1)
                            else:
                                act.activation(r[:, n % 2, :], z_bank(0, n), ACT.Relu).then_inc(r_ready, 1)
                                act.wait_ge(r_ready, turn * PER + n + 1)
                                if not (first and n < 2):
                                    act.wait_ge(y_ps, turn * PER + n - 1)
                                act.activation(h[:, n % 2, :], r[:, n % 2, :], ACT.Square).then_inc(h_ready, 1)
                    turn_body(0, first=True)
                    with act.Fori(1, TURNS) as turn:
                        turn_body(turn)

                @block.vector
                def _(dve):
                    def accumulate(n, turn, first):
                        w, b = n // NB, n % NB
                        if b == 0:
                            dve.tensor_copy(cexp[:, w, :], comb[:, :, bass.ds(turn * 2 + w + comb_at, 1)].rearrange(
                                "p t o -> p (t o)")).then_inc(c_ready, 1)
                            dve.wait_ge(c_ready, turn * 2 + w + 1)
                        dve.wait_ge(y_ps, turn * PER + n + 1)
                        for t in range(TPB):
                            tile = b * TPB + t
                            last = dve.scalar_tensor_tensor(acc[:, tile, :], y_bank(n, t), cexp[:, w, tile:tile + 1],
                                                            acc[:, tile, :], ALU.mult, ALU.add)
                        last.then_inc(y_used, 1)

                    def gate(n, turn, first):
                        dve.wait_ge(r_ready, turn * PER + n + 1)
                        if not (first and n < 2):
                            dve.wait_ge(y_ps, turn * PER + n - 1)
                        dve.tensor_tensor(r[:, n % 2, :], z_bank(0, n), r[:, n % 2, :], ALU.max).then_inc(leaky, 1)
                        dve.wait_ge(leaky, turn * PER + n + 1)
                        dve.tensor_tensor(h[:, n % 2, :], r[:, n % 2, :], z_bank(1, n), ALU.mult).then_inc(h_ready, 1)

                    def turn_body(turn, first=False, final=False):
                        for n in range(PER):
                            if gated:
                                if n + 1 < PER or not final:
                                    gate(n + 1, turn, first)
                            accumulate(n, turn, first)
                    if gated:
                        gate(0, 0, True)
                    turn_body(0, first=True)
                    if TURNS > 2:
                        with dve.Fori(1, TURNS - 1) as turn:
                            turn_body(turn)
                    turn_body(TURNS - 1, final=True)

        def attention1():
            ph = ExitStack()
            with ph:
                def sb(name, shape, dt=F32):
                    return ph.enter_context(nc.sbuf_tensor("a1_" + name, shape, dt))

                def sem(name):
                    return ctx.enter_context(nc.semaphore("a1_" + name))

                wq, wk, wv, wo = (sb(n, [P, C, D]) for n in ("wq", "wk", "wv", "wo"))
                rel = sb("rel", [H1, BUCKETS])
                reld = sb("reld", [H1, REL])
                bias = sb("bias", [P, H1, S])
                own = sb("own", [P, 8])
                xb = sb("xb", [P, TPB, D])
                xres = sb("xres", [P, TPB, D])
                xo = sb("xo", [P, 2, D])
                hT = sb("hT", [P, C, BT])
                qT = sb("qT", [P, C, BT])
                kT = sb("kT", [P, C, BT])
                kbd = sb("kbd", [P, 2, C, 2, 8, S])
                vbd = sb("vbd", [P, TPB, 8, 2, 2, DK1])
                sc = sb("sc", [P, 2, H1, S])
                mx = sb("mx", [P, 2, H1])
                rs = sb("rs", [P, 2, H1])
                pT = sb("pT", [P, 2, 8, P])
                at = sb("at", [P, D])
                atT = sb("atT", [P, C, P])
                bst = sb("bst", [P, 6])
                mv = sb("mv", [P, 2])
                w_in, rel_in, rel_sb, rel_out, bias_in, res_in = (
                    sem(n) for n in ("w_in", "rel_in", "rel_sb", "rel_out", "bias_in", "res_in"))
                s_add, added, kept = sem("s_add"), sem("added"), sem("kept")
                own_step, own_ready, v_zero = sem("own_step"), sem("own_ready"), sem("v_zero")
                xb_ready, hT_ps, hT_act, hT_dve = sem("xb_ready"), sem("hT_ps"), sem("hT_act"), sem("hT_dve")
                qk_ps, qT_sb, kT_sb, v_ps, v_sb = sem("qk_ps"), sem("qT_sb"), sem("kT_sb"), sem("v_ps"), sem("v_sb")
                kbd_ready, s_ps, s_sh, e_ready, rs_ready = (
                    sem(n) for n in ("kbd_ready", "s_ps", "s_sh", "e_ready", "rs_ready"))
                pT_ps, pT_sb, o_ps, at_sb, aT_ps, aT_sb, yo_ps, tile_done, dve_step = (
                    sem(n) for n in ("pT_ps", "pT_sb", "o_ps", "at_sb", "aT_ps", "aT_sb", "yo_ps", "tile_done",
                                     "dve_step"))
                block = ph.enter_context(nc.Block())
                runs = bucket_runs()

                @block.sync
                def _(sp):
                    for dst, src in ((wq, wqT), (wk, wkT), (wv, wvT), (wo, woT)):
                        sp.dma_start(dst[:], src.rearrange("(c p) n -> p c n", p=P)).then_inc(w_in, 16)
                    sp.dma_start(rel[:], relT).then_inc(rel_in, 16)
                    sp.wait_ge(rel_sb, len(runs))
                    sp.dma_start(rel_rows.rearrange("q h r -> h q r"),
                                 reld[:].unsqueeze(1).to_broadcast([H1, S, REL])).then_inc(rel_out, 16)
                    sp.wait_ge(rel_out, 16)
                    for s in range(2):
                        diag = bass.AP(rel_rows.tensor, S - 1, [[H1 * REL - 1, S], [REL, H1], [1, S]])
                        sp.dma_start(bias[s * S:(s + 1) * S], diag).then_inc(bias_in, 16)
                    xv = x.rearrange("(t p) d -> p t d", p=P)

                    def residual(b):
                        wait(sp, added, b * TPB)
                        sp.dma_start(xres[:], xv[:, bass.ds(b * TPB, TPB), :]).then_inc(res_in, 16)
                    turns(sp, NB, residual)

                @block.gpsimd
                def _(pool):
                    pool.memset(own[:], 1.0).then_inc(own_step, 1)
                    pool.wait_ge(own_step, 1)
                    pool.affine_select(out=own[:], in_=own[:], compare_op=ALU.is_ge, fill=0.0, base=0,
                                       pattern=[[-DK1, 8]], channel_multiplier=1).then_inc(own_step, 1)
                    pool.wait_ge(own_step, 2)
                    pool.affine_select(out=own[:], in_=own[:], compare_op=ALU.is_ge, fill=0.0, base=DK1 - 1,
                                       pattern=[[DK1, 8]], channel_multiplier=-1).then_inc(own_ready, 1)
                    pool.wait_ge(own_ready, 1)
                    pool.memset(vbd[:], 0.0).then_inc(v_zero, 1)

                    def hidden(b):
                        wait(pool, hT_ps, b)
                        pool.tensor_copy(xb[:], acc[:, bass.ds(b * TPB, TPB), :]).then_inc(xb_ready, 1)

                    def keys_apart(b, t):
                        pool.wait_ge(kT_sb, b * C + C)
                        wait(pool, s_ps, b * TPB + t - 1)
                        for c in range(C):
                            kk = kT[:, c, t * P:(t + 1) * P].rearrange("p (s k) -> p s k", s=2)
                            pool.tensor_tensor(kbd[:, t % 2, c], kk.unsqueeze(2).to_broadcast([P, 2, 8, S]),
                                               own[:].unsqueeze(1).unsqueeze(3).to_broadcast([P, 2, 8, S]),
                                               ALU.mult).then_inc(kbd_ready, 1)

                    def body(b, final):
                        for t in range(TPB):
                            keys_apart(b, t)
                            if t == 1 and not final:
                                hidden(b + 1)
                    hidden(0)
                    blocks(pool, body)

                @block.tensor
                def _(pe):
                    def scores(b, t):
                        n = b * TPB + t
                        pe.wait_ge(kbd_ready, (n + 1) * C)
                        if t >= 2:
                            pe.wait_ge(s_add, n - 1)
                        else:
                            pe.wait_ge(qT_sb, b * C + C)
                            pe.wait_ge(kT_sb, b * C + C)
                        for c in range(C):
                            for s in range(2):
                                last = pe.matmul(ps[s * S:(s + 1) * S, 2 + 2 * (t % 2) + c, :],
                                                 qT[:, c, t * P + s * S:t * P + (s + 1) * S],
                                                 kbd[:, t % 2, c, s].rearrange("p h k -> p (h k)"),
                                                 start=True, stop=True)
                        last.then_inc(s_ps, 1)

                    def transpose_x(b):
                        pe.wait_ge(xb_ready, b + 1)
                        wait(pe, s_add, b * TPB - 1)
                        for c in range(C):
                            for t in range(TPB):
                                last = pe.transpose(ps[:, 2 + c, t * P:(t + 1) * P], xb[:, t, c * P:(c + 1) * P],
                                                    ident[:])
                        last.then_inc(hT_ps, 1)

                    def queries_keys(b):
                        pe.wait_ge(hT_act, b + 1)
                        pe.wait_ge(hT_dve, b + 1)
                        wait(pe, s_add, b * TPB)
                        for w, bank in ((wq, 4), (wk, 2)):
                            for m in range(C):
                                for c in range(C):
                                    last = pe.matmul(ps[:, bank + m, :], w[:, c, m * P:(m + 1) * P], hT[:, c, :],
                                                     start=(c == 0), stop=(c == C - 1))
                                last.then_inc(qk_ps, 1)

                    def values(b):
                        wait(pe, pT_sb, b * TPB)
                        for t in range(TPB):
                            for c in range(C):
                                last = pe.matmul(ps[:, 6 + t // 2, (t % 2) * D:(t % 2 + 1) * D],
                                                 hT[:, c, t * P:(t + 1) * P], wv[:, c, :],
                                                 start=(c == 0), stop=(c == C - 1))
                        last.then_inc(v_ps, 1)

                    def transpose_p(b, t):
                        n = b * TPB + t
                        pe.wait_ge(e_ready, n + 1)
                        if t == 0:
                            pe.wait_ge(v_sb, b * 4 + 4)
                        else:
                            pe.wait_ge(pT_sb, n)
                        for j in range(8):
                            last = pe.transpose(ps[:, 6 + j // 4, (j % 4) * P:(j % 4 + 1) * P],
                                                sc[:, t % 2, 2 * j:2 * j + 2, :].rearrange("p h k -> p (h k)"),
                                                ident[:])
                        last.then_inc(pT_ps, 1)

                    def outputs(b, t):
                        n = b * TPB + t
                        pe.wait_ge(pT_sb, n + 1)
                        wait(pe, at_sb, n)
                        for j in range(8):
                            last = pe.matmul(ps[:, 0, j * 64:(j + 1) * 64], pT[:, t % 2, j, :],
                                             vbd[:, t, j].rearrange("p s h d -> p (s h d)"),
                                             start=True, stop=True)
                        last.then_inc(o_ps, 1)

                    def transpose_o(b, t):
                        n = b * TPB + t
                        pe.wait_ge(at_sb, n + 1)
                        wait(pe, added, n)
                        for c in range(C):
                            last = pe.transpose(ps[:, 1, c * P:(c + 1) * P], at[:, c * P:(c + 1) * P], ident[:])
                        last.then_inc(aT_ps, 1)

                    def project(b, t):
                        pe.wait_ge(aT_sb, b * TPB + t + 1)
                        for c in range(C):
                            last = pe.matmul(ps[:, 1, D:2 * D], atT[:, c, :], wo[:, c, :],
                                             start=(c == 0), stop=(c == C - 1))
                        last.then_inc(yo_ps, 1)

                    pe.wait_ge(w_in, 64)
                    transpose_x(0)
                    queries_keys(0)
                    values(0)
                    scores(0, 0)
                    scores(0, 1)

                    def body(b, final):
                        for t in range(TPB):
                            transpose_p(b, t)
                            if t >= 2:
                                project(b, t - 2)
                            if t >= 1:
                                outputs(b, t - 1)
                            if t + 2 < TPB:
                                scores(b, t + 2)
                            elif t + 2 == TPB and not final:
                                transpose_x(b + 1)
                            elif not final:
                                queries_keys(b + 1)
                            if t >= 1:
                                transpose_o(b, t - 1)
                        project(b, TPB - 2)
                        outputs(b, TPB - 1)
                        if not final:
                            values(b + 1)
                        transpose_o(b, TPB - 1)
                        if not final:
                            scores(b + 1, 0)
                        project(b, TPB - 1)
                        if not final:
                            scores(b + 1, 1)
                    blocks(pe, body)

                @block.scalar
                def _(act):
                    def features_0(b):
                        act.wait_ge(hT_ps, b + 1)
                        act.copy(hT[:, 0, :], ps[:, 2, :]).then_inc(hT_act, 1)

                    def queries_keys(b):
                        for m in range(C):
                            act.wait_ge(qk_ps, b * 2 * C + m + 1)
                            act.activation(qT[:, m, :], ps[:, 4 + m, :], ACT.Copy, scale=DK1 ** -0.5).then_inc(qT_sb, 1)
                        for m in range(C):
                            act.wait_ge(qk_ps, b * 2 * C + C + m + 1)
                            act.copy(kT[:, m, :], ps[:, 2 + m, :]).then_inc(kT_sb, 1)

                    def exponential(b, t):
                        act.wait_ge(s_sh, b * TPB + t + 1)
                        act.activation(sc[:, t % 2], sc[:, t % 2], ACT.Exp).then_inc(e_ready, 1)

                    def transposed_p(b, t):
                        n = b * TPB + t
                        act.wait_ge(pT_ps, n + 1)
                        wait(act, o_ps, n - 1)
                        act.copy(pT[:, t % 2].rearrange("p j q -> p (j q)"), ps[:, 6:8, :].rearrange("p a b -> p (a b)")
                                 ).then_inc(pT_sb, 1)

                    def transposed_o(b, t):
                        n = b * TPB + t
                        act.wait_ge(aT_ps, n + 1)
                        wait(act, yo_ps, n)
                        act.copy(atT[:].rearrange("p c q -> p (c q)"), ps[:, 1, 0:C * P]).then_inc(aT_sb, 1)

                    def keep(b, t):
                        n = b * TPB + t
                        act.wait_ge(added, n + 1)
                        act.nop(nofuse=True)
                        act.copy(acc[:, bass.ds(n, 1), :].rearrange("p o d -> p (o d)"), xo[:, t % 2, :]).then_inc(kept, 1)

                    features_0(0)
                    queries_keys(0)
                    exponential(0, 0)

                    def body(b, final):
                        for t in range(TPB):
                            transposed_p(b, t)
                            if t >= 3:
                                keep(b, t - 3)
                            if t + 1 < TPB:
                                exponential(b, t + 1)
                            if t + 2 == TPB and not final:
                                features_0(b + 1)
                            if t + 1 == TPB and not final:
                                queries_keys(b + 1)
                            if t >= 1:
                                transposed_o(b, t - 1)
                        keep(b, TPB - 3)
                        transposed_o(b, TPB - 1)
                        keep(b, TPB - 2)
                        if not final:
                            exponential(b + 1, 0)
                        keep(b, TPB - 1)
                    blocks(act, body)

                @block.vector
                def _(dve):
                    dve.wait_ge(rel_in, 16)
                    for lo, hi, bucket in runs:
                        dve.tensor_copy(reld[:, lo:hi], rel[:, bucket:bucket + 1].to_broadcast([H1, hi - lo])
                                        ).then_inc(rel_sb, 1)
                    dve.wait_ge(v_zero, 1)
                    dve.wait_ge(bias_in, 32)
                    PER, AHEAD = TPB * 5, 3

                    def features_1(b):
                        dve.wait_ge(hT_ps, b + 1)
                        dve.tensor_copy(hT[:, 1, :], ps[:, 3, :]).then_inc(hT_dve, 1)

                    def values(b):
                        dve.wait_ge(v_ps, b + 1)
                        for s in range(2):
                            for h in range(2):
                                src = ps[s * S:(s + 1) * S, 6:8, :].rearrange("p a (t j h d) -> p (a t j) h d",
                                                                              t=2, j=8, h=2)[:, :, h, :]
                                dst = vbd[h * S:(h + 1) * S, :, :, s, h, :].rearrange("p t j d -> p (t j) d")
                                dve.tensor_copy(dst, src).then_inc(v_sb, 1)

                    def shift(b, t, st):
                        n = b * TPB + t
                        dve.wait_ge(s_ps, n + 1)
                        wait(dve, pT_ps, n - 1)
                        q = sc[:, t % 2]
                        dve.tensor_tensor(q.rearrange("p h k -> p (h k)"),
                                          ps[:, 2 + 2 * (t % 2):4 + 2 * (t % 2), :].rearrange("p a b -> p (a b)"),
                                          bias[:].rearrange("p h k -> p (h k)"), ALU.add).then_inc(s_add, 1)
                        dve.wait_ge(s_add, n + 1)
                        st.done(dve.tensor_reduce(mx[:, t % 2], q, AX.X, ALU.max))
                        dve.tensor_tensor(q, q, mx[:, t % 2].unsqueeze(2).to_broadcast([P, H1, S]), ALU.subtract
                                          ).then_inc(s_sh, 1)

                    def row_sums(b, t, st):
                        dve.wait_ge(e_ready, b * TPB + t + 1)
                        wait(dve, at_sb, b * TPB + t - 1)
                        st.done(dve.tensor_reduce(rs[:, t % 2], sc[:, t % 2], AX.X, ALU.add))
                        st.done(dve.reciprocal(rs[:, t % 2], rs[:, t % 2]))

                    def output(b, t):
                        n = b * TPB + t
                        dve.wait_ge(o_ps, n + 1)
                        wait(dve, aT_ps, n)
                        for s in range(2):
                            src = ps[s * S:(s + 1) * S, 0, :].rearrange(
                                "p (j s h d) -> p j s (h d)", j=8, s=2, h=2)[:, :, s, :]
                            src = src.rearrange("p j (h d) -> p j h d", h=2)
                            dst = at[s * S:(s + 1) * S, :].rearrange("p (j h d) -> p j h d", j=8, h=2)
                            sel = rs[s * S:(s + 1) * S, t % 2, :].rearrange("p (j h) -> p j h", h=2)
                            last = dve.tensor_tensor(dst, src, sel.unsqueeze(3).to_broadcast([S, 8, 2, DK1]),
                                                     ALU.mult)
                        last.then_inc(at_sb, 1)

                    def projected(b, t, st):
                        n = b * TPB + t
                        dve.wait_ge(yo_ps, n + 1)
                        wait(dve, kept, n - 1)
                        if t == 0:
                            dve.wait_ge(res_in, b * 16 + 16)
                        dve.tensor_tensor(xo[:, t % 2, :], ps[:, 1, D:2 * D], xres[:, t, :], ALU.add).then_inc(added, 1)
                        dve.wait_ge(added, n + 1)
                        st.done(dve.bn_stats(bst[:], xo[:, t % 2, :]))
                        dve.nop(nofuse=True)
                        st.done(dve.bn_aggr(mv[:], bst[:]))
                        dve.nop(nofuse=True)
                        dve.tensor_copy(mv1[:, bass.ds(n, 1), :].rearrange("p o d -> p (o d)"), mv[:]
                                        ).then_inc(tile_done, 1)

                    st = Steps(dve, dve_step)
                    features_1(0)
                    values(0)
                    shift(0, 0, st)
                    row_sums(0, 0, st)

                    def body(b, final):
                        st = Steps(dve, dve_step, b, PER, AHEAD)
                        for t in range(TPB):
                            if t + 1 < TPB:
                                shift(b, t + 1, st)
                            if t >= 1:
                                output(b, t - 1)
                            if t >= 2:
                                projected(b, t - 2, st)
                            if t + 1 < TPB:
                                row_sums(b, t + 1, st)
                            if t + 2 == TPB and not final:
                                features_1(b + 1)
                        projected(b, TPB - 2, st)
                        output(b, TPB - 1)
                        if not final:
                            values(b + 1)
                            shift(b + 1, 0, st)
                        projected(b, TPB - 1, st)
                        if not final:
                            row_sums(b + 1, 0, st)
                            st.close()
                    blocks(dve, body)

        def deviations(tag):
            ph = ExitStack()
            with ph:
                tmp = ph.enter_context(nc.sbuf_tensor(tag + "tmp", [P, NT], F32))
                added = ctx.enter_context(nc.semaphore(tag + "added"))
                rooted = ctx.enter_context(nc.semaphore(tag + "rooted"))
                block = ph.enter_context(nc.Block())

                @block.vector
                def _(dve):
                    dve.tensor_scalar(tmp[:], mv1[:, :, 1], EPS, None, ALU.add).then_inc(added, 1)
                    dve.wait_ge(rooted, 1)
                    dve.reciprocal(rstd[:], tmp[:])

                @block.scalar
                def _(act):
                    act.wait_ge(added, 1)
                    act.activation(tmp[:], tmp[:], ACT.Sqrt).then_inc(rooted, 1)

        def attention2():
            ph = ExitStack()
            with ph:
                def sb(name, shape, dt=F32):
                    return ph.enter_context(nc.sbuf_tensor("a2_" + name, shape, dt))

                def sem(name):
                    return ctx.enter_context(nc.semaphore("a2_" + name))

                wq = sb("wq", [P, C, H2 * DH2])
                wkv = sb("wkv", [P, C, 2 * DH2])
                wkk = sb("wkk", [P, C, 2, DH2])
                wo = sb("wo", [P, J2, D])
                gin = sb("gin", [P, C])
                bias = sb("bias", [P, 2, J2, KN])
                mask8 = sb("mask8", [P, NT, S], U8)
                madd = sb("madd", [P, NT, KN])
                bm = sb("bm", [P, 2, 2, J2, KN])
                xb = sb("xb", [P, TPB, D])
                xT_ = sb("xnT", [P, C, BT])
                q = sb("q", [P, J2, BT])
                k = sb("k", [P, SPB, KN])
                v = sb("v", [P, SPB, DH2])
                sc = sb("sc", [P, 2, 2, 4, KN])
                mx = sb("mx", [P, 2, 8])
                rs = sb("rs", [P, 2, 8])
                pT = sb("pT", [KN, 2, 2, 4, P])
                oT = sb("oT", [P, J2, P])
                bst = sb("bst", [P, 6])
                mv = sb("mv", [P, 2])
                pad = sb("pad", [P, ROW])
                pad_i = sb("pad_i", [P, 1], I32)
                pad_step, pad_ready, padded = sem("pad_step"), sem("pad_ready"), sem("padded")
                w_in, small_in, bias_in, mask_in, bias2_in = (
                    sem(n) for n in ("w_in", "small_in", "bias_in", "mask_in", "bias2_in"))
                causal, madd_ready, kk_ready, null_ready = (
                    sem(n) for n in ("causal", "madd_ready", "kk_ready", "null_ready"))
                xb_ready, xT_ps, xT_act, xT_dve, q_ps, q_act, q_dve = (
                    sem(n) for n in ("xb_ready", "xT_ps", "xT_act", "xT_dve", "q_ps", "q_act", "q_dve"))
                kv_ps, k_sb, v_sb, bm_ready, s_ps, s_sh, s_add, e_ready, r_ready, p_ready = (
                    sem(n) for n in ("kv_ps", "k_sb", "v_sb", "bm_ready", "s_ps", "s_sh", "s_add", "e_ready",
                                     "r_ready", "p_ready"))
                pT_ps, pT_sb, o_ps, oT_sb, yo_ps, tile_done, dve_step = (
                    sem(n) for n in ("pT_ps", "pT_sb", "o_ps", "oT_sb", "yo_ps", "tile_done", "dve_step"))
                HB = 2 * TPB
                block = ph.enter_context(nc.Block())

                @block.sync
                def _(sp):
                    sp.dma_start(wq[:], wq2.rearrange("(c p) n -> p c n", p=P)).then_inc(w_in, 16)
                    sp.dma_start(wkv[:], wkv2.rearrange("(c p) n -> p c n", p=P)).then_inc(w_in, 16)
                    sp.dma_start(wo[:], wo2.rearrange("(j p) n -> p j n", p=P)).then_inc(w_in, 16)
                    sp.dma_start(gin[:], g_in).then_inc(small_in, 16)
                    for h in range(2):
                        sp.dma_start(bias[0:S, h, :, 0:S],
                                     bias2.rearrange("(j h) q k -> h q j k", h=2)[h]).then_inc(bias_in, 16)
                    for s in range(2):
                        for h in range(2):
                            sp.dma_start(bias[s * S:(s + 1) * S, h, :, S:KN],
                                         nbias.rearrange("(j h) -> h j", h=2)[h:h + 1].unsqueeze(2)
                                         .to_broadcast([S, J2, 1])).then_inc(bias2_in, 16)
                    for s in range(2):
                        sp.dma_start(mask8[s * S:(s + 1) * S],
                                     mask.rearrange("(t s) k -> s t k", s=2)[s:s + 1]
                                     .to_broadcast([S, NT, S])).then_inc(mask_in, 16)
                    for h in range(2):
                        sp.dma_start(k[h * DH2:(h + 1) * DH2, :, S:KN],
                                     cond[0, :].rearrange("(d o) -> d o", o=1).unsqueeze(1)
                                     .to_broadcast([DH2, SPB, 1])).then_inc(null_ready, 16)
                    sp.dma_start(v[S:KN, :, :], cond[1:2, :].unsqueeze(1).to_broadcast([1, SPB, DH2])
                                 ).then_inc(null_ready, 16)
                    sp.wait_ge(pad_ready, 1)
                    for i in range(NBLK // 8):
                        sp.dma_start(x_slots[i * 8 * P:(i + 1) * 8 * P, :].rearrange("(b p) d -> p b d", p=P),
                                     pad[:].unsqueeze(1).to_broadcast([P, 8, ROW])).then_inc(padded, 16)
                    sp.wait_ge(padded, NBLK // 8 * 16)

                @block.gpsimd
                def _(pool):
                    pool.memset(pad[:], 0.0).then_inc(pad_step, 1)
                    pool.iota(pad_i[:], pattern=[[0, 1]], base=0, channel_multiplier=-1).then_inc(pad_step, 1)
                    pool.wait_ge(pad_step, 2)
                    pool.tensor_copy(pad[:, D:D + 1], pad_i[:]).then_inc(pad_ready, 1)
                    pool.wait_ge(bias_in, 32)
                    for h in range(2):
                        pool.affine_select(out=bias[0:S, h, :, 0:S], in_=bias[0:S, h, :, 0:S], compare_op=ALU.is_ge,
                                           fill=MASKED, base=0, pattern=[[0, J2], [-1, S]], channel_multiplier=1
                                           ).then_inc(causal, 1)
                    pool.wait_ge(causal, 3)
                    pool.wait_ge(bias2_in, 64)
                    pool.wait_ge(madd_ready, 1)

                    def bias_mask(n, w):
                        wait(pool, s_add, 2 * (n - 1))
                        pool.tensor_tensor(bm[:, w].rearrange("p h j k -> p (h j) k"),
                                           bias[:].rearrange("p h j k -> p (h j) k"),
                                           madd[:, bass.ds(n, 1), :].to_broadcast([P, H2, KN]),
                                           ALU.add).then_inc(bm_ready, 1)

                    def normalize(m, g):
                        pool.wait_ge(r_ready, m + 1)
                        p_ = sc[:, g].rearrange("p h j k -> p (h j) k")
                        pool.tensor_tensor(p_, p_, rs[:, g].unsqueeze(2).to_broadcast([P, 8, KN]),
                                           ALU.mult).then_inc(p_ready, 1)

                    def pair(i, final=False):
                        for w in range(2):
                            n = i * 2 + w
                            normalize(2 * n, 0)
                            if not (final and w == 1):
                                bias_mask(n + 1, 1 - w)
                            normalize(2 * n + 1, 1)

                    bias_mask(0, 0)
                    pair(0)
                    with pool.Fori(1, NT // 2 - 1) as i:
                        pair(i)
                    pair(NT // 2 - 1, final=True)

                @block.tensor
                def _(pe):
                    Q_BANK = (2, 3, 6, 7, 4, 5, 6, 7)

                    def scores(b, i):
                        m, t, g = b * HB + i, i // 2, i % 2
                        if i >= 2:
                            pe.wait_ge(s_add, m - 1)
                        else:
                            pe.wait_ge(q_act, b * 4 + 2 + 2 * i)
                            pe.wait_ge(q_dve, b * 4 + 2 + 2 * i)
                        pe.nop(nofuse=True)
                        for jj in range(4):
                            j = 4 * g + jj
                            for s in range(2):
                                for h in range(2):
                                    last = pe.matmul(
                                        ps[s * S:(s + 1) * S, 2 + 2 * g + h, jj * P:jj * P + KN],
                                        q[h * DH2:(h + 1) * DH2, j, t * P + s * S:t * P + (s + 1) * S],
                                        k[h * DH2:(h + 1) * DH2, 2 * t + s, :], start=True, stop=True)
                        last.then_inc(s_ps, 1)

                    def transpose_x(b):
                        pe.wait_ge(xb_ready, b + 1)
                        wait(pe, s_add, b * HB - 1)
                        for c in range(C):
                            for t in range(TPB):
                                last = pe.transpose(ps[:, 2 + c, t * P:(t + 1) * P], xb[:, t, c * P:(c + 1) * P],
                                                    ident[:])
                        last.then_inc(xT_ps, 1)

                    def keys_values(b):
                        pe.wait_ge(xT_act, b + 1)
                        pe.wait_ge(xT_dve, b + 1)
                        wait(pe, s_add, b * HB)
                        for c in range(C):
                            pe.matmul(ps[:, 4, :], wkk[:, c].rearrange("p a d -> p (a d)"), xT_[:, c, :],
                                      start=(c == 0), stop=(c == C - 1))
                        for t in range(TPB):
                            for c in range(C):
                                last = pe.matmul(ps[:, 5, t * DH2:(t + 1) * DH2], xT_[:, c, t * P:(t + 1) * P],
                                                 wkv[:, c, DH2:2 * DH2], start=(c == 0), stop=(c == C - 1))
                        last.then_inc(kv_ps, 1)

                    def queries(b):
                        for j in range(J2):
                            if j == 2:
                                wait(pe, pT_sb, b * HB)
                            elif j == 4:
                                pe.wait_ge(k_sb, b + 1)
                            elif j == 5:
                                pe.wait_ge(v_sb, b * 2 + 2)
                            elif j >= 6:
                                pe.wait_ge(q_act if j % 2 == 0 else q_dve, b * 4 + 2)
                            for c in range(C):
                                last = pe.matmul(ps[:, Q_BANK[j], :], wq[:, c, j * P:(j + 1) * P], xT_[:, c, :],
                                                 start=(c == 0), stop=(c == C - 1))
                            last.then_inc(q_ps, 1)

                    def transpose_p(b, i):
                        m, g = b * HB + i, i % 2
                        pe.wait_ge(p_ready, m + 1)
                        wait(pe, pT_sb, m)
                        for h in range(2):
                            for jj in range(4):
                                last = pe.transpose(ps[0:KN, 6 + h, jj * P:(jj + 1) * P], sc[:, g, h, jj, :], ident[:])
                        last.then_inc(pT_ps, 1)

                    def outputs(b, i):
                        m, t = b * HB + i, i // 2
                        pe.wait_ge(pT_sb, m + 1)
                        wait(pe, oT_sb, m)
                        for s in range(2):
                            for h in range(2):
                                last = pe.matmul(
                                    ps[h * DH2:(h + 1) * DH2, 0, :].rearrange(
                                        "p (j s q) -> p j s q", j=4, s=2)[:, :, s, :],
                                    v[0:KN, 2 * t + s, :], pT[:, i % 2, h, :, s * S:(s + 1) * S],
                                    start=True, stop=True)
                        last.then_inc(o_ps, 1)

                    def project(b, t):
                        n = b * TPB + t
                        pe.wait_ge(oT_sb, 2 * n + 2)
                        wait(pe, tile_done, n)
                        for j in range(J2):
                            last = pe.matmul(ps[:, 1, 0:D], oT[:, j, :], wo[:, j, :],
                                             start=(j == 0), stop=(j == J2 - 1))
                        last.then_inc(yo_ps, 1)

                    pe.wait_ge(w_in, 48)
                    pe.wait_ge(kk_ready, 1)
                    pe.wait_ge(null_ready, 48)
                    transpose_x(0)
                    keys_values(0)
                    queries(0)
                    scores(0, 0)
                    scores(0, 1)

                    def body(b, final):
                        for i in range(HB):
                            transpose_p(b, i)
                            if i > 0:
                                outputs(b, i - 1)
                            if i + 2 < HB:
                                scores(b, i + 2)
                            elif i + 2 == HB and not final:
                                transpose_x(b + 1)
                            elif not final:
                                keys_values(b + 1)
                            if i % 2 == 0 and i > 0:
                                project(b, i // 2 - 1)
                        outputs(b, HB - 1)
                        if not final:
                            queries(b + 1)
                            scores(b + 1, 0)
                        project(b, TPB - 1)
                        if not final:
                            scores(b + 1, 1)
                    blocks(pe, body)

                @block.scalar
                def _(act):
                    act.wait_ge(causal, 2)
                    act.copy(bias[S:P, :, :, 0:S].rearrange("p h j k -> p (h j) k"),
                             bias[0:S, :, :, 0:S].rearrange("p h j k -> p (h j) k")).then_inc(causal, 1)
                    act.wait_ge(w_in, 48)
                    for h in range(2):
                        last = act.copy(wkk[:, :, h, :], wkv[:, :, 0:DH2])
                    last.then_inc(kk_ready, 1)
                    act.wait_ge(small_in, 16)

                    def features_0(b):
                        act.wait_ge(xT_ps, b + 1)
                        act.activation(xT_[:, 0, :], ps[:, 2, :], ACT.Copy, scale=gin[:, 0:1]).then_inc(xT_act, 1)

                    def keys_and_queries(b):
                        act.wait_ge(kv_ps, b + 1)
                        act.copy(k[:, :, 0:S], ps[:, 4, :].rearrange("p (s k) -> p s k", s=SPB)).then_inc(k_sb, 1)
                        for j in range(0, J2, 2):
                            act.wait_ge(q_ps, b * J2 + j + 1)
                            act.activation(q[:, j, :], ps[:, (2, 6, 4, 6)[j // 2], :], ACT.Copy, scale=DH2 ** -0.5
                                           ).then_inc(q_act, 1)

                    def exponential(b, i):
                        act.wait_ge(s_sh, b * HB + i + 1)
                        act.activation(sc[:, i % 2], sc[:, i % 2], ACT.Exp).then_inc(e_ready, 1)

                    def transposed(b, i):
                        m = b * HB + i
                        act.wait_ge(pT_ps, m + 1)
                        wait(act, o_ps, m - 1)
                        act.copy(pT[:, i % 2].rearrange("p h j q -> p (h j q)"),
                                 ps[0:KN, 6:8, :].rearrange("p a b -> p (a b)")).then_inc(pT_sb, 1)

                    features_0(0)
                    keys_and_queries(0)
                    exponential(0, 0)

                    def body(b, final):
                        for i in range(HB):
                            transposed(b, i)
                            if i + 1 < HB:
                                exponential(b, i + 1)
                            if i + 2 == HB and not final:
                                features_0(b + 1)
                        if not final:
                            keys_and_queries(b + 1)
                            exponential(b + 1, 0)
                    blocks(act, body)

                @block.vector
                def _(dve):
                    dve.wait_ge(mask_in, 32)
                    dve.memset(madd[:, :, S:KN], 0.0)
                    dve.tensor_scalar(madd[:, :, 0:S], mask8[:], 1.0, -MASKED, ALU.subtract, ALU.mult
                                      ).then_inc(madd_ready, 1)
                    dve.wait_ge(small_in, 16)
                    PER, AHEAD = TPB * 6, 2

                    def normalized(b):
                        wait(dve, xT_ps, b)
                        for t in range(TPB):
                            n = b * TPB + t
                            last = dve.tensor_scalar(xb[:, t, :], acc[:, bass.ds(n, 1), :].rearrange("p o d -> p (o d)"),
                                                     mv1[:, bass.ds(n, 1), 0], rstd[:, bass.ds(n, 1)],
                                                     ALU.subtract, ALU.mult)
                        last.then_inc(xb_ready, 1)

                    def features_1(b):
                        dve.wait_ge(xT_ps, b + 1)
                        dve.tensor_scalar(xT_[:, 1, :], ps[:, 3, :], gin[:, 1:2], None, ALU.mult).then_inc(xT_dve, 1)

                    def values_and_queries(b):
                        dve.wait_ge(kv_ps, b + 1)
                        for s in range(2):
                            dve.tensor_copy(v[0:S, :, :].rearrange("p (t s) d -> p t s d", s=2)[:, :, s, :],
                                            ps[s * S:(s + 1) * S, 5, 0:TPB * DH2].rearrange("p (t d) -> p t d", t=TPB)
                                            ).then_inc(v_sb, 1)
                        for j in range(1, J2, 2):
                            dve.wait_ge(q_ps, b * J2 + j + 1)
                            dve.tensor_scalar(q[:, j, :], ps[:, (3, 7, 5, 7)[j // 2], :], DH2 ** -0.5, None, ALU.mult
                                              ).then_inc(q_dve, 1)

                    def shift(b, i, st):
                        m, n, g = b * HB + i, b * TPB + i // 2, i % 2
                        dve.wait_ge(s_ps, m + 1)
                        dve.wait_ge(bm_ready, n + 1)
                        wait(dve, pT_ps, m - 1)
                        dve.tensor_tensor(sc[:, g], ps[:, 2 + 2 * g:4 + 2 * g, :].rearrange(
                            "p h (j k) -> p h j k", j=4)[:, :, :, 0:KN], bm[:, i // 2 % 2, :, 4 * g:4 * g + 4, :],
                            ALU.add).then_inc(s_add, 1)
                        dve.wait_ge(s_add, m + 1)
                        s_ = sc[:, g].rearrange("p h j k -> p (h j) k")
                        st.done(dve.tensor_reduce(mx[:, g], s_, AX.X, ALU.max))
                        dve.tensor_tensor(s_, s_, mx[:, g].unsqueeze(2).to_broadcast([P, 8, KN]), ALU.subtract
                                          ).then_inc(s_sh, 1)

                    def row_sums(b, i, st):
                        g = i % 2
                        dve.wait_ge(e_ready, b * HB + i + 1)
                        st.done(dve.tensor_reduce(rs[:, g], sc[:, g].rearrange("p h j k -> p (h j) k"), AX.X, ALU.add))
                        dve.reciprocal(rs[:, g], rs[:, g]).then_inc(r_ready, 1)

                    def output(b, i):
                        g = i % 2
                        dve.wait_ge(o_ps, b * HB + i + 1)
                        wait(dve, yo_ps, b * TPB + i // 2)
                        dve.tensor_copy(oT[:, 4 * g:4 * g + 4, :].rearrange("p j q -> p (j q)"), ps[:, 0, :]
                                        ).then_inc(oT_sb, 1)

                    def projected(b, t, st):
                        n = b * TPB + t
                        dve.wait_ge(yo_ps, n + 1)
                        dve.tensor_copy(att[:, bass.ds(n, 1), :].rearrange("p o d -> p (o d)"), ps[:, 1, 0:D])
                        st.done(dve.bn_stats(bst[:], ps[:, 1, 0:D]))
                        dve.nop(nofuse=True)
                        st.done(dve.bn_aggr(mv[:], bst[:]))
                        dve.nop(nofuse=True)
                        dve.tensor_copy(mv1[:, bass.ds(n, 1), :].rearrange("p o d -> p (o d)"), mv[:]
                                        ).then_inc(tile_done, 1)

                    st = Steps(dve, dve_step)
                    normalized(0)
                    features_1(0)
                    values_and_queries(0)
                    shift(0, 0, st)
                    row_sums(0, 0, st)

                    def body(b, final):
                        st = Steps(dve, dve_step, b, PER, AHEAD)
                        for i in range(HB):
                            if i + 1 < HB:
                                shift(b, i + 1, st)
                            if i % 2 == 1 and i >= 3:
                                projected(b, (i - 3) // 2, st)
                            if i + 1 < HB:
                                row_sums(b, i + 1, st)
                            if i > 0:
                                output(b, i - 1)
                            if i + 3 == HB and not final:
                                normalized(b + 1)
                            if i + 2 == HB and not final:
                                features_1(b + 1)
                        output(b, HB - 1)
                        if not final:
                            values_and_queries(b + 1)
                            shift(b + 1, 0, st)
                        projected(b, TPB - 1, st)
                        if not final:
                            row_sums(b + 1, 0, st)
                            st.close()
                    blocks(dve, body)

        def route():
            ph = ExitStack()
            with ph:
                def sb(name, shape, dt=F32):
                    return ph.enter_context(nc.sbuf_tensor("rt_" + name, shape, dt))

                def sem(name):
                    return ctx.enter_context(nc.semaphore("rt_" + name))

                goutb = sb("goutb", [P, D])
                rw = sb("rw", [P, C, P])
                cb = sb("cb", [P, E2])
                before = sb("before", [P, P])
                ones = sb("ones", [P, P])
                ids_i = sb("ids_i", [P, NT, K2], I32)
                ids = sb("ids", [P, NT, K2])
                w_su = sb("w_su", [P, SH2, C, M2])
                w_sd = sb("w_sd", [P, SH2, D])
                at_h, at_z = 2 * K2 * ROW, 2 * K2 * ROW + SH2 * BT
                z = wide[:, at_z:at_z + TPB * D].rearrange("p (t d) -> p t d", t=TPB)
                zT = sb("zT", [P, C, BT])
                r = sb("r", [P, 2, BT])
                h = wide[:, at_h:at_z].rearrange("p (i n) -> p i n", i=SH2)
                lT = sb("lT", [P, BT])
                GR = TPB * GROUPS
                score = sb("score", [P, TPB, E2])
                sfc = sb("sfc", [P, TPB, E2])
                left = sb("left", [P, TPB, E2])
                sel = sb("sel", [P, TPB, E2])
                hi, lo = sb("hi", [P, GR, 4]), sb("lo", [P, GR, 4])
                hi2, lo2, t2 = (sb(n, [P, GR, 2]) for n in ("hi2", "lo2", "t2"))
                gs, gl = sb("gs", [P, TPB, GROUPS]), sb("gl", [P, TPB, GROUPS])
                top8 = sb("top8", [P, TPB, 8])
                stat = sb("stat", [P, TPB])
                free = sb("free", [P, E2])
                nxt = sb("nxt", [P, E2])
                used = sb("used", [P, 1])
                late = sb("late", [P, TPB, E2])
                jump = sb("jump", [P, E2])
                grew = sb("grew", [P, E2])
                first = sb("first", [P, E2])
                fresh = sb("fresh", [P, 3])
                now = sb("now", [P, 3])
                sv = sb("sv", [P, TPB, E2])
                top8s = sb("top8s", [P, TPB, K2])
                sidx = sb("sidx", [P, 2, K2], I32)
                junk = sb("junk", [P, K2, E2])
                stage = wide[:, 0:2 * K2 * ROW].rearrange("p (w k r) -> p w k r", w=2, k=K2)
                blk_i = sb("blk_i", [P, 3], I32)
                blk = sb("blk", [P, 3])
                nb_i = sb("nb_i", [P, E2], I32)
                nb = sb("nb", [P, E2])
                end = sb("end", [P, E2])
                ones64 = sb("ones64", [P, E2])
                le = sb("le", [P, 3, E2])
                be = sb("be", [P, 3])
                be_i = sb("be_i", [P, 3], I32)
                small_in, padded, made, mul_ready, z_ready, zT_ps, zT_act, zT_dve = (
                    sem(n) for n in ("small_in", "padded", "made", "mul_ready", "z_ready", "zT_ps", "zT_act", "zT_dve"))
                lT_ps, lT_sb, l_ps, e_ready, sel_ready, rank_ps, rank_read, init = (
                    sem(n) for n in ("lT_ps", "lT_sb", "l_ps", "e_ready", "sel_ready", "rank_ps", "rank_read", "init"))
                sz_ps, r_ready, h_ready, sy_ps, sy_done, z_staged, w_staged, tables, tables_out, dve_step = (
                    sem(n) for n in ("sz_ps", "r_ready", "h_ready", "sy_ps", "sy_done", "z_staged", "w_staged",
                                     "tables", "tables_out", "dve_step"))
                sent = [sem("sent0"), sem("sent1")]
                block = ph.enter_context(nc.Block())
                FILLS = 5

                @block.sync
                def _(sp):
                    sp.dma_start(goutb[:], g_row.to_broadcast([P, D])).then_inc(small_in, 16)
                    sp.dma_start(cb[:], cbias.rearrange("(o e) -> o e", o=1).to_broadcast([P, E2])).then_inc(small_in, 16)
                    sp.dma_start(w_su[:], up2s).then_inc(small_in, 16)
                    sp.dma_start(w_sd[:], down2s).then_inc(small_in, 16)
                    sp.wait_ge(padded, 1)
                    sp.dma_start(rw[:, :, 0:E2], rwT.rearrange("(c p) e -> p c e", p=P)).then_inc(small_in, 16)
                    sp.dma_start(w_up[:], up2).then_inc(w_res, 16)
                    sp.wait_ge(tables, 1)
                    sp.dma_start(block_expert.rearrange("(c p) -> p c", p=P).unsqueeze(2), be_i[:].unsqueeze(2)
                                 ).then_inc(tables_out, 16)
                    sp.wait_ge(tables_out, 16)

                @block.gpsimd
                def _(pool):
                    pool.memset(rw[:], 0.0).then_inc(padded, 1)
                    pool.memset(before[:], 1.0).then_inc(made, 1)
                    pool.wait_ge(made, 1)
                    pool.affine_select(out=before[:], in_=before[:], compare_op=ALU.is_gt, fill=0.0, base=0,
                                       pattern=[[1, P]], channel_multiplier=-1).then_inc(made, 1)
                    pool.memset(ones[:], 1.0).then_inc(made, 1)
                    pool.iota(ids_i[:], pattern=[[-P * K2, NT], [-1, K2]], base=T * K2, channel_multiplier=-K2
                              ).then_inc(made, 1)
                    pool.iota(blk_i[:], pattern=[[P, 3]], base=0, channel_multiplier=1).then_inc(made, 1)
                    pool.wait_ge(small_in, FILLS * 16)

                    def body(b):
                        pool.wait_ge(mul_ready, b + 1)
                        pool.tensor_tensor(z, z, goutb[:].unsqueeze(1).to_broadcast([P, TPB, D]), ALU.mult
                                           ).then_inc(z_ready, 1)
                        for t in range(TPB):
                            n = b * TPB + t
                            pool.wait_ge(z_staged, n + 1)
                            pool.wait_ge(w_staged, n + 1)
                            pool.nop(nofuse=True)
                            for k in range(K2):
                                pool.indirect_dma_start(
                                    out=x_slots, out_offset=bass.IndirectOffsetOnAxis(ap=sidx[:, t % 2, k:k + 1], axis=0),
                                    in_=stage[:, t % 2, k, :], in_offset=None).then_inc(sent[t % 2], 16)
                    turns(pool, NB, body)
                    for w in range(2):
                        pool.wait_ge(sent[w], NT // 2 * 16 * K2)

                @block.tensor
                def _(pe):
                    pe.wait_ge(small_in, FILLS * 16)
                    pe.wait_ge(made, 5)

                    def body(b):
                        pe.wait_ge(z_ready, b + 1)
                        wait(pe, sy_done, b * 2)
                        for c in range(C):
                            for t in range(TPB):
                                last = pe.transpose(ps[:, c, t * P:(t + 1) * P], z[:, t, c * P:(c + 1) * P], ident[:])
                        last.then_inc(zT_ps, 1)
                        pe.wait_ge(zT_act, b + 1)
                        pe.wait_ge(zT_dve, b + 1)
                        for c in range(C):
                            last = pe.matmul(ps[:, 2, :], rw[:, c, :], zT[:, c, :], start=(c == 0), stop=(c == C - 1))
                        last.then_inc(lT_ps, 1)
                        for i in range(SH2):
                            if i == 1:
                                pe.wait_ge(lT_sb, b + 1)
                                wait(pe, e_ready, b)
                                for t in range(TPB):
                                    last = pe.transpose(ps[:, 3, t * P:(t + 1) * P], lT[:, t * P:(t + 1) * P], ident[:])
                                last.then_inc(l_ps, 1)
                            wait(pe, h_ready, b * SH2 + i - 1)
                            for c in range(C):
                                last = pe.matmul(ps[:, 5 + i % 2, :], w_su[:, i, c, :], zT[:, c, :],
                                                 start=(c == 0), stop=(c == C - 1))
                            last.then_inc(sz_ps, 1)
                        pe.wait_ge(h_ready, b * SH2 + SH2)
                        for t in range(TPB):
                            for i in range(SH2):
                                last = pe.matmul(ps[:, t // 2, (t % 2) * D:(t % 2 + 1) * D],
                                                 h[:, i, t * P:(t + 1) * P], w_sd[:, i, :],
                                                 start=(i == 0), stop=(i == SH2 - 1))
                        last.then_inc(sy_ps, 1)
                        pe.wait_ge(sel_ready, b + 1)
                        wait(pe, rank_read, b)
                        for t in range(TPB + 1):
                            for i in range(min(t + 1, TPB)):
                                last = pe.matmul(ps[:, 4, t * E2:(t + 1) * E2], before[:] if i == t else ones[:],
                                                 sel[:, i, :], start=(i == 0), stop=(i == min(t, TPB - 1)))
                        last.then_inc(rank_ps, 1)
                    turns(pe, NB, body)

                @block.scalar
                def _(act):
                    def body(b):
                        act.wait_ge(zT_ps, b + 1)
                        wait(act, sz_ps, b * SH2)
                        act.copy(zT[:, 0, :], ps[:, 0, :]).then_inc(zT_act, 1)
                        act.wait_ge(lT_ps, b + 1)
                        wait(act, l_ps, b)
                        act.copy(lT[:], ps[:, 2, :]).then_inc(lT_sb, 1)
                        act.wait_ge(l_ps, b + 1)
                        wait(act, w_staged, b * TPB)
                        act.activation(score[:], ps[:, 3, :].rearrange("p (t e) -> p t e", t=TPB)[:, :, 0:E2], ACT.Exp,
                                       scale=-1.0).then_inc(e_ready, 1)
                        for i in range(SH2):
                            n = b * SH2 + i
                            act.wait_ge(sz_ps, n + 1)
                            if i == 0:
                                wait(act, sy_ps, b)
                            act.activation(r[:, i % 2, :], ps[:, 5 + i % 2, :], ACT.Relu).then_inc(r_ready, 1)
                            act.wait_ge(r_ready, n + 1)
                            act.activation(h[:, i, :], r[:, i % 2, :], ACT.Square).then_inc(h_ready, 1)
                        for t in range(TPB):
                            wait(act, sent[t % 2], (b * 2 + t // 2) * 16 * K2)
                            act.copy(stage[:, t % 2, :, 0:D], z[:, t, :].unsqueeze(1).to_broadcast([P, K2, D])
                                     ).then_inc(z_staged, 1)
                    turns(act, NB, body)

                @block.vector
                def _(dve):
                    dve.wait_ge(made, 5)
                    dve.wait_ge(small_in, FILLS * 16)
                    for zero in (free, used, be):
                        dve.memset(zero[:], 0.0)
                    dve.memset(nxt[:], 1.0)
                    dve.memset(ones64[:], 1.0)
                    dve.tensor_copy(blk[:], blk_i[:])
                    dve.tensor_copy(ids[:], ids_i[:]).then_inc(init, 1)
                    dve.wait_ge(init, 1)
                    PER = 47

                    def body(b):
                        st = Steps(dve, dve_step, b, PER)
                        wait(dve, z_staged, b * TPB)
                        for t in range(TPB):
                            n = b * TPB + t
                            last = dve.tensor_scalar(z[:, t, :], att[:, bass.ds(n, 1), :].rearrange("p o d -> p (o d)"),
                                                     mv1[:, bass.ds(n, 1), 0], rstd[:, bass.ds(n, 1)],
                                                     ALU.subtract, ALU.mult)
                        last.then_inc(mul_ready, 1)
                        dve.wait_ge(zT_ps, b + 1)
                        dve.tensor_copy(zT[:, 1, :], ps[:, 1, :]).then_inc(zT_dve, 1)
                        dve.wait_ge(e_ready, b + 1)
                        st.done(dve.tensor_scalar(score[:], score[:], 1.0, None, ALU.add))
                        st.done(dve.reciprocal(score[:], score[:]))
                        st.done(dve.tensor_tensor(sfc[:], score[:], cb[:].unsqueeze(1).to_broadcast([P, TPB, E2]), ALU.add))
                        grp = sfc[:].rearrange("p t (g e) -> p (t g) e", g=GROUPS)
                        dve.tensor_tensor(hi[:], grp[:, :, 0:4], grp[:, :, 4:8], ALU.max)
                        st.done(dve.tensor_tensor(lo[:], grp[:, :, 0:4], grp[:, :, 4:8], ALU.min))

                        def merge(h_, l_, h_out, l_out, tmp, n):
                            dve.tensor_tensor(h_out, h_[:, :, 0:n], h_[:, :, n:2 * n], ALU.max)
                            dve.tensor_tensor(tmp, h_[:, :, 0:n], h_[:, :, n:2 * n], ALU.min)
                            st.done(dve.tensor_tensor(l_out, l_[:, :, 0:n], l_[:, :, n:2 * n], ALU.max))
                            st.done(dve.tensor_tensor(l_out, l_out, tmp, ALU.max))
                        merge(hi[:], lo[:], hi2[:], lo2[:], t2[:], 2)
                        merge(hi2[:], lo2[:], hi[:, :, 0:1], lo[:, :, 0:1], t2[:, :, 0:1], 1)
                        st.done(dve.tensor_tensor(gs[:].rearrange("p t (g o) -> p (t g) o", o=1), hi[:, :, 0:1],
                                                  lo[:, :, 0:1], ALU.add))
                        dve.nop(nofuse=True)
                        for t in range(TPB):
                            last = dve.max(top8[:, t, :], gs[:, t, :])
                        st.done(last)
                        st.done(dve.memset(top8[:, :, TOPG:8], UNMATCHED))
                        dve.nop(nofuse=True)
                        for t in range(TPB):
                            last = dve.match_replace(gl[:, t, :], top8[:, t, :], gs[:, t, :], TAKEN)
                        st.done(last)
                        st.done(dve.tensor_scalar(gl[:], gl[:], TAKEN, None, ALU.is_equal))
                        st.done(dve.tensor_tensor(grp, grp, gl[:].rearrange("p t g -> p (t g)").unsqueeze(2)
                                                  .to_broadcast([P, GR, 8]), ALU.mult))
                        dve.nop(nofuse=True)
                        for t in range(TPB):
                            last = dve.max(top8[:, t, :], sfc[:, t, :])
                        st.done(last)
                        dve.nop(nofuse=True)
                        for t in range(TPB):
                            last = dve.match_replace(left[:, t, :], top8[:, t, :], sfc[:, t, :], TAKEN)
                        st.done(last)
                        dve.tensor_scalar(sel[:], left[:], TAKEN, None, ALU.is_equal).then_inc(sel_ready, 1)
                        dve.wait_ge(sel_ready, b + 1)
                        st.done(dve.tensor_tensor(score[:], score[:], sel[:], ALU.mult))
                        st.done(dve.tensor_reduce(stat[:], score[:], AX.X, ALU.add))
                        st.done(dve.tensor_scalar(stat[:], stat[:], 1e-20, None, ALU.add))
                        st.done(dve.reciprocal(stat[:], stat[:]))
                        st.done(dve.tensor_scalar(stat[:], stat[:], ROUTE_SCALE, None, ALU.mult))
                        st.done(dve.tensor_tensor(score[:], score[:], stat[:].unsqueeze(2).to_broadcast([P, TPB, E2]),
                                                  ALU.mult))
                        dve.wait_ge(sy_ps, b + 1)
                        for i in range(2):
                            a_ = acc[:, bass.ds(b * TPB + 2 * i, 2), :].rearrange("p t d -> p (t d)")
                            dve.tensor_tensor(a_, ps[:, i, :], a_, ALU.add).then_inc(sy_done, 1)
                        dve.wait_ge(rank_ps, b + 1)
                        rank = ps[:, 4, 0:TPB * E2].rearrange("p (t e) -> p t e", e=E2)
                        tot = ps[:, 4, TPB * E2:(TPB + 1) * E2]

                        def over(ap, shape):
                            return ap.unsqueeze(1).to_broadcast(shape)
                        st.done(dve.tensor_tensor(grew[:], tot, free[:], ALU.subtract))
                        st.done(dve.tensor_scalar(nb_i[:], grew[:], float(P - 1), 0.0, ALU.add, ALU.max))
                        st.done(dve.tensor_scalar(nb_i[:], nb_i[:], 7, None, ALU.logical_shift_right))
                        st.done(dve.tensor_copy(nb[:], nb_i[:]))
                        st.done(dve.tensor_tensor_scan(end[:], ones64[:], nb[:], used[:], ALU.mult, ALU.add))
                        st.done(dve.tensor_tensor(first[:], end[:], nb[:], ALU.subtract))
                        dve.tensor_tensor(jump[:], free[:], nxt[:], ALU.add)
                        st.done(dve.tensor_scalar(first[:], first[:], float(P), 1.0, ALU.mult, ALU.add))
                        st.done(dve.tensor_tensor(jump[:], first[:], jump[:], ALU.subtract))
                        st.done(dve.tensor_tensor(late[:], rank, over(free[:], [P, TPB, E2]), ALU.is_ge))
                        dve.tensor_tensor(sv[:], rank, over(nxt[:], [P, TPB, E2]), ALU.add)
                        st.done(dve.tensor_tensor(late[:], late[:], over(jump[:], [P, TPB, E2]), ALU.mult))
                        st.done(dve.tensor_tensor(sv[:], sv[:], late[:], ALU.add))
                        dve.tensor_tensor(le[:], over(end[:], [P, 3, E2]), blk[:].unsqueeze(2).to_broadcast([P, 3, E2]),
                                          ALU.is_le)
                        st.done(dve.tensor_tensor(fresh[:], blk[:], used[:].to_broadcast([P, 3]), ALU.is_ge))
                        st.done(dve.tensor_reduce(now[:], le[:], AX.X, ALU.add))
                        st.done(dve.scalar_tensor_tensor(now[:], now[:], float(E2 - 1), fresh[:], ALU.min, ALU.mult))
                        dve.tensor_tensor(sv[:], sv[:], sel[:], ALU.mult)
                        st.done(dve.tensor_tensor(fresh[:], blk[:], end[:, E2 - 1:E2].to_broadcast([P, 3]), ALU.is_lt))
                        st.done(dve.tensor_tensor(now[:], now[:], fresh[:], ALU.mult))
                        dve.tensor_tensor(be[:], be[:], now[:], ALU.add)
                        st.done(dve.tensor_scalar(grew[:], nb[:], 1.0, None, ALU.min))
                        st.done(dve.tensor_tensor(jump[:], jump[:], grew[:], ALU.mult))
                        dve.scalar_tensor_tensor(free[:], nb[:], float(P), free[:], ALU.mult, ALU.add)
                        st.done(dve.tensor_tensor(nxt[:], nxt[:], jump[:], ALU.add))
                        dve.tensor_copy(used[:], end[:, E2 - 1:E2])
                        dve.tensor_tensor(nxt[:], tot, nxt[:], ALU.add)
                        st.done(dve.tensor_tensor(free[:], free[:], tot, ALU.subtract))
                        dve.sem_inc(rank_read, 1)
                        dve.nop(nofuse=True)
                        for t in range(TPB):
                            last = dve.max(top8s[:, t, :], sv[:, t, :])
                        st.done(last)
                        for t in range(TPB):
                            w = t % 2
                            wait(dve, sent[w], (b * 2 + t // 2) * 16 * K2)
                            st.done(dve.tensor_scalar(sidx[:, w, :], top8s[:, t, :], 1.0, None, ALU.subtract))
                            dve.tensor_copy(stage[:, w, :, D:D + 1].rearrange("p k o -> p (k o)"),
                                            ids[:, bass.ds(b * TPB + t, 1), :].rearrange("p o k -> p (o k)"))
                            for k in range(K2):
                                last = dve.scalar_tensor_tensor(junk[:, k], sv[:, t, :], top8s[:, t, k:k + 1],
                                                                score[:, t, :], ALU.is_equal, ALU.mult,
                                                                accum_out=stage[:, w, k, D + 1:D + 2])
                            last.then_inc(w_staged, 1)
                            dve.wait_ge(w_staged, b * TPB + t + 1)
                        st.close()
                    turns(dve, NB, body)

                    dve.tensor_copy(be_i[:], be[:]).then_inc(tables, 1)

        def slot_experts():
            ph = ExitStack()
            with ph:
                def sb(name, shape, dt=F32):
                    return ph.enter_context(nc.sbuf_tensor("se_" + name, shape, dt))

                def sem(name):
                    return ctx.enter_context(nc.semaphore("se_" + name))

                XR = 4
                be_row = sb("be_row", [1, 3 * P], I32)
                xs = sb("xs", [P, XR, GB, ROW])
                xsT = sb("xsT", [P, 2, GB, C, P])
                r = sb("r", [P, GB, P])
                h = sb("h", [P, 2, GB, P])
                hT = sb("hT", [P, 2, GB, P])
                ys = sb("ys", [P, 2, GB, D])
                yidx = sb("yidx", [P, 2, GB], I32)
                tail = sb("tail", [P, XR, GB, 2])
                be_in = sem("be_in")
                wd_in = sem("wd_in")
                x_in = [sem(f"x_in{i}") for i in range(XR)]
                y_out = [sem("y_out0"), sem("y_out1")]
                t_ps, t_act, t_dve, z_ps, r_ready, h_ready, hT_ps, hT_sb, y_ps, y_act, y_dve = (
                    sem(n) for n in ("t_ps", "t_act", "t_dve", "z_ps", "r_ready", "h_ready", "hT_ps", "hT_sb",
                                     "y_ps", "y_act", "y_dve"))
                block = ph.enter_context(nc.Block())
                LAG = 3

                def pipeline(eng, turn):
                    for n in range(2 * XR):
                        turn(n, n % XR, n // XR, lambda lag, n=n: 0 <= n - lag < NG)
                    with eng.Fori(2, NG // XR) as q:
                        for w in range(XR):
                            turn(q * XR + w, w, q, lambda lag: True)
                    for w in range(LAG):
                        turn(NG + w, w, NG // XR, lambda lag, w=w: 0 <= NG + w - lag < NG)

                def half(q, w, lag):
                    return q * 2 + (w - lag) // 2

                @block.sync
                def _(sp):
                    sp.dma_start(be_row[:], block_expert.rearrange("(o n) -> o n", o=1)).then_inc(be_in, 16)
                    xv = x_slots.rearrange("(g b p) d -> g p b d", p=P, b=GB)

                    def turn(n, w, q, live):
                        if live(0):
                            wait(sp, t_dve, n - XR + 1)
                            sp.dma_start(xs[:, w], xv[bass.ds(n, 1)].rearrange("o p b d -> p (o b) d")
                                         ).then_inc(x_in[w], 16)
                            if isinstance(n, int) and n == 0:
                                sp.dma_start(w_dn, down2).then_inc(wd_in, 16)
                    pipeline(sp, turn)

                @block.gpsimd
                def _(pool):
                    def turn(n, w, q, live):
                        if live(3):
                            g = n - 3
                            pool.wait_ge(y_act, g + 1)
                            pool.wait_ge(y_dve, g + 1)
                            pool.nop(nofuse=True)
                            for b in range(GB):
                                pool.indirect_dma_start(
                                    out=y_rows, out_offset=bass.IndirectOffsetOnAxis(ap=yidx[:, (w - 3) % 2, b:b + 1],
                                                                                     axis=0),
                                    in_=ys[:, (w - 3) % 2, b, :], in_offset=None,
                                    bounds_check=T * K2 - 1, oob_is_err=False).then_inc(y_out[(w - 3) % 2], 16)
                    pipeline(pool, turn)
                    for w in range(2):
                        pool.wait_ge(y_out[w], NG // 2 * 16 * GB)

                @block.tensor
                def _(pe):
                    pe.wait_ge(be_in, 16)
                    pe.wait_ge(w_res, 16)
                    regs = [pe.alloc_register(name=f"expert{i}") for i in range(GB)]

                    def experts_of(g):
                        pe.load(regs, be_row[0:1, bass.ds(g * GB, GB)])
                        return [pe.snap(reg, min_val=0, max_val=E2 - 1) for reg in regs]

                    def turn(n, w, q, live):
                        if live(0):
                            pe.wait_ge(x_in[w], (q + 1) * 16)
                            wait(pe, t_act, n)
                            wait(pe, t_dve, n)
                            for b in range(GB):
                                for c in range(C):
                                    last = pe.transpose(ps[:, b // 2, (b % 2 * C + c) * P:(b % 2 * C + c + 1) * P],
                                                        xs[:, w, b, c * P:(c + 1) * P], ident[:])
                            last.then_inc(t_ps, 1)
                        if live(1):
                            g = n - 1
                            e = experts_of(g)
                            pe.wait_ge(t_act, g + 1)
                            pe.wait_ge(t_dve, g + 1)
                            wait(pe, h_ready, g)
                            for b in range(GB):
                                for c in range(C):
                                    last = pe.matmul(ps[:, 2, b * P:(b + 1) * P], xsT[:, (w - 1) % 2, b, c, :],
                                                     w_up[:, bass.ds(e[b], 1), c, :].rearrange("p o m -> p (o m)"),
                                                     start=(c == 0), stop=(c == C - 1))
                            last.then_inc(z_ps, 1)
                        if live(2):
                            g = n - 2
                            pe.wait_ge(h_ready, g + 1)
                            wait(pe, hT_sb, g)
                            for b in range(GB):
                                last = pe.transpose(ps[:, 3, b * P:(b + 1) * P], h[:, w % 2, b, :], ident[:])
                            last.then_inc(hT_ps, 1)
                        if live(3):
                            g = n - 3
                            e = experts_of(g)
                            pe.wait_ge(hT_sb, g + 1)
                            if isinstance(g, int) and g == 0:
                                pe.wait_ge(wd_in, 16)
                            wait(pe, y_act, g)
                            wait(pe, y_dve, g)
                            for b in range(GB):
                                last = pe.matmul(ps[:, 4 + b // 2, (b % 2) * D:(b % 2 + 1) * D],
                                                 hT[:, (w - 3) % 2, b, :],
                                                 w_dn[:, bass.ds(e[b], 1), :].rearrange("p o n -> p (o n)"),
                                                 start=True, stop=True)
                            last.then_inc(y_ps, 1)
                    pipeline(pe, turn)

                @block.scalar
                def _(act):
                    def turn(n, w, q, live):
                        if live(0):
                            act.wait_ge(t_ps, n + 1)
                            wait(act, z_ps, n - 1)
                            act.copy(xsT[:, w % 2, 0:2].rearrange("p b c m -> p (b c m)"), ps[:, 0, :]).then_inc(t_act, 1)
                        if live(1):
                            g = n - 1
                            act.wait_ge(z_ps, g + 1)
                            wait(act, h_ready, g)
                            act.activation(r[:].rearrange("p b m -> p (b m)"), ps[:, 2, :], ACT.Relu).then_inc(r_ready, 1)
                        if live(2):
                            g = n - 2
                            act.wait_ge(hT_ps, g + 1)
                            wait(act, y_ps, g - 1)
                            act.copy(hT[:, w % 2].rearrange("p b m -> p (b m)"), ps[:, 3, :]).then_inc(hT_sb, 1)
                        if live(3):
                            g = n - 3
                            act.wait_ge(y_ps, g + 1)
                            wait(act, y_out[(w - 3) % 2], half(q, w, 3) * 16 * GB)
                            for b in range(2):
                                last = act.activation(ys[:, (w - 3) % 2, b, :], ps[:, 4, b * D:(b + 1) * D], ACT.Copy,
                                                      scale=tail[:, (w - 3) % XR, b, 1:2])
                            last.then_inc(y_act, 1)
                    pipeline(act, turn)

                @block.vector
                def _(dve):
                    def turn(n, w, q, live):
                        if live(0):
                            dve.wait_ge(t_ps, n + 1)
                            wait(dve, z_ps, n - 1)
                            wait(dve, y_act, n - XR + 1)
                            wait(dve, y_dve, n - XR + 1)
                            dve.nop(nofuse=True)
                            dve.tensor_copy(tail[:, w % XR], xs[:, w % XR, :, D:D + 2])
                            dve.tensor_copy(xsT[:, w % 2, 2:4].rearrange("p b c m -> p (b c m)"), ps[:, 1, :]
                                            ).then_inc(t_dve, 1)
                        if live(1):
                            g = n - 1
                            dve.wait_ge(r_ready, g + 1)
                            wait(dve, hT_ps, g - 1)
                            dve.scalar_tensor_tensor(h[:, (w - 1) % 2].rearrange("p b m -> p (b m)"), ps[:, 2, :], 0.0,
                                                     r[:].rearrange("p b m -> p (b m)"), ALU.max, ALU.mult
                                                     ).then_inc(h_ready, 1)
                        if live(3):
                            g = n - 3
                            dve.wait_ge(y_ps, g + 1)
                            wait(dve, y_out[(w - 3) % 2], half(q, w, 3) * 16 * GB)
                            dve.tensor_scalar(yidx[:, (w - 3) % 2, :], tail[:, (w - 3) % XR, :, 0], -1.0, float(T * K2),
                                              ALU.mult, ALU.add)
                            for b in range(2, GB):
                                last = dve.tensor_scalar(ys[:, (w - 3) % 2, b, :], ps[:, 5, (b - 2) * D:(b - 1) * D],
                                                         tail[:, (w - 3) % XR, b, 1:2], None, ALU.mult)
                            last.then_inc(y_dve, 1)
                    pipeline(dve, turn)

        def combine():
            ph = ExitStack()
            with ph:
                def sb(name, shape, dt=F32):
                    return ph.enter_context(nc.sbuf_tensor("cb_" + name, shape, dt))

                def sem(name):
                    return ctx.enter_context(nc.semaphore("cb_" + name))

                RING = 4
                got = wide[:, 0:RING * K2 * D].rearrange("p (r k d) -> p r k d", r=RING, k=K2)
                part = sb("part", [P, 2, D])
                total = sb("total", [P, 2, D])
                here = [sem(f"here{i}") for i in range(RING)]
                summed, added, stored = sem("summed"), sem("added"), [sem("stored0"), sem("stored1")]
                block = ph.enter_context(nc.Block())
                ov = out.rearrange("(t p) d -> t p d", p=P)
                yv = y_rows[0:T * K2, :].rearrange("(t p k) d -> t p k d", p=P, k=K2)

                @block.sync
                def _(sp):
                    def body(q):
                        for w in range(RING):
                            n = q * RING + w
                            wait(sp, summed, n - RING + 1)
                            sp.dma_start(got[:, w], yv[bass.ds(n, 1)].rearrange("o p k d -> p (o k) d")
                                         ).then_inc(here[w], 16)
                    turns(sp, NT // RING, body)

                @block.vector
                def _(dve):
                    def body(q):
                        for w in range(RING):
                            n = q * RING + w
                            dve.wait_ge(here[w], (q + 1) * 16)
                            wait(dve, added, n - 1)
                            dve.tensor_reduce(part[:, w % 2, :], got[:, w].rearrange("p k d -> p d k"), AX.X, ALU.add
                                              ).then_inc(summed, 1)
                            wait(dve, stored[w % 2], (q * 2 + w // 2) * 16)
                            dve.wait_ge(summed, n + 1)
                            dve.nop(nofuse=True)
                            dve.tensor_tensor(total[:, w % 2, :], part[:, w % 2, :],
                                              acc[:, bass.ds(n, 1), :].rearrange("p o d -> p (o d)"), ALU.add
                                              ).then_inc(added, 1)
                    turns(dve, NT // RING, body)

                @block.scalar
                def _(act):
                    def body(q):
                        for w in range(2):
                            act.wait_ge(added, q * 2 + w + 1)
                            act.dma_start(ov[bass.ds(q * 2 + w, 1)].rearrange("o p d -> p (o d)"), total[:, w, :]
                                          ).then_inc(stored[w], 16)
                    turns(act, NT // 2, body)
                    for w in range(2):
                        act.wait_ge(stored[w], NT // 2 * 16)

        router1()
        experts("e1_", N1, comb1, 0, [w1gate, w1up], w1down, True)
        attention1()
        deviations("ln1_")
        attention2()
        deviations("ln2_")
        w_up = sb("w_up", [P, E2, C, M2])
        w_res = sem("w_res")
        route()
        w_dn = wide[:].rearrange("p (e n) -> p e n", e=E2)
        slot_experts()
        combine()


def kernel(x, cond_64, fside_16xSxS_0, mask_BxS_bk0, L0_cond_wt, L0_cond_wg, L0_cond_w_gate, L0_cond_w_up,
           L0_cond_w_down, L0_cond_sw_gate, L0_cond_sw_up, L0_cond_sw_down, L0_attn_Wq, L0_attn_Wk, L0_attn_Wv,
           L0_attn_Wo, L0_attn_rel_emb, L0_cond2_g_in, L0_cond2_null_attn_bias, L0_cond2_Wq, L0_cond2_Wkv,
           L0_cond2_Wo, L0_cond2_g_out, L0_ffn_router_w, L0_ffn_correction_bias, L0_ffn_up_w, L0_ffn_down_w,
           L0_ffn_shared_up_w, L0_ffn_shared_down_w):
    import numpy as _np
    import concourse.bacc as _bacc
    from concourse import mybir as _mybir
    from concourse.bass_utils import run_bass_kernel_spmd as _run

    def arr(a):
        return _np.asarray(a)

    def columns(w, n):
        w = arr(w)
        return w.reshape(w.shape[0], n, w.shape[1] // n).transpose(1, 0, 2)

    def rows(w, n):
        w = arr(w)
        return w.reshape(n, w.shape[0] // n, w.shape[1])

    def up_rows(w):
        return w.reshape(w.shape[0], C, P, w.shape[2]).transpose(2, 0, 1, 3)

    flat = arr(x).reshape(T, D)
    laid = {
        "x": flat,
        "xT": flat.T,
        "condT": arr(cond_64).T,
        "cond": arr(cond_64),
        "bias2": arr(fside_16xSxS_0),
        "mask": arr(mask_BxS_bk0),
        "w1gate": _np.concatenate([arr(L0_cond_w_gate), columns(L0_cond_sw_gate, SH1)]),
        "w1up": _np.concatenate([arr(L0_cond_w_up), columns(L0_cond_sw_up, SH1)]),
        "w1down": _np.concatenate([arr(L0_cond_w_down), rows(L0_cond_sw_down, SH1)]),
        "wtT": arr(L0_cond_wt).T,
        "wgT": arr(L0_cond_wg).T,
        "wqT": arr(L0_attn_Wq).T,
        "wkT": arr(L0_attn_Wk).T,
        "wvT": arr(L0_attn_Wv).T,
        "woT": arr(L0_attn_Wo).T,
        "relT": arr(L0_attn_rel_emb).T,
        "g_in": arr(L0_cond2_g_in).reshape(C, P).T,
        "nbias": arr(L0_cond2_null_attn_bias),
        "wq2": arr(L0_cond2_Wq),
        "wkv2": arr(L0_cond2_Wkv),
        "wo2": arr(L0_cond2_Wo),
        "g_row": arr(L0_cond2_g_out).reshape(1, D),
        "rwT": arr(L0_ffn_router_w).T,
        "cbias": arr(L0_ffn_correction_bias),
        "up2": up_rows(arr(L0_ffn_up_w)),
        "down2": arr(L0_ffn_down_w).transpose(1, 0, 2),
        "up2s": up_rows(columns(L0_ffn_shared_up_w, SH2)),
        "down2s": rows(L0_ffn_shared_down_w, SH2).transpose(1, 0, 2),
    }
    nc = _bacc.Bacc("TRN2", target_bir_lowering=False, num_devices=1)
    arrays, args = {}, {}
    for name, a in laid.items():
        a = _np.ascontiguousarray(a)
        arrays[f"in_{name}"] = a
        args[name] = nc.dram_tensor(f"in_{name}", a.shape, _mybir.dt.from_np(a.dtype), kind="ExternalInput").ap()
    args["out"] = nc.dram_tensor("out_x", (T, D), _mybir.dt.float32, kind="ExternalOutput").ap()
    build(nc, **args)
    r = _run(nc, [arrays], core_ids=[0])
    return r.results[0]["out_x"].reshape(SEQS, S, D)
```

```python
import math
from contextlib import ExitStack

import numpy as np
import concourse.bass as bass
from concourse import mybir

F32 = mybir.dt.float32
F32R = mybir.dt.float32r
U8 = mybir.dt.uint8
ALU = mybir.AluOpType
ACT = mybir.ActivationFunctionType
AX = mybir.AxisListType

P = 128
SEQS, S, D = 64, 64, 256
T = SEQS * S
NT = T // P
BT = 512
NB = T // BT
TPB = BT // P
SPB = BT // S
C = D // P

E1, M1 = 8, 128
SH1 = 2
N1 = E1 + SH1
K1 = 2
G = 64

H1, DK1 = 16, 16
H2, DH2 = 16, 64
J2 = H2 // 2
KN = S + 1
BUCKETS = 32
REL = 2 * S - 1

E2, M2 = 64, 128
GROUPS, TOPG, K2 = 8, 4, 8
SH2 = 4
N2 = E2 + SH2
ROUTE_SCALE = 2.5
NBLK = -(-(T * K2 // P + E2 - 1) // 8) * 8
GB = 4
NG = NBLK // GB
ROW = D + 2
I32 = mybir.dt.int32
EPS = 1e-5
MASKED = -1.0e30
TAKEN = -3.0e38
UNMATCHED = 3.0e38


def bucket_runs():
    half, exact = BUCKETS // 2, BUCKETS // 4
    rel = np.arange(-(S - 1), S)
    n = np.abs(rel)
    far = np.log(np.maximum(n, 1).astype(np.float32) / np.float32(exact)) / np.float32(math.log(128 / exact))
    far = np.minimum(exact + (far * np.float32(half - exact)).astype(np.int32), half - 1)
    bucket = np.where(n < exact, n, far) + (rel > 0) * half
    runs, at = [], 0
    for i in range(1, REL + 1):
        if i == REL or bucket[i] != bucket[at]:
            runs.append((at, i, int(bucket[at])))
            at = i
    return runs


class Steps:

    def __init__(self, eng, sem, turn=0, per=0, start=0):
        self.eng, self.sem, self.per, self.k = eng, sem, per, 0
        self.base = turn * per + start if per else start

    def done(self, ins):
        self.k += 1
        ins.then_inc(self.sem, 1)
        self.eng.wait_ge(self.sem, self.base + self.k)

    def close(self):
        assert self.k == self.per, (self.k, self.per)


def wait(eng, sem, value):
    if not (isinstance(value, int) and value <= 0):
        eng.wait_ge(sem, value)


def turns(eng, n, body):
    body(0)
    with eng.Fori(1, n) as i:
        body(i)


def blocks(eng, body):
    body(0, False)
    with eng.Fori(1, NB - 1) as b:
        body(b, False)
    body(NB - 1, True)


def build(nc, x, xT, condT, cond, bias2, mask, w1gate, w1up, w1down, wtT, wgT,
          wqT, wkT, wvT, woT, relT, g_in, nbias, wq2, wkv2, wo2, rwT, cbias, up2, down2,
          up2s, down2s, g_row, out):
    ctx = ExitStack()
    with ctx:
        def sb(name, shape, dt=F32):
            return ctx.enter_context(nc.sbuf_tensor(name, shape, dt))

        def sem(name):
            return ctx.enter_context(nc.semaphore(name))

        rel_rows = nc.dram_tensor("rel_rows", (S, H1, REL), F32).ap()
        x_slots = nc.dram_tensor("x_slots", (NBLK * P, ROW), F32).ap()
        y_rows = nc.dram_tensor("y_rows", (T * K2, D), F32).ap()
        block_expert = nc.dram_tensor("block_expert", (3 * P,), I32).ap()

        ctx.enter_context(nc.allow_non_contiguous_dma(reason="a few columns of constants"))
        ps = ctx.enter_context(nc.psum_tensor("ps", [P, 8, 512], F32))

        EARLY = 31
        wide = sb("wide", [P, E2 * D])
        feat = wide[:, 0:C * T].rearrange("p (c t) -> p c t", c=C)
        acc = sb("acc", [P, NT, D])
        ident = sb("ident", [P, P])
        mv1 = sb("mv1", [P, NT, 2])
        rstd = sb("rstd", [P, NT])

        def make_identity(pool, seen, done):
            pool.memset(ident[:], 0.0).then_inc(seen, 1)
            pool.wait_ge(seen, 1)
            pool.affine_select(out=ident[:], in_=ident[:], compare_op=ALU.not_equal, fill=1.0, base=0,
                               pattern=[[-1, P]], channel_multiplier=1).then_inc(done, 1)

        halves = ExitStack()
        WIDE = 2 * C * M1 + D
        xh, xl, wh, wl = (halves.enter_context(nc.sbuf_tensor(name, shape, F32R)) for name, shape in (
            ("xh", [P, C, T]), ("xl", [P, C, T]), ("wh", [P, 2, WIDE]), ("wl", [P, 2, WIDE])))
        comb1 = halves.enter_context(nc.sbuf_tensor("comb1", [P, NT, N1], F32))
        wf = halves.enter_context(nc.sbuf_tensor("wf", [P, 2, WIDE], F32))
        w_in = [sem("weights0"), sem("weights1")]
        xh_ready, xl_ready, wh_ready, wl_ready = (sem(n) for n in ("xh_ready", "xl_ready", "wh_ready", "wl_ready"))

        def load_expert(sp, e, w):
            for i, src in enumerate((w1gate, w1up)):
                sp.dma_start(wf[:, w, i * C * M1:(i + 1) * C * M1].rearrange("p (c m) -> p c m", c=C),
                             src[bass.ds(e, 1)].rearrange("o (c p) m -> p (o c) m", p=P)).then_inc(w_in[w], 16)
            sp.dma_start(wf[:, w, 2 * C * M1:], w1down[bass.ds(e, 1)].rearrange("o p n -> p (o n)")
                         ).then_inc(w_in[w], 16)

        def router1():
            ph = ExitStack()
            with ph:
                def sb(name, shape, dt=F32):
                    return ph.enter_context(nc.sbuf_tensor(name, shape, dt))

                def sem(name):
                    return ctx.enter_context(nc.semaphore("r1_" + name))

                wt = sb("wt", [P, C, P])
                wg = sb("wg", [P, P])
                cT = sb("cT", [P, SEQS])
                lT = sb("lT", [P, BT])
                s1 = sb("s1", [P, NT, E1])
                left = sb("left", [P, NT, E1])
                top8 = sb("top8", [P, NT, 8])
                stat = sb("stat", [P, NT])
                small_in, x_in = sem("small_in"), sem("x_in")
                zeroed, id_ready, padded = sem("zeroed"), sem("id_ready"), sem("padded")
                lT_ps, lT_sb, l_ps, l_sb = sem("lT_ps"), sem("lT_sb"), sem("l_ps"), sem("l_sb")
                shifted, expd, dve_step = sem("shifted"), sem("expd"), sem("dve_step")
                block = ph.enter_context(nc.Block())

                @block.sync
                def _(sp):
                    for c in range(C):
                        sp.dma_start(feat[:, c, :], xT[c * P:(c + 1) * P, :]).then_inc(x_in, 16)
                    sp.wait_ge(padded, 3)
                    sp.dma_start(wt[:, :, 0:E1], wtT.rearrange("(c p) e -> p c e", p=P)).then_inc(small_in, 16)
                    sp.dma_start(wg[0:G, 0:E1], wgT).then_inc(small_in, 16)
                    sp.dma_start(cT[0:G], condT).then_inc(small_in, 16)
                    for w in range(2):
                        load_expert(sp, w, w)

                @block.gpsimd
                def _(pool):
                    for pad in (wt, wg, cT):
                        pool.memset(pad[:], 0.0).then_inc(padded, 1)
                    make_identity(pool, zeroed, id_ready)
                    pool.memset(acc[:], 0.0)
                    pool.wait_ge(wh_ready, 1)
                    pool.tensor_tensor(wl[:, 0, :], wf[:, 0, :], wh[:, 0, :], ALU.subtract).then_inc(wl_ready, 1)

                @block.tensor
                def _(pe):
                    pe.wait_ge(small_in, 48)
                    pe.wait_ge(x_in, 16 * C)
                    pe.wait_ge(id_ready, 1)

                    def body(b):
                        for c in range(C):
                            pe.matmul(ps[:, 0, :], wt[:, c, :], feat[:, c, bass.ds(b * BT, BT)],
                                      start=(c == 0), stop=False)
                        pe.matmul(ps[:, 0, :], wg[:],
                                  cT[:, bass.ds(b * SPB, SPB)].unsqueeze(2).to_broadcast([P, SPB, S]),
                                  start=False, stop=True).then_inc(lT_ps, 1)
                        pe.wait_ge(lT_sb, b + 1)
                        wait(pe, l_sb, b)
                        for t in range(TPB):
                            last = pe.transpose(ps[:, 1, t * P:(t + 1) * P], lT[:, t * P:(t + 1) * P], ident[:])
                        last.then_inc(l_ps, 1)
                    turns(pe, NB, body)

                @block.scalar
                def _(act):
                    def body(b):
                        act.wait_ge(lT_ps, b + 1)
                        wait(act, l_ps, b)
                        act.activation(lT[:], ps[:, 0, :], ACT.Copy, scale=0.5).then_inc(lT_sb, 1)
                        act.copy(xh[:, :, bass.ds(b * BT, BT)], feat[:, :, bass.ds(b * BT, BT)]).then_inc(xh_ready, 1)
                    turns(act, NB, body)
                    act.wait_ge(w_in[0], 48)
                    act.copy(wh[:, 0, :], wf[:, 0, :]).then_inc(wh_ready, 1)
                    act.wait_ge(shifted, 1)
                    act.activation(s1[:], s1[:], ACT.Exp).then_inc(expd, 1)

                @block.vector
                def _(dve):
                    with dve.Fori(0, NB) as b:
                        dve.wait_ge(l_ps, b + 1)
                        dve.tensor_copy(s1[:, bass.ds(b * TPB, TPB), :],
                                        ps[:, 1, :].rearrange("p (t e) -> p t e", t=TPB)[:, :, 0:E1]).then_inc(l_sb, 1)
                        dve.wait_ge(xh_ready, b + 1)
                        dve.nop(nofuse=True)
                        dve.tensor_tensor(xl[:, :, bass.ds(b * BT, BT)], feat[:, :, bass.ds(b * BT, BT)],
                                          xh[:, :, bass.ds(b * BT, BT)], ALU.subtract).then_inc(xl_ready, 1)
                    dve.wait_ge(l_sb, NB)
                    st = Steps(dve, dve_step)
                    st.done(dve.tensor_reduce(stat[:], s1[:], AX.X, ALU.max))
                    dve.tensor_tensor(s1[:], s1[:], stat[:].unsqueeze(2).to_broadcast([P, NT, E1]),
                                      ALU.subtract).then_inc(shifted, 1)
                    dve.wait_ge(expd, 1)
                    st.done(dve.tensor_reduce(stat[:], s1[:], AX.X, ALU.add))
                    st.done(dve.reciprocal(stat[:], stat[:]))
                    st.done(dve.tensor_tensor(s1[:], s1[:], stat[:].unsqueeze(2).to_broadcast([P, NT, E1]), ALU.mult))
                    for t in range(NT):
                        last = dve.max(top8[:, t, :], s1[:, t, :])
                    st.done(last)
                    st.done(dve.memset(top8[:, :, K1:8], UNMATCHED))
                    for t in range(NT):
                        last = dve.match_replace(left[:, t, :], top8[:, t, :], s1[:, t, :], -1.0)
                    st.done(last)
                    st.done(dve.tensor_scalar(left[:], left[:], -1.0, None, ALU.is_equal))
                    st.done(dve.tensor_tensor(s1[:], s1[:], left[:], ALU.mult))
                    st.done(dve.tensor_reduce(stat[:], s1[:], AX.X, ALU.add))
                    st.done(dve.tensor_scalar(stat[:], stat[:], 1e-20, None, ALU.add))
                    st.done(dve.reciprocal(stat[:], stat[:]))
                    dve.tensor_tensor(comb1[:, :, 0:E1], s1[:], stat[:].unsqueeze(2).to_broadcast([P, NT, E1]),
                                      ALU.mult)
                    dve.memset(comb1[:, :, E1:N1], 1.0)

        def experts():
            ph = ExitStack()
            TURNS = N1 // 2
            PER = 2 * NB
            with ph:
                def sb(name, shape, dt=F32):
                    return ph.enter_context(nc.sbuf_tensor("e1_" + name, shape, dt))

                def sem(name):
                    return ctx.enter_context(nc.semaphore("e1_" + name))

                r = sb("r", [P, 2, BT])
                h = sb("h", [P, 2, BT])
                hh, hl = sb("hh", [P, 2, BT], F32R), sb("hl", [P, 2, BT], F32R)
                cexp = sb("cexp", [P, 2, NT])
                hh_ready, hl_ready = sem("hh_ready"), sem("hl_ready")
                z_ps, y_ps, r_ready, leaky, h_ready, y_used, c_ready = (
                    sem(n) for n in ("z_ps", "y_ps", "r_ready", "leaky", "h_ready", "y_used", "c_ready"))
                block = ph.enter_context(nc.Block())

                def z_bank(i, n):
                    return ps[:, 2 * (n % 2) + i, :]

                def y_bank(n, t):
                    return ps[:, 4 + 2 * (n % 2) + t // 2, (t % 2) * D:(t % 2 + 1) * D]

                def turns_of(eng, body):
                    body(0, False)
                    with eng.Fori(1, TURNS - 1) as turn:
                        body(turn, False)
                    body(TURNS - 1, True)

                @block.sync
                def _(sp):
                    def body(i):
                        for w in range(2):
                            sp.wait_ge(wl_ready, i * 2 + w + 1)
                            load_expert(sp, i * 2 + 2 + w, w)
                    with sp.Fori(0, TURNS - 1) as i:
                        body(i)

                @block.tensor
                def _(pe):
                    def product(out, h0, l0, h1, l1, start, stop):
                        pe.matmul(out, h0, h1, start=start, stop=False)
                        pe.matmul(out, h0, l1, start=False, stop=False)
                        return pe.matmul(out, l0, h1, start=False, stop=stop)

                    def z(n, turn):
                        w, b = n // NB % 2, n % NB
                        wait(pe, h_ready, turn * PER + n - 1)
                        if b == 0:
                            pe.wait_ge(wl_ready, turn * 2 + n // NB + 1)
                        for i in range(2):
                            for c in range(C):
                                cols = slice((i * C + c) * M1, (i * C + c + 1) * M1)
                                last = product(z_bank(i, n), wh[:, w, cols], wl[:, w, cols],
                                               xh[:, c, b * BT:(b + 1) * BT], xl[:, c, b * BT:(b + 1) * BT],
                                               c == 0, c == C - 1)
                        last.then_inc(z_ps, 1)

                    def y(n, turn):
                        w = n // NB
                        pe.wait_ge(hl_ready, turn * PER + n + 1)
                        wait(pe, y_used, turn * PER + n - 1)
                        for t in range(TPB):
                            rows = slice(t * P, (t + 1) * P)
                            last = product(y_bank(n, t), hh[:, n % 2, rows], hl[:, n % 2, rows],
                                           wh[:, w, 2 * C * M1:], wl[:, w, 2 * C * M1:], True, True)
                        last.then_inc(y_ps, 1)

                    def body(turn, final):
                        for n in range(PER):
                            if not (final and n + 2 >= PER):
                                z(n + 2, turn)
                            y(n, turn)
                    z(0, 0)
                    z(1, 0)
                    turns_of(pe, body)

                @block.scalar
                def _(act):
                    def weights(pair, w):
                        act.wait_ge(w_in[w], (pair + 1) * 48)
                        wait(act, y_ps, (pair * 2 + w - 1) * NB)
                        act.copy(wh[:, w, :], wf[:, w, :]).then_inc(wh_ready, 1)

                    def body(turn, final):
                        for n in range(PER):
                            N = turn * PER + n
                            act.wait_ge(z_ps, N + 1)
                            wait(act, h_ready, N - 1)
                            act.activation(r[:, n % 2, :], z_bank(0, n), ACT.Copy, scale=0.01).then_inc(r_ready, 1)
                            act.wait_ge(h_ready, N + 1)
                            wait(act, y_ps, N - 1)
                            act.copy(hh[:, n % 2, :], h[:, n % 2, :]).then_inc(hh_ready, 1)
                            if n == 3:
                                weights(turn, 1)
                            elif n == NB + 3 and not final:
                                weights(turn + 1, 0)
                    turns_of(act, body)

                @block.gpsimd
                def _(pool):
                    def weights(e, w):
                        pool.wait_ge(wh_ready, e + 1)
                        pool.tensor_tensor(wl[:, w, :], wf[:, w, :], wh[:, w, :], ALU.subtract).then_inc(wl_ready, 1)

                    def body(turn, final):
                        for n in range(PER):
                            pool.wait_ge(hh_ready, turn * PER + n + 1)
                            pool.tensor_tensor(hl[:, n % 2, :], h[:, n % 2, :], hh[:, n % 2, :], ALU.subtract
                                               ).then_inc(hl_ready, 1)
                            if n == 3:
                                weights(turn * 2 + 1, 1)
                            elif n == NB + 3 and not final:
                                weights(turn * 2 + 2, 0)
                    turns_of(pool, body)

                @block.vector
                def _(dve):
                    def accumulate(n, turn):
                        w, b = n // NB, n % NB
                        if b == 0:
                            dve.tensor_copy(cexp[:, w, :], comb1[:, :, bass.ds(turn * 2 + w, 1)].rearrange(
                                "p t o -> p (t o)")).then_inc(c_ready, 1)
                            dve.wait_ge(c_ready, turn * 2 + w + 1)
                        dve.wait_ge(y_ps, turn * PER + n + 1)
                        for t in range(TPB):
                            tile = b * TPB + t
                            last = dve.scalar_tensor_tensor(acc[:, tile, :], y_bank(n, t), cexp[:, w, tile:tile + 1],
                                                            acc[:, tile, :], ALU.mult, ALU.add)
                        last.then_inc(y_used, 1)

                    def gate(n, turn):
                        N = turn * PER + n
                        dve.wait_ge(r_ready, N + 1)
                        dve.tensor_tensor(r[:, n % 2, :], z_bank(0, n), r[:, n % 2, :], ALU.max).then_inc(leaky, 1)
                        dve.wait_ge(leaky, N + 1)
                        wait(dve, hl_ready, N - 1)
                        dve.tensor_tensor(h[:, n % 2, :], r[:, n % 2, :], z_bank(1, n), ALU.mult).then_inc(h_ready, 1)

                    def body(turn, final):
                        for n in range(PER):
                            if not (final and n + 2 >= PER):
                                gate(n + 2, turn)
                            accumulate(n, turn)
                    gate(0, 0)
                    gate(1, 0)
                    turns_of(dve, body)

        def attention1():
            ph = ExitStack()
            with ph:
                def sb(name, shape, dt=F32):
                    return ph.enter_context(nc.sbuf_tensor("a1_" + name, shape, dt))

                def sem(name):
                    return ctx.enter_context(nc.semaphore("a1_" + name))

                wq, wk, wv, wo = (sb(n, [P, C, D]) for n in ("wq", "wk", "wv", "wo"))
                rel = sb("rel", [H1, BUCKETS])
                reld = sb("reld", [H1, REL])
                bias = sb("bias", [P, H1, S])
                own = sb("own", [P, 8])
                xb = sb("xb", [P, TPB, D])
                xres = sb("xres", [P, TPB, D])
                xo = sb("xo", [P, 2, D])
                pad = sb("pad", [P, ROW])
                pad_i = sb("pad_i", [P, 1], I32)
                pad_step = sem("pad_step")
                hT = sb("hT", [P, C, BT])
                qT = sb("qT", [P, C, BT])
                kT = sb("kT", [P, C, BT])
                kbd = sb("kbd", [P, 2, C, 2, 8, S])
                vbd = sb("vbd", [P, TPB, 8, 2, 2, DK1])
                sc = sb("sc", [P, 2, H1, S])
                mx = sb("mx", [P, 2, H1])
                rs = sb("rs", [P, 2, H1])
                pT = sb("pT", [P, 2, 8, P])
                at = sb("at", [P, D])
                atT = sb("atT", [P, C, P])
                bst = sb("bst", [P, 6])
                mv = sb("mv", [P, 2])
                w_in, rel_in, rel_sb, rel_out, bias_in, res_in = (
                    sem(n) for n in ("w_in", "rel_in", "rel_sb", "rel_out", "bias_in", "res_in"))
                padded = sem("padded")
                s_add, added, kept = sem("s_add"), sem("added"), sem("kept")
                own_step, v_zero = sem("own_step"), sem("v_zero")
                xb_ready, hT_ps, hT_act, hT_dve = sem("xb_ready"), sem("hT_ps"), sem("hT_act"), sem("hT_dve")
                qk_ps, qT_sb, kT_sb, v_ps, v_sb = sem("qk_ps"), sem("qT_sb"), sem("kT_sb"), sem("v_ps"), sem("v_sb")
                kbd_ready, s_ps, s_sh, e_ready, rs_ready = (
                    sem(n) for n in ("kbd_ready", "s_ps", "s_sh", "e_ready", "rs_ready"))
                pT_ps, pT_sb, o_ps, at_sb, aT_ps, aT_sb, yo_ps, tile_done, dve_step = (
                    sem(n) for n in ("pT_ps", "pT_sb", "o_ps", "at_sb", "aT_ps", "aT_sb", "yo_ps", "tile_done",
                                     "dve_step"))
                block = ph.enter_context(nc.Block())
                runs = bucket_runs()

                def value_parts(a):
                    for s in range(2):
                        for h in range(2):
                            src = ps[s * S:(s + 1) * S, 6 + a, :].rearrange("p (t j h d) -> p (t j) h d",
                                                                            t=2, j=8, h=2)[:, :, h, :]
                            dst = vbd[h * S:(h + 1) * S, 2 * a:2 * a + 2, :, s, h, :]
                            yield dst.rearrange("p t j d -> p (t j) d"), src

                @block.sync
                def _(sp):
                    for dst, src in ((wq, wqT), (wk, wkT), (wv, wvT), (wo, woT)):
                        sp.dma_start(dst[:], src.rearrange("(c p) n -> p c n", p=P)).then_inc(w_in, 16)
                    sp.dma_start(rel[:], relT).then_inc(rel_in, 16)
                    sp.wait_ge(rel_sb, len(runs))
                    sp.dma_start(rel_rows.rearrange("q h r -> h q r"),
                                 reld[:].unsqueeze(1).to_broadcast([H1, S, REL])).then_inc(rel_out, 16)
                    sp.wait_ge(rel_out, 16)
                    for s in range(2):
                        diag = bass.AP(rel_rows.tensor, S - 1, [[H1 * REL - 1, S], [REL, H1], [1, S]])
                        sp.dma_start(bias[s * S:(s + 1) * S], diag).then_inc(bias_in, 16)
                    xv = x.rearrange("(t p) d -> p t d", p=P)

                    def residual(b):
                        wait(sp, added, b * TPB)
                        sp.dma_start(xres[:], xv[:, bass.ds(b * TPB, TPB), :]).then_inc(res_in, 16)
                        if isinstance(b, int):
                            sp.wait_ge(pad_step, 3)
                        for i in range(NBLK // 8 // NB):
                            sp.dma_start(slots8[bass.ds(b * (NBLK // 8 // NB) + i, 1)].rearrange("o p b d -> p (o b) d"),
                                         pad[:].unsqueeze(1).to_broadcast([P, 8, ROW])).then_inc(padded, 16)
                    slots8 = x_slots.rearrange("(g b p) d -> g p b d", p=P, b=8)
                    turns(sp, NB, residual)
                    sp.wait_ge(padded, NBLK // 8 * 16)

                @block.gpsimd
                def _(pool):
                    pool.memset(pad[:], 0.0).then_inc(pad_step, 1)
                    pool.iota(pad_i[:], pattern=[[0, 1]], base=0, channel_multiplier=-1).then_inc(pad_step, 1)
                    pool.wait_ge(pad_step, 2)
                    pool.tensor_copy(pad[:, D:D + 1], pad_i[:]).then_inc(pad_step, 1)
                    pool.memset(own[:], 1.0).then_inc(own_step, 1)
                    pool.wait_ge(own_step, 1)
                    pool.affine_select(out=own[:], in_=own[:], compare_op=ALU.is_ge, fill=0.0, base=0,
                                       pattern=[[-DK1, 8]], channel_multiplier=1).then_inc(own_step, 1)
                    pool.wait_ge(own_step, 2)
                    pool.affine_select(out=own[:], in_=own[:], compare_op=ALU.is_ge, fill=0.0, base=DK1 - 1,
                                       pattern=[[DK1, 8]], channel_multiplier=-1).then_inc(own_step, 1)
                    pool.wait_ge(own_step, 3)
                    pool.memset(vbd[:], 0.0).then_inc(v_zero, 1)

                    def keys_apart(b, t):
                        pool.wait_ge(kT_sb, b * C + C)
                        wait(pool, s_ps, b * TPB + t - 1)
                        for c in range(C):
                            kk = kT[:, c, t * P:(t + 1) * P].rearrange("p (s k) -> p s k", s=2)
                            pool.tensor_tensor(kbd[:, t % 2, c], kk.unsqueeze(2).to_broadcast([P, 2, 8, S]),
                                               own[:].unsqueeze(1).unsqueeze(3).to_broadcast([P, 2, 8, S]),
                                               ALU.mult).then_inc(kbd_ready, 1)

                    def body(b, final):
                        for t in range(TPB):
                            keys_apart(b, t)
                    blocks(pool, body)

                @block.tensor
                def _(pe):
                    def scores(b, t):
                        n = b * TPB + t
                        pe.wait_ge(kbd_ready, (n + 1) * C)
                        if t >= 2:
                            pe.wait_ge(s_add, n - 1)
                        else:
                            pe.wait_ge(qT_sb, b * C + C)
                            pe.wait_ge(kT_sb, b * C + C)
                        for c in range(C):
                            for s in range(2):
                                last = pe.matmul(ps[s * S:(s + 1) * S, 2 + 2 * (t % 2) + c, :],
                                                 qT[:, c, t * P + s * S:t * P + (s + 1) * S],
                                                 kbd[:, t % 2, c, s].rearrange("p h k -> p (h k)"),
                                                 start=True, stop=True)
                        last.then_inc(s_ps, 1)

                    def transpose_x(b):
                        pe.wait_ge(xb_ready, b + 1)
                        wait(pe, s_add, b * TPB - 1)
                        for c in range(C):
                            for t in range(TPB):
                                last = pe.transpose(ps[:, 2 + c, t * P:(t + 1) * P], xb[:, t, c * P:(c + 1) * P],
                                                    ident[:])
                        last.then_inc(hT_ps, 1)

                    def queries_keys(b):
                        pe.wait_ge(hT_act, b + 1)
                        pe.wait_ge(hT_dve, b + 1)
                        wait(pe, s_add, b * TPB)
                        for w, bank in ((wk, 2), (wq, 4)):
                            for m in range(C):
                                for c in range(C):
                                    last = pe.matmul(ps[:, bank + m, :], w[:, c, m * P:(m + 1) * P], hT[:, c, :],
                                                     start=(c == 0), stop=(c == C - 1))
                                last.then_inc(qk_ps, 1)

                    def values(b):
                        wait(pe, pT_sb, b * TPB)
                        for t in range(TPB):
                            for c in range(C):
                                last = pe.matmul(ps[:, 6 + t // 2, (t % 2) * D:(t % 2 + 1) * D],
                                                 hT[:, c, t * P:(t + 1) * P], wv[:, c, :],
                                                 start=(c == 0), stop=(c == C - 1))
                        last.then_inc(v_ps, 1)

                    def transpose_p(b, t):
                        n = b * TPB + t
                        pe.wait_ge(e_ready, n + 1)
                        if t == 0:
                            pe.wait_ge(v_sb, b * 8 + 8)
                        else:
                            pe.wait_ge(pT_sb, n)
                        for j in range(8):
                            last = pe.transpose(ps[:, 6 + j // 4, (j % 4) * P:(j % 4 + 1) * P],
                                                sc[:, t % 2, 2 * j:2 * j + 2, :].rearrange("p h k -> p (h k)"),
                                                ident[:])
                        last.then_inc(pT_ps, 1)

                    def outputs(b, t):
                        n = b * TPB + t
                        pe.wait_ge(pT_sb, n + 1)
                        wait(pe, at_sb, n)
                        for j in range(8):
                            last = pe.matmul(ps[:, 0, j * 64:(j + 1) * 64], pT[:, t % 2, j, :],
                                             vbd[:, t, j].rearrange("p s h d -> p (s h d)"),
                                             start=True, stop=True)
                        last.then_inc(o_ps, 1)

                    def transpose_o(b, t):
                        n = b * TPB + t
                        pe.wait_ge(at_sb, n + 1)
                        wait(pe, added, n)
                        for c in range(C):
                            last = pe.transpose(ps[:, 1, c * P:(c + 1) * P], at[:, c * P:(c + 1) * P], ident[:])
                        last.then_inc(aT_ps, 1)

                    def project(b, t):
                        pe.wait_ge(aT_sb, b * TPB + t + 1)
                        for c in range(C):
                            last = pe.matmul(ps[:, 1, D:2 * D], atT[:, c, :], wo[:, c, :],
                                             start=(c == 0), stop=(c == C - 1))
                        last.then_inc(yo_ps, 1)

                    pe.wait_ge(w_in, 64)
                    transpose_x(0)
                    queries_keys(0)
                    scores(0, 0)
                    values(0)
                    scores(0, 1)

                    def body(b, final):
                        for t in range(TPB):
                            transpose_p(b, t)
                            if t >= 2:
                                project(b, t - 2)
                            if t >= 1:
                                outputs(b, t - 1)
                            if t + 2 < TPB:
                                scores(b, t + 2)
                            elif t + 2 == TPB and not final:
                                transpose_x(b + 1)
                            elif not final:
                                queries_keys(b + 1)
                            if t >= 1:
                                transpose_o(b, t - 1)
                        project(b, TPB - 2)
                        outputs(b, TPB - 1)
                        if not final:
                            scores(b + 1, 0)
                        transpose_o(b, TPB - 1)
                        if not final:
                            values(b + 1)
                        project(b, TPB - 1)
                        if not final:
                            scores(b + 1, 1)
                    blocks(pe, body)

                @block.scalar
                def _(act):
                    def hidden(b):
                        wait(act, hT_ps, b)
                        act.nop(nofuse=True)
                        act.copy(xb[:], acc[:, bass.ds(b * TPB, TPB), :]).then_inc(xb_ready, 1)

                    def features_0(b):
                        act.wait_ge(hT_ps, b + 1)
                        act.copy(hT[:, 0, :], ps[:, 2, :]).then_inc(hT_act, 1)

                    def queries_keys(b):
                        for m in range(C):
                            act.wait_ge(qk_ps, b * 2 * C + m + 1)
                            act.copy(kT[:, m, :], ps[:, 2 + m, :]).then_inc(kT_sb, 1)
                        for m in range(C):
                            act.wait_ge(qk_ps, b * 2 * C + C + m + 1)
                            act.activation(qT[:, m, :], ps[:, 4 + m, :], ACT.Copy, scale=DK1 ** -0.5).then_inc(qT_sb, 1)

                    def exponential(b, t):
                        act.wait_ge(s_sh, b * TPB + t + 1)
                        act.activation(sc[:, t % 2], sc[:, t % 2], ACT.Exp).then_inc(e_ready, 1)

                    def transposed_p(b, t):
                        n = b * TPB + t
                        act.wait_ge(pT_ps, n + 1)
                        wait(act, o_ps, n - 1)
                        act.copy(pT[:, t % 2].rearrange("p j q -> p (j q)"), ps[:, 6:8, :].rearrange("p a b -> p (a b)")
                                 ).then_inc(pT_sb, 1)

                    def transposed_o(b, t):
                        n = b * TPB + t
                        act.wait_ge(aT_ps, n + 1)
                        wait(act, yo_ps, n)
                        act.copy(atT[:].rearrange("p c q -> p (c q)"), ps[:, 1, 0:C * P]).then_inc(aT_sb, 1)

                    def values(b):
                        act.wait_ge(v_ps, b + 1)
                        for dst, src in value_parts(0):
                            act.copy(dst, src).then_inc(v_sb, 1)

                    def keep(b, t):
                        n = b * TPB + t
                        act.wait_ge(added, n + 1)
                        act.nop(nofuse=True)
                        act.copy(acc[:, bass.ds(n, 1), :].rearrange("p o d -> p (o d)"), xo[:, t % 2, :]).then_inc(kept, 1)

                    hidden(0)
                    features_0(0)
                    queries_keys(0)
                    exponential(0, 0)
                    values(0)

                    def body(b, final):
                        for t in range(TPB):
                            transposed_p(b, t)
                            if t >= 3:
                                keep(b, t - 3)
                            if t + 1 < TPB:
                                exponential(b, t + 1)
                            if t == 0 and not final:
                                hidden(b + 1)
                            if t + 2 == TPB and not final:
                                features_0(b + 1)
                            if t + 1 == TPB and not final:
                                queries_keys(b + 1)
                            if t >= 1:
                                transposed_o(b, t - 1)
                        keep(b, TPB - 3)
                        transposed_o(b, TPB - 1)
                        keep(b, TPB - 2)
                        if not final:
                            exponential(b + 1, 0)
                            values(b + 1)
                        keep(b, TPB - 1)
                    blocks(act, body)

                @block.vector
                def _(dve):
                    dve.wait_ge(rel_in, 16)
                    for lo, hi, bucket in runs:
                        dve.tensor_copy(reld[:, lo:hi], rel[:, bucket:bucket + 1].to_broadcast([H1, hi - lo])
                                        ).then_inc(rel_sb, 1)
                    dve.wait_ge(v_zero, 1)
                    dve.wait_ge(bias_in, 32)
                    PER, AHEAD = TPB * 5, 3

                    def features_1(b):
                        dve.wait_ge(hT_ps, b + 1)
                        dve.tensor_copy(hT[:, 1, :], ps[:, 3, :]).then_inc(hT_dve, 1)

                    def values(b):
                        dve.wait_ge(v_ps, b + 1)
                        for dst, src in value_parts(1):
                            dve.tensor_copy(dst, src).then_inc(v_sb, 1)

                    def shift(b, t, st):
                        n = b * TPB + t
                        dve.wait_ge(s_ps, n + 1)
                        wait(dve, pT_ps, n - 1)
                        q = sc[:, t % 2]
                        dve.tensor_tensor(q.rearrange("p h k -> p (h k)"),
                                          ps[:, 2 + 2 * (t % 2):4 + 2 * (t % 2), :].rearrange("p a b -> p (a b)"),
                                          bias[:].rearrange("p h k -> p (h k)"), ALU.add).then_inc(s_add, 1)
                        dve.wait_ge(s_add, n + 1)
                        st.done(dve.tensor_reduce(mx[:, t % 2], q, AX.X, ALU.max))
                        dve.tensor_tensor(q, q, mx[:, t % 2].unsqueeze(2).to_broadcast([P, H1, S]), ALU.subtract
                                          ).then_inc(s_sh, 1)

                    def row_sums(b, t, st):
                        dve.wait_ge(e_ready, b * TPB + t + 1)
                        wait(dve, at_sb, b * TPB + t - 1)
                        st.done(dve.tensor_reduce(rs[:, t % 2], sc[:, t % 2], AX.X, ALU.add))
                        st.done(dve.reciprocal(rs[:, t % 2], rs[:, t % 2]))

                    def output(b, t):
                        n = b * TPB + t
                        dve.wait_ge(o_ps, n + 1)
                        wait(dve, aT_ps, n)
                        for s in range(2):
                            src = ps[s * S:(s + 1) * S, 0, :].rearrange(
                                "p (j s h d) -> p j s (h d)", j=8, s=2, h=2)[:, :, s, :]
                            src = src.rearrange("p j (h d) -> p j h d", h=2)
                            dst = at[s * S:(s + 1) * S, :].rearrange("p (j h d) -> p j h d", j=8, h=2)
                            sel = rs[s * S:(s + 1) * S, t % 2, :].rearrange("p (j h) -> p j h", h=2)
                            last = dve.tensor_tensor(dst, src, sel.unsqueeze(3).to_broadcast([S, 8, 2, DK1]),
                                                     ALU.mult)
                        last.then_inc(at_sb, 1)

                    def projected(b, t, st):
                        n = b * TPB + t
                        dve.wait_ge(yo_ps, n + 1)
                        wait(dve, kept, n - 1)
                        if t == 0:
                            dve.wait_ge(res_in, b * 16 + 16)
                        dve.tensor_tensor(xo[:, t % 2, :], ps[:, 1, D:2 * D], xres[:, t, :], ALU.add).then_inc(added, 1)
                        dve.wait_ge(added, n + 1)
                        st.done(dve.bn_stats(bst[:], xo[:, t % 2, :]))
                        dve.nop(nofuse=True)
                        st.done(dve.bn_aggr(mv[:], bst[:]))
                        dve.nop(nofuse=True)
                        dve.tensor_copy(mv1[:, bass.ds(n, 1), :].rearrange("p o d -> p (o d)"), mv[:]
                                        ).then_inc(tile_done, 1)

                    st = Steps(dve, dve_step)
                    features_1(0)
                    shift(0, 0, st)
                    values(0)
                    row_sums(0, 0, st)

                    def body(b, final):
                        st = Steps(dve, dve_step, b, PER, AHEAD)
                        for t in range(TPB):
                            if t + 1 < TPB:
                                shift(b, t + 1, st)
                            if t >= 1:
                                output(b, t - 1)
                            if t >= 2:
                                projected(b, t - 2, st)
                            if t + 1 < TPB:
                                row_sums(b, t + 1, st)
                            if t + 2 == TPB and not final:
                                features_1(b + 1)
                        projected(b, TPB - 2, st)
                        output(b, TPB - 1)
                        if not final:
                            shift(b + 1, 0, st)
                            values(b + 1)
                        projected(b, TPB - 1, st)
                        if not final:
                            row_sums(b + 1, 0, st)
                            st.close()
                    blocks(dve, body)

        def deviations(tag):
            ph = ExitStack()
            with ph:
                tmp = ph.enter_context(nc.sbuf_tensor(tag + "tmp", [P, NT], F32))
                added = ctx.enter_context(nc.semaphore(tag + "added"))
                rooted = ctx.enter_context(nc.semaphore(tag + "rooted"))
                block = ph.enter_context(nc.Block())

                @block.vector
                def _(dve):
                    dve.tensor_scalar(tmp[:], mv1[:, :, 1], EPS, None, ALU.add).then_inc(added, 1)
                    dve.wait_ge(rooted, 1)
                    dve.reciprocal(rstd[:], tmp[:])

                @block.scalar
                def _(act):
                    act.wait_ge(added, 1)
                    act.activation(tmp[:], tmp[:], ACT.Sqrt).then_inc(rooted, 1)

        def attention2():
            ph = ExitStack()
            with ph:
                def sb(name, shape, dt=F32):
                    return ph.enter_context(nc.sbuf_tensor("a2_" + name, shape, dt))

                def sem(name):
                    return ctx.enter_context(nc.semaphore("a2_" + name))

                held = 0

                def piece(n):
                    nonlocal held
                    held += n
                    return up_flat[:, held - n:held]
                wq = piece(C * H2 * DH2).rearrange("p (c n) -> p c n", c=C)
                wkv = sb("wkv", [P, C, 2 * DH2])
                wkk = sb("wkk", [P, C, 2, DH2])
                wo = piece(J2 * D).rearrange("p (j n) -> p j n", j=J2)
                gin = sb("gin", [P, C])
                bias = piece(2 * J2 * KN).rearrange("p (h j k) -> p h j k", h=2, j=J2)
                mask8 = sb("mask8", [P, NT, S], U8)
                madd = piece(NT * KN).rearrange("p (t k) -> p t k", t=NT)
                bm = piece(4 * J2 * KN).rearrange("p (w h j k) -> p w h j k", w=2, h=2, j=J2)
                xb = piece(TPB * D).rearrange("p (t d) -> p t d", t=TPB)
                xT_ = piece(C * BT).rearrange("p (c t) -> p c t", c=C)
                q = piece(J2 * BT).rearrange("p (j t) -> p j t", j=J2)
                k = piece(SPB * KN).rearrange("p (s k) -> p s k", s=SPB)
                v = sb("v", [P, SPB, DH2])
                sc = sb("sc", [P, 2, 2, 4, KN])
                mx = sb("mx", [P, 2, 8])
                rs = sb("rs", [P, 2, 8])
                pT = sb("pT", [KN, 2, 2, 4, P])
                oT = sb("oT", [P, J2, P])
                bst = sb("bst", [P, 6])
                mvb = sb("mvb", [P, TPB, 2])
                wo_in, wkv_in = sem("wo_in"), sem("wkv_in")
                w_in, small_in, bias_in, mask_in, bias2_in = (
                    sem(n) for n in ("w_in", "small_in", "bias_in", "mask_in", "bias2_in"))
                causal, madd_ready, kk_ready, null_ready = (
                    sem(n) for n in ("causal", "madd_ready", "kk_ready", "null_ready"))
                xb_ready, xT_ps, xT_act, xT_dve, q_ps, q_act, q_dve = (
                    sem(n) for n in ("xb_ready", "xT_ps", "xT_act", "xT_dve", "q_ps", "q_act", "q_dve"))
                kv_ps, k_sb, v_sb, bm_ready, s_ps, s_sh, s_add, e_ready, r_ready, p_ready = (
                    sem(n) for n in ("kv_ps", "k_sb", "v_sb", "bm_ready", "s_ps", "s_sh", "s_add", "e_ready",
                                     "r_ready", "p_ready"))
                pT_ps, pT_sb, o_ps, oT_sb, yo_ps, tile_done, dve_step = (
                    sem(n) for n in ("pT_ps", "pT_sb", "o_ps", "oT_sb", "yo_ps", "tile_done", "dve_step"))
                goutb = sb("goutb", [P, D])
                rw = sb("rw", [P, C, E2])
                cb = sb("cb", [P, E2])
                before = sb("before", [P, P])
                ones = sb("ones", [P, P])
                ids_i = sb("ids_i", [P, NT, K2], I32)
                ids = sb("ids", [P, NT, K2])
                r_ = sb("r_", [P, 2, BT])
                sd = sb("sd", [P, TPB])
                GR = TPB * GROUPS
                score = sb("score", [P, TPB, E2])
                sfc = sb("sfc", [P, TPB, E2])
                left = sb("left", [P, TPB, E2])
                sel = sb("sel", [P, TPB, E2])
                hi, lo = sb("hi", [P, GR, 4]), sb("lo", [P, GR, 4])
                hi2, lo2, t2 = (sb(n, [P, GR, 2]) for n in ("hi2", "lo2", "t2"))
                gs, gl = sb("gs", [P, TPB, GROUPS]), sb("gl", [P, TPB, GROUPS])
                top8 = sb("top8", [P, TPB, 8])
                stat = sb("stat", [P, TPB])
                free = sb("free", [P, E2])
                nxt = sb("nxt", [P, E2])
                used = sb("used", [P, 1])
                late = sb("late", [P, TPB, E2])
                jump = sb("jump", [P, E2])
                grew = sb("grew", [P, E2])
                first = sb("first", [P, E2])
                fresh = sb("fresh", [P, 3])
                now = sb("now", [P, 3])
                sv = sb("sv", [P, TPB, E2])
                top8s = sb("top8s", [P, TPB, K2])
                sidx = sb("sidx", [P, TPB, K2], I32)
                blk_i = sb("blk_i", [P, 3], I32)
                blk = sb("blk", [P, 3])
                nb_i = sb("nb_i", [P, E2], I32)
                nb = sb("nb", [P, E2])
                end = sb("end", [P, E2])
                ones64 = sb("ones64", [P, E2])
                le = sb("le", [P, 3, E2])
                be = sb("be", [P, 3])
                be_i = sb("be_i", [P, 3], I32)
                at = 0

                def part(n):
                    nonlocal at
                    at += n
                    return wide[:, at - n:at]
                z = part(TPB * D).rearrange("p (t d) -> p t d", t=TPB)
                h_ = part(SH2 * BT).rearrange("p (i n) -> p i n", i=SH2)
                att = part(TPB * D).rearrange("p (t d) -> p t d", t=TPB)
                junk = part(K2 * E2).rearrange("p (k e) -> p k e", k=K2)
                w_su = part(SH2 * C * M2).rearrange("p (i c m) -> p i c m", i=SH2, c=C)
                w_sd = part(SH2 * D).rearrange("p (i d) -> p i d", i=SH2)
                zT = part(C * BT).rearrange("p (c t) -> p c t", c=C)
                ranked = part((TPB + 1) * E2)
                assert at >= EARLY * D
                stage = part(TPB * K2 * ROW).rearrange("p (t k r) -> p t k r", t=TPB, k=K2)
                route_in, made, init, eps_added, rooted, zc_ready, z_ready, zT_ps, zT_act, zT_dve = (
                    sem(n) for n in ("route_in", "made", "init", "eps_added", "rooted", "zc_ready", "z_ready",
                                     "zT_ps", "zT_act", "zT_dve"))
                l_ps, score_ready, sel_ready, rank_ps, rank_read = (
                    sem(n) for n in ("l_ps", "score_ready", "sel_ready", "rank_ps", "rank_read"))
                sz_ps, relu_ready, h_ready, sy_ps, sy_done, z_staged, w_staged, tables, tables_out, route_step = (
                    sem(n) for n in ("sz_ps", "relu_ready", "h_ready", "sy_ps", "sy_done", "z_staged", "w_staged",
                                     "tables", "tables_out", "route_step"))
                sent = [sem(f"sent{t}") for t in range(TPB)]
                FILLS = 5

                def steps(eng, body, last):
                    for b in range(3):
                        body(b, b - 1 if b > 0 else None, b - 2 if b > 1 else None, False)
                    with eng.Fori(3, NB - 1) as b:
                        body(b, b - 1, b - 2, False)
                    body(NB - 1, NB - 2, NB - 3, True)
                    last()

                HB = 2 * TPB
                block = ph.enter_context(nc.Block())

                @block.sync
                def _(sp):
                    sp.dma_start(gin[:], g_in).then_inc(small_in, 16)
                    sp.dma_start(wkv[:], wkv2.rearrange("(c p) n -> p c n", p=P)).then_inc(wkv_in, 16)
                    for h in range(2):
                        sp.dma_start(bias[0:S, h, :, 0:S],
                                     bias2.rearrange("(j h) q k -> h q j k", h=2)[h]).then_inc(bias_in, 16)
                    for s in range(2):
                        for h in range(2):
                            sp.dma_start(bias[s * S:(s + 1) * S, h, :, S:KN],
                                         nbias.rearrange("(j h) -> h j", h=2)[h:h + 1].unsqueeze(2)
                                         .to_broadcast([S, J2, 1])).then_inc(bias2_in, 16)
                    for s in range(2):
                        sp.dma_start(mask8[s * S:(s + 1) * S],
                                     mask.rearrange("(t s) k -> s t k", s=2)[s:s + 1]
                                     .to_broadcast([S, NT, S])).then_inc(mask_in, 16)
                    for h in range(2):
                        sp.dma_start(k[h * DH2:(h + 1) * DH2, :, S:KN],
                                     cond[0, :].rearrange("(d o) -> d o", o=1).unsqueeze(1)
                                     .to_broadcast([DH2, SPB, 1])).then_inc(null_ready, 16)
                    sp.dma_start(v[S:KN, :, :], cond[1:2, :].unsqueeze(1).to_broadcast([1, SPB, DH2])
                                 ).then_inc(null_ready, 16)
                    sp.dma_start(wq, wq2.rearrange("(c p) n -> p c n", p=P)).then_inc(w_in, 16)
                    sp.dma_start(wo, wo2.rearrange("(j p) n -> p j n", p=P)).then_inc(wo_in, 16)
                    sp.dma_start(goutb[:], g_row.to_broadcast([P, D])).then_inc(route_in, 16)
                    sp.dma_start(cb[:], cbias.rearrange("(o e) -> o e", o=1).to_broadcast([P, E2])).then_inc(route_in, 16)
                    sp.dma_start(w_su, up2s).then_inc(route_in, 16)
                    sp.dma_start(w_sd, down2s).then_inc(route_in, 16)
                    sp.dma_start(rw[:], rwT.rearrange("(c p) e -> p c e", p=P)).then_inc(route_in, 16)
                    sp.wait_ge(tile_done, NT)
                    sp.dma_start(w_up, up2).then_inc(w_res, 16)
                    sp.wait_ge(z_staged, NT)
                    sp.wait_ge(w_staged, NT)
                    sp.wait_ge(sy_done, NB * 2)
                    sp.dma_start(w_dn[:, 0:EARLY], down2[:, 0:EARLY]).then_inc(wd_in, 16)
                    sp.wait_ge(tables, 1)
                    sp.dma_start(block_expert.rearrange("(c p) -> p c", p=P).unsqueeze(2), be_i[:].unsqueeze(2)
                                 ).then_inc(tables_out, 16)
                    sp.wait_ge(tables_out, 16)

                @block.gpsimd
                def _(pool):
                    pool.memset(before[:], 1.0).then_inc(made, 1)
                    pool.wait_ge(made, 1)
                    pool.affine_select(out=before[:], in_=before[:], compare_op=ALU.is_gt, fill=0.0, base=0,
                                       pattern=[[1, P]], channel_multiplier=-1).then_inc(made, 1)
                    pool.memset(ones[:], 1.0).then_inc(made, 1)
                    pool.iota(ids_i[:], pattern=[[-P * K2, NT], [-1, K2]], base=T * K2, channel_multiplier=-K2
                              ).then_inc(made, 1)
                    pool.iota(blk_i[:], pattern=[[P, 3]], base=0, channel_multiplier=1).then_inc(made, 1)
                    pool.wait_ge(bias_in, 32)
                    for h in range(2):
                        pool.affine_select(out=bias[0:S, h, :, 0:S], in_=bias[0:S, h, :, 0:S], compare_op=ALU.is_ge,
                                           fill=MASKED, base=0, pattern=[[0, J2], [-1, S]], channel_multiplier=1
                                           ).then_inc(causal, 1)
                    pool.wait_ge(causal, 3)
                    pool.wait_ge(bias2_in, 64)
                    pool.wait_ge(madd_ready, 1)

                    def bias_mask(n, w):
                        wait(pool, s_add, 2 * (n - 1))
                        pool.tensor_tensor(bm[:, w].rearrange("p h j k -> p (h j) k"),
                                           bias.rearrange("p h j k -> p (h j) k"),
                                           madd[:, bass.ds(n, 1), :].to_broadcast([P, H2, KN]),
                                           ALU.add).then_inc(bm_ready, 1)

                    def normalize(m, g):
                        pool.wait_ge(r_ready, m + 1)
                        p_ = sc[:, g].rearrange("p h j k -> p (h j) k")
                        pool.tensor_tensor(p_, p_, rs[:, g].unsqueeze(2).to_broadcast([P, 8, KN]),
                                           ALU.mult).then_inc(p_ready, 1)

                    def send(q, i):
                        t = i // 2
                        if i % 2 == 0:
                            pool.wait_ge(w_staged, q * TPB + t + 1)
                            pool.wait_ge(z_staged, q * TPB + t + 1)
                            pool.nop(nofuse=True)
                        for k_ in range(K2 // 2 * (i % 2), K2 // 2 * (i % 2 + 1)):
                            pool.indirect_dma_start(
                                out=x_slots, out_offset=bass.IndirectOffsetOnAxis(ap=sidx[:, t, k_:k_ + 1], axis=0),
                                in_=stage[:, t, k_, :], in_offset=None).then_inc(sent[t], 16)

                    bias_mask(0, 0)
                    normalize(0, 0)
                    bias_mask(1, 1)

                    def body(b, r, q, final):
                        for i in range(HB):
                            if i + 1 < HB:
                                normalize(b * HB + i + 1, (i + 1) % 2)
                                if i % 2 == 1 and not (final and (i + 3) // 2 == TPB):
                                    bias_mask(b * TPB + (i + 3) // 2, (i + 3) // 2 % 2)
                            if q is not None:
                                send(q, i)
                        if not final:
                            normalize((b + 1) * HB, 0)
                            bias_mask((b + 1) * TPB + 1, 1)

                    def last():
                        for q in (NB - 2, NB - 1):
                            for i in range(HB):
                                send(q, i)
                        for t in range(TPB):
                            pool.wait_ge(sent[t], NB * 16 * K2)
                    steps(pool, body, last)

                @block.tensor
                def _(pe):
                    Q_BANK = (2, 3, 4, 5, 6, 7, 4, 5)

                    def scores(b, i):
                        m, t, g = b * HB + i, i // 2, i % 2
                        if i >= 1:
                            pe.wait_ge(s_add, m)
                        if i < 2:
                            pe.wait_ge(q_act, b * 4 + 2 + 2 * i)
                            pe.wait_ge(q_dve, b * 4 + 2 + 2 * i)
                        pe.nop(nofuse=True)
                        for jj in range(4):
                            j = 4 * g + jj
                            for s in range(2):
                                for h in range(2):
                                    last = pe.matmul(
                                        ps[s * S:(s + 1) * S, 2 + h, jj * P:jj * P + KN],
                                        q[h * DH2:(h + 1) * DH2, j, t * P + s * S:t * P + (s + 1) * S],
                                        k[h * DH2:(h + 1) * DH2, 2 * t + s, :], start=True, stop=True)
                        last.then_inc(s_ps, 1)

                    def transpose_x(b):
                        pe.wait_ge(xb_ready, b + 1)
                        wait(pe, s_add, b * HB)
                        for c in range(C):
                            for t in range(TPB):
                                last = pe.transpose(ps[:, 2 + c, t * P:(t + 1) * P], xb[:, t, c * P:(c + 1) * P],
                                                    ident[:])
                        last.then_inc(xT_ps, 1)

                    def keys_values(b):
                        pe.wait_ge(xT_act, b + 1)
                        pe.wait_ge(xT_dve, b + 1)
                        wait(pe, pT_sb, b * HB)
                        for c in range(C):
                            pe.matmul(ps[:, 6, :], wkk[:, c].rearrange("p a d -> p (a d)"), xT_[:, c, :],
                                      start=(c == 0), stop=(c == C - 1))
                        for t in range(TPB):
                            for c in range(C):
                                last = pe.matmul(ps[:, 7, t * DH2:(t + 1) * DH2], xT_[:, c, t * P:(t + 1) * P],
                                                 wkv[:, c, DH2:2 * DH2], start=(c == 0), stop=(c == C - 1))
                        last.then_inc(kv_ps, 1)

                    def queries(b, r):
                        for j in range(J2):
                            if j in (2, 3) and r is not None:
                                pe.wait_ge(sy_done, r * 2 + j - 1)
                            elif j == 4:
                                pe.wait_ge(k_sb, b + 1)
                            elif j == 5:
                                pe.wait_ge(v_sb, b * 2 + 2)
                            elif j >= 6:
                                pe.wait_ge(q_act if j % 2 == 0 else q_dve, b * 4 + 2)
                            for c in range(C):
                                last = pe.matmul(ps[:, Q_BANK[j], :], wq[:, c, j * P:(j + 1) * P], xT_[:, c, :],
                                                 start=(c == 0), stop=(c == C - 1))
                            last.then_inc(q_ps, 1)

                    def transpose_p(b, i):
                        m, g = b * HB + i, i % 2
                        pe.wait_ge(p_ready, m + 1)
                        wait(pe, pT_sb, m)
                        for h in range(2):
                            for jj in range(4):
                                last = pe.transpose(ps[0:KN, 6 + h, jj * P:(jj + 1) * P], sc[:, g, h, jj, :], ident[:])
                        last.then_inc(pT_ps, 1)

                    def outputs(b, i):
                        m, t = b * HB + i, i // 2
                        pe.wait_ge(pT_sb, m + 1)
                        wait(pe, oT_sb, m)
                        for s in range(2):
                            for h in range(2):
                                last = pe.matmul(
                                    ps[h * DH2:(h + 1) * DH2, 0, :].rearrange(
                                        "p (j s q) -> p j s q", j=4, s=2)[:, :, s, :],
                                    v[0:KN, 2 * t + s, :], pT[:, i % 2, h, :, s * S:(s + 1) * S],
                                    start=True, stop=True)
                        last.then_inc(o_ps, 1)

                    def project(b, t):
                        n = b * TPB + t
                        pe.wait_ge(oT_sb, 2 * n + 2)
                        wait(pe, tile_done, n)
                        for j in range(J2):
                            last = pe.matmul(ps[:, 1, 0:D], oT[:, j, :], wo[:, j, :],
                                             start=(j == 0), stop=(j == J2 - 1))
                        last.then_inc(yo_ps, 1)

                    def z_features(r):
                        pe.wait_ge(z_ready, r + 1)
                        for c in range(C):
                            for t in range(TPB):
                                last = pe.transpose(ps[:, 4 + c, t * P:(t + 1) * P], z[:, t, c * P:(c + 1) * P], ident[:])
                        last.then_inc(zT_ps, 1)

                    def logits(r):
                        pe.wait_ge(zT_act, r + 1)
                        pe.wait_ge(zT_dve, r + 1)
                        for t in range(TPB):
                            for c in range(C):
                                last = pe.matmul(ps[:, 4, t * E2:(t + 1) * E2], zT[:, c, t * P:(t + 1) * P], rw[:, c, :],
                                                 start=(c == 0), stop=(c == C - 1))
                        last.then_inc(l_ps, 1)

                    def shared_up(r, i):
                        if i == 1:
                            pe.wait_ge(score_ready, r + 1)
                        elif i > 1:
                            pe.wait_ge(relu_ready, r * SH2 + i - 1)
                        for c in range(C):
                            last = pe.matmul(ps[:, 5 - i % 2, :], w_su[:, i, c, :], zT[:, c, :],
                                             start=(c == 0), stop=(c == C - 1))
                        last.then_inc(sz_ps, 1)

                    def ranks(r):
                        pe.wait_ge(sel_ready, r + 1)
                        pe.wait_ge(h_ready, r * SH2 + 3)
                        for t in range(TPB + 1):
                            for i in range(min(t + 1, TPB)):
                                last = pe.matmul(ps[:, 5, t * E2:(t + 1) * E2], before[:] if i == t else ones[:],
                                                 sel[:, i, :], start=(i == 0), stop=(i == min(t, TPB - 1)))
                        last.then_inc(rank_ps, 1)

                    def shared_down(r, half):
                        if half == 0:
                            pe.wait_ge(h_ready, r * SH2 + SH2)
                        else:
                            pe.wait_ge(rank_read, r + 1)
                        for a in range(2):
                            t = 2 * half + a
                            for i in range(SH2):
                                last = pe.matmul(ps[:, 4 + half, a * D:(a + 1) * D], h_[:, i, t * P:(t + 1) * P],
                                                 w_sd[:, i, :], start=(i == 0), stop=(i == SH2 - 1))
                        last.then_inc(sy_ps, 1)

                    def route_piece(r, i):
                        if i == 1:
                            z_features(r)
                        elif i == 2:
                            logits(r)
                            shared_up(r, 0)
                        elif i == 3:
                            shared_up(r, 1)
                            shared_up(r, 2)
                        elif i == 4:
                            shared_up(r, 3)
                        elif i == 5:
                            ranks(r)
                            shared_down(r, 0)
                        elif i == 7:
                            shared_down(r, 1)

                    transpose_x(0)
                    pe.wait_ge(kk_ready, 1)
                    keys_values(0)
                    pe.wait_ge(w_in, 16)
                    pe.wait_ge(null_ready, 48)
                    queries(0, None)
                    scores(0, 0)
                    scores(0, 1)

                    def body(b, r, q_, final):
                        if isinstance(b, int) and b == 0:
                            pe.wait_ge(wo_in, 16)
                        if isinstance(b, int) and b == 1:
                            pe.wait_ge(route_in, FILLS * 16)
                            pe.wait_ge(made, 5)
                        for i in range(HB):
                            transpose_p(b, i)
                            if i > 0:
                                outputs(b, i - 1)
                            if i + 2 < HB:
                                scores(b, i + 2)
                            elif i + 2 == HB and not final:
                                transpose_x(b + 1)
                            if i % 2 == 0 and i > 0:
                                project(b, i // 2 - 1)
                            if r is not None:
                                route_piece(r, i)
                            if i + 1 == HB and not final:
                                keys_values(b + 1)
                        outputs(b, HB - 1)
                        if not final:
                            queries(b + 1, r)
                            scores(b + 1, 0)
                        project(b, TPB - 1)
                        if not final:
                            scores(b + 1, 1)

                    def last():
                        pe.wait_ge(sy_done, 2 * (NB - 1))
                        for i in range(HB):
                            route_piece(NB - 1, i)
                    steps(pe, body, last)

                @block.scalar
                def _(act):
                    act.wait_ge(causal, 2)
                    act.copy(bias[S:P, :, :, 0:S].rearrange("p h j k -> p (h j) k"),
                             bias[0:S, :, :, 0:S].rearrange("p h j k -> p (h j) k")).then_inc(causal, 1)
                    act.wait_ge(wkv_in, 16)
                    for h in range(2):
                        last = act.copy(wkk[:, :, h, :], wkv[:, :, 0:DH2])
                    last.then_inc(kk_ready, 1)
                    act.wait_ge(small_in, 16)

                    def features_0(b):
                        act.wait_ge(xT_ps, b + 1)
                        act.activation(xT_[:, 0, :], ps[:, 2, :], ACT.Copy, scale=gin[:, 0:1]).then_inc(xT_act, 1)

                    def keys_and_queries(b):
                        act.wait_ge(kv_ps, b + 1)
                        act.copy(k[:, :, 0:S], ps[:, 6, :].rearrange("p (s k) -> p s k", s=SPB)).then_inc(k_sb, 1)
                        for j in range(0, J2, 2):
                            act.wait_ge(q_ps, b * J2 + j + 1)
                            act.activation(q[:, j, :], ps[:, (2, 4, 6, 4)[j // 2], :], ACT.Copy, scale=DH2 ** -0.5
                                           ).then_inc(q_act, 1)

                    def exponential(b, i):
                        act.wait_ge(s_sh, b * HB + i + 1)
                        act.activation(sc[:, i % 2], sc[:, i % 2], ACT.Exp).then_inc(e_ready, 1)

                    def transposed(b, i):
                        m = b * HB + i
                        act.wait_ge(pT_ps, m + 1)
                        wait(act, o_ps, m - 1)
                        act.copy(pT[:, i % 2].rearrange("p h j q -> p (h j q)"),
                                 ps[0:KN, 6:8, :].rearrange("p a b -> p (a b)")).then_inc(pT_sb, 1)

                    def root(r):
                        act.wait_ge(eps_added, r + 1)
                        act.activation(sd[:], sd[:], ACT.Sqrt).then_inc(rooted, 1)

                    def scale_z(r):
                        act.wait_ge(zc_ready, r + 1)
                        for t in range(TPB):
                            last = act.activation(z[:, t, :], z[:, t, :], ACT.Copy, scale=sd[:, t:t + 1])
                        last.then_inc(z_ready, 1)

                    def z_features_0(r):
                        act.wait_ge(zT_ps, r + 1)
                        wait(act, sz_ps, r * SH2)
                        act.copy(zT[:, 0, :], ps[:, 4, :]).then_inc(zT_act, 1)

                    def exp_logits(r):
                        act.wait_ge(l_ps, r + 1)
                        wait(act, w_staged, r * TPB)
                        act.activation(score[:], ps[:, 4, 0:TPB * E2].rearrange("p (t e) -> p t e", t=TPB), ACT.Exp,
                                       scale=-1.0).then_inc(score_ready, 1)

                    def square(r, i):
                        n = r * SH2 + i
                        act.wait_ge(sz_ps, n + 1)
                        if i == 0:
                            wait(act, sy_ps, r * 2)
                        act.activation(r_[:, i % 2, :], ps[:, 5 - i % 2, :], ACT.Relu).then_inc(relu_ready, 1)
                        act.wait_ge(relu_ready, n + 1)
                        act.activation(h_[:, i, :], r_[:, i % 2, :], ACT.Square).then_inc(h_ready, 1)

                    def stage_z(r, t):
                        wait(act, sent[t], r * 16 * K2)
                        act.copy(stage[:, t, :, 0:D], z[:, t, :].unsqueeze(1).to_broadcast([P, K2, D])
                                 ).then_inc(z_staged, 1)

                    def early_piece(r, i):
                        if i == 1:
                            scale_z(r)
                        elif i == 2:
                            z_features_0(r)
                        elif i == 3:
                            exp_logits(r)
                        elif i == 4:
                            square(r, 1)
                        elif i == 5:
                            square(r, 3)

                    def late_piece(r, i):
                        if i == 3:
                            square(r, 0)
                            stage_z(r, 0)
                        elif i == 4:
                            square(r, 2)
                        elif i == 5:
                            stage_z(r, 1)
                        elif i == 7:
                            stage_z(r, 2)

                    features_0(0)
                    keys_and_queries(0)
                    exponential(0, 0)

                    def body(b, r, q_, final):
                        for i in range(HB):
                            if i + 1 < HB:
                                exponential(b, i + 1)
                            transposed(b, i)
                            if r is not None:
                                early_piece(r, i)
                            if i + 2 == HB and not final:
                                features_0(b + 1)
                            if r is not None:
                                late_piece(r, i)
                        if not final:
                            keys_and_queries(b + 1)
                        if r is not None:
                            stage_z(r, TPB - 1)
                        if not final:
                            exponential(b + 1, 0)
                        root(b)

                    def last():
                        for i in range(HB):
                            early_piece(NB - 1, i)
                            late_piece(NB - 1, i)
                        stage_z(NB - 1, TPB - 1)
                    steps(act, body, last)

                @block.vector
                def _(dve):
                    dve.wait_ge(mask_in, 32)
                    dve.memset(madd[:, :, S:KN], 0.0)
                    dve.tensor_scalar(madd[:, :, 0:S], mask8[:], 1.0, -MASKED, ALU.subtract, ALU.mult
                                      ).then_inc(madd_ready, 1)
                    dve.wait_ge(small_in, 16)
                    PER, AHEAD = TPB * 5, 2

                    def normalized(b):
                        wait(dve, xT_ps, b)
                        for t in range(TPB):
                            n = b * TPB + t
                            last = dve.tensor_scalar(xb[:, t, :], acc[:, bass.ds(n, 1), :].rearrange("p o d -> p (o d)"),
                                                     mv1[:, bass.ds(n, 1), 0], rstd[:, bass.ds(n, 1)],
                                                     ALU.subtract, ALU.mult)
                        last.then_inc(xb_ready, 1)

                    def features_1(b):
                        dve.wait_ge(xT_ps, b + 1)
                        dve.tensor_scalar(xT_[:, 1, :], ps[:, 3, :], gin[:, 1:2], None, ALU.mult).then_inc(xT_dve, 1)

                    def values_and_queries(b):
                        dve.wait_ge(kv_ps, b + 1)
                        for s in range(2):
                            dve.tensor_copy(v[0:S, :, :].rearrange("p (t s) d -> p t s d", s=2)[:, :, s, :],
                                            ps[s * S:(s + 1) * S, 7, 0:TPB * DH2].rearrange("p (t d) -> p t d", t=TPB)
                                            ).then_inc(v_sb, 1)
                        for j in range(1, J2, 2):
                            dve.wait_ge(q_ps, b * J2 + j + 1)
                            dve.tensor_scalar(q[:, j, :], ps[:, (3, 5, 7, 5)[j // 2], :], DH2 ** -0.5, None, ALU.mult
                                              ).then_inc(q_dve, 1)

                    def shift(b, i, st):
                        m, n, g = b * HB + i, b * TPB + i // 2, i % 2
                        dve.wait_ge(s_ps, m + 1)
                        dve.wait_ge(bm_ready, n + 1)
                        wait(dve, pT_ps, m - 1)
                        dve.tensor_tensor(sc[:, g], ps[:, 2:4, :].rearrange(
                            "p h (j k) -> p h j k", j=4)[:, :, :, 0:KN], bm[:, i // 2 % 2, :, 4 * g:4 * g + 4, :],
                            ALU.add).then_inc(s_add, 1)
                        dve.wait_ge(s_add, m + 1)
                        s_ = sc[:, g].rearrange("p h j k -> p (h j) k")
                        st.done(dve.tensor_reduce(mx[:, g], s_, AX.X, ALU.max))
                        dve.tensor_tensor(s_, s_, mx[:, g].unsqueeze(2).to_broadcast([P, 8, KN]), ALU.subtract
                                          ).then_inc(s_sh, 1)

                    def row_sums(b, i, st):
                        g = i % 2
                        dve.wait_ge(e_ready, b * HB + i + 1)
                        st.done(dve.tensor_reduce(rs[:, g], sc[:, g].rearrange("p h j k -> p (h j) k"), AX.X, ALU.add))
                        dve.reciprocal(rs[:, g], rs[:, g]).then_inc(r_ready, 1)

                    def output(b, i):
                        g = i % 2
                        dve.wait_ge(o_ps, b * HB + i + 1)
                        wait(dve, yo_ps, b * TPB + i // 2)
                        dve.tensor_copy(oT[:, 4 * g:4 * g + 4, :].rearrange("p j q -> p (j q)"), ps[:, 0, :]
                                        ).then_inc(oT_sb, 1)

                    def projected(b, t, st):
                        n = b * TPB + t
                        dve.wait_ge(yo_ps, n + 1)
                        if t == 0:
                            wait(dve, zc_ready, b)
                            dve.nop(nofuse=True)
                        dve.tensor_copy(att[:, t, :], ps[:, 1, 0:D])
                        st.done(dve.bn_stats(bst[:], ps[:, 1, 0:D]))
                        dve.nop(nofuse=True)
                        dve.bn_aggr(mvb[:, t, :], bst[:]).then_inc(tile_done, 1)
                        if t + 1 == TPB:
                            dve.wait_ge(tile_done, n + 1)
                            wait(dve, z_ready, b)
                            dve.tensor_scalar(sd[:], mvb[:, :, 1], EPS, None, ALU.add).then_inc(eps_added, 1)

                    ROUTE = 43

                    def center_z(r):
                        dve.wait_ge(rooted, r + 1)
                        dve.reciprocal(sd[:], sd[:])
                        wait(dve, z_staged, r * TPB)
                        for t in range(TPB):
                            last = dve.scalar_tensor_tensor(z[:, t, :], att[:, t, :], mvb[:, t, 0:1], goutb[:],
                                                            ALU.subtract, ALU.mult)
                        last.then_inc(zc_ready, 1)

                    def z_features_1(r):
                        dve.wait_ge(zT_ps, r + 1)
                        dve.tensor_copy(zT[:, 1, :], ps[:, 5, :]).then_inc(zT_dve, 1)

                    def scores_of(r, st):
                        dve.wait_ge(score_ready, r + 1)
                        st.done(dve.tensor_scalar(score[:], score[:], 1.0, None, ALU.add))
                        st.done(dve.reciprocal(score[:], score[:]))
                        st.done(dve.tensor_tensor(sfc[:], score[:], cb[:].unsqueeze(1).to_broadcast([P, TPB, E2]), ALU.add))
                        grp = sfc[:].rearrange("p t (g e) -> p (t g) e", g=GROUPS)
                        dve.tensor_tensor(hi[:], grp[:, :, 0:4], grp[:, :, 4:8], ALU.max)
                        st.done(dve.tensor_tensor(lo[:], grp[:, :, 0:4], grp[:, :, 4:8], ALU.min))

                        def merge(h_, l_, h_out, l_out, tmp, n):
                            dve.tensor_tensor(h_out, h_[:, :, 0:n], h_[:, :, n:2 * n], ALU.max)
                            dve.tensor_tensor(tmp, h_[:, :, 0:n], h_[:, :, n:2 * n], ALU.min)
                            st.done(dve.tensor_tensor(l_out, l_[:, :, 0:n], l_[:, :, n:2 * n], ALU.max))
                            st.done(dve.tensor_tensor(l_out, l_out, tmp, ALU.max))
                        merge(hi[:], lo[:], hi2[:], lo2[:], t2[:], 2)
                        merge(hi2[:], lo2[:], hi[:, :, 0:1], lo[:, :, 0:1], t2[:, :, 0:1], 1)
                        st.done(dve.tensor_tensor(gs[:].rearrange("p t (g o) -> p (t g) o", o=1), hi[:, :, 0:1],
                                                  lo[:, :, 0:1], ALU.add))

                    def choose(r, st):
                        grp = sfc[:].rearrange("p t (g e) -> p (t g) e", g=GROUPS)
                        dve.nop(nofuse=True)
                        for t in range(TPB):
                            last = dve.max(top8[:, t, :], gs[:, t, :])
                        st.done(last)
                        st.done(dve.memset(top8[:, :, TOPG:8], UNMATCHED))
                        dve.nop(nofuse=True)
                        for t in range(TPB):
                            last = dve.match_replace(gl[:, t, :], top8[:, t, :], gs[:, t, :], TAKEN)
                        st.done(last)
                        st.done(dve.tensor_scalar(gl[:], gl[:], TAKEN, None, ALU.is_equal))
                        st.done(dve.tensor_tensor(grp, grp, gl[:].rearrange("p t g -> p (t g)").unsqueeze(2)
                                                  .to_broadcast([P, GR, 8]), ALU.mult))
                        dve.nop(nofuse=True)
                        for t in range(TPB):
                            last = dve.max(top8[:, t, :], sfc[:, t, :])
                        st.done(last)
                        dve.nop(nofuse=True)
                        for t in range(TPB):
                            last = dve.match_replace(left[:, t, :], top8[:, t, :], sfc[:, t, :], TAKEN)
                        st.done(last)
                        dve.tensor_scalar(sel[:], left[:], TAKEN, None, ALU.is_equal).then_inc(sel_ready, 1)
                        dve.wait_ge(sel_ready, r + 1)

                    def weigh(r, st):
                        st.done(dve.tensor_tensor(score[:], score[:], sel[:], ALU.mult))
                        st.done(dve.tensor_reduce(stat[:], score[:], AX.X, ALU.add))
                        st.done(dve.tensor_scalar(stat[:], stat[:], 1e-20, None, ALU.add))
                        st.done(dve.reciprocal(stat[:], stat[:]))
                        st.done(dve.tensor_scalar(stat[:], stat[:], ROUTE_SCALE, None, ALU.mult))
                        st.done(dve.tensor_tensor(score[:], score[:], stat[:].unsqueeze(2).to_broadcast([P, TPB, E2]),
                                                  ALU.mult))

                    def add_shared(b, half):
                        dve.wait_ge(sy_ps, b * 2 + half + 1)
                        dve.nop(nofuse=True)
                        a_ = acc[:, bass.ds(b * TPB + 2 * half, 2), :].rearrange("p t d -> p (t d)")
                        dve.tensor_tensor(a_, ps[:, 4 + half, :], a_, ALU.add).then_inc(sy_done, 1)

                    def slots(r, st):
                        dve.wait_ge(rank_ps, r + 1)
                        dve.tensor_copy(ranked, ps[:, 5, 0:(TPB + 1) * E2]).then_inc(rank_read, 1)
                        dve.wait_ge(rank_read, r + 1)
                        rank = ranked[:, 0:TPB * E2].rearrange("p (t e) -> p t e", e=E2)
                        tot = ranked[:, TPB * E2:(TPB + 1) * E2]

                        def over(ap, shape):
                            return ap.unsqueeze(1).to_broadcast(shape)
                        st.done(dve.tensor_tensor(grew[:], tot, free[:], ALU.subtract))
                        st.done(dve.tensor_scalar(nb_i[:], grew[:], float(P - 1), 0.0, ALU.add, ALU.max))
                        st.done(dve.tensor_scalar(nb_i[:], nb_i[:], 7, None, ALU.logical_shift_right))
                        st.done(dve.tensor_copy(nb[:], nb_i[:]))
                        st.done(dve.tensor_tensor_scan(end[:], ones64[:], nb[:], used[:], ALU.mult, ALU.add))
                        st.done(dve.tensor_tensor(first[:], end[:], nb[:], ALU.subtract))
                        dve.tensor_tensor(jump[:], free[:], nxt[:], ALU.add)
                        st.done(dve.tensor_scalar(first[:], first[:], float(P), 1.0, ALU.mult, ALU.add))
                        st.done(dve.tensor_tensor(jump[:], first[:], jump[:], ALU.subtract))
                        st.done(dve.tensor_tensor(late[:], rank, over(free[:], [P, TPB, E2]), ALU.is_ge))
                        dve.tensor_tensor(sv[:], rank, over(nxt[:], [P, TPB, E2]), ALU.add)
                        st.done(dve.tensor_tensor(late[:], late[:], over(jump[:], [P, TPB, E2]), ALU.mult))
                        st.done(dve.tensor_tensor(sv[:], sv[:], late[:], ALU.add))
                        dve.tensor_tensor(le[:], over(end[:], [P, 3, E2]), blk[:].unsqueeze(2).to_broadcast([P, 3, E2]),
                                          ALU.is_le)
                        st.done(dve.tensor_tensor(fresh[:], blk[:], used[:].to_broadcast([P, 3]), ALU.is_ge))
                        st.done(dve.tensor_reduce(now[:], le[:], AX.X, ALU.add))
                        st.done(dve.scalar_tensor_tensor(now[:], now[:], float(E2 - 1), fresh[:], ALU.min, ALU.mult))
                        dve.tensor_tensor(sv[:], sv[:], sel[:], ALU.mult)
                        st.done(dve.tensor_tensor(fresh[:], blk[:], end[:, E2 - 1:E2].to_broadcast([P, 3]), ALU.is_lt))
                        st.done(dve.tensor_tensor(now[:], now[:], fresh[:], ALU.mult))
                        dve.tensor_tensor(be[:], be[:], now[:], ALU.add)
                        st.done(dve.tensor_scalar(grew[:], nb[:], 1.0, None, ALU.min))
                        st.done(dve.tensor_tensor(jump[:], jump[:], grew[:], ALU.mult))
                        dve.scalar_tensor_tensor(free[:], nb[:], float(P), free[:], ALU.mult, ALU.add)
                        st.done(dve.tensor_tensor(nxt[:], nxt[:], jump[:], ALU.add))
                        dve.tensor_copy(used[:], end[:, E2 - 1:E2])
                        dve.tensor_tensor(nxt[:], tot, nxt[:], ALU.add)
                        st.done(dve.tensor_tensor(free[:], free[:], tot, ALU.subtract))
                        dve.nop(nofuse=True)
                        for t in range(TPB):
                            last = dve.max(top8s[:, t, :], sv[:, t, :])
                        st.done(last)

                    def stage_weights(r, t):
                        n = r * TPB + t
                        wait(dve, sent[t], r * 16 * K2)
                        dve.nop(nofuse=True)
                        dve.tensor_scalar(sidx[:, t, :], top8s[:, t, :], 1.0, None, ALU.subtract)
                        dve.tensor_copy(stage[:, t, :, D:D + 1].rearrange("p k o -> p (k o)"),
                                        ids[:, bass.ds(n, 1), :].rearrange("p o k -> p (o k)"))
                        for k_ in range(K2):
                            last = dve.scalar_tensor_tensor(junk[:, k_], sv[:, t, :], top8s[:, t, k_:k_ + 1],
                                                            score[:, t, :], ALU.is_equal, ALU.mult,
                                                            accum_out=stage[:, t, k_, D + 1:D + 2])
                        last.then_inc(w_staged, 1)
                        dve.wait_ge(w_staged, n + 1)

                    def route_piece(r, i, st):
                        if i == 0:
                            center_z(r)
                        elif i == 2:
                            z_features_1(r)
                        elif i == 3:
                            scores_of(r, st)
                        elif i == 4:
                            choose(r, st)
                        elif i == 5:
                            weigh(r, st)
                        elif i == 6:
                            add_shared(r, 0)
                            slots(r, st)
                        elif i == 7:
                            stage_weights(r, 0)
                            add_shared(r, 1)
                            st.close()

                    dve.wait_ge(made, 5)
                    for zero in (free, used, be):
                        dve.memset(zero[:], 0.0)
                    dve.memset(nxt[:], 1.0)
                    dve.memset(ones64[:], 1.0)
                    dve.tensor_copy(blk[:], blk_i[:])
                    dve.tensor_copy(ids[:], ids_i[:]).then_inc(init, 1)
                    dve.wait_ge(init, 1)

                    st = Steps(dve, dve_step)
                    normalized(0)
                    features_1(0)
                    values_and_queries(0)
                    shift(0, 0, st)
                    row_sums(0, 0, st)

                    def body(b, r, q_, final):
                        st = Steps(dve, dve_step, b, PER, AHEAD)
                        if isinstance(b, int) and b == 1:
                            dve.wait_ge(route_in, FILLS * 16)
                        if r is not None:
                            rst = Steps(dve, route_step, r, ROUTE)
                        for i in range(HB):
                            if i + 1 < HB:
                                shift(b, i + 1, st)
                            if i % 2 == 1 and i >= 3:
                                projected(b, (i - 3) // 2, st)
                            if i == 2 and r is not None:
                                route_piece(r, i, rst)
                            if i + 1 < HB:
                                row_sums(b, i + 1, st)
                            if i > 0:
                                output(b, i - 1)
                            if i + 3 == HB and not final:
                                normalized(b + 1)
                            if i + 2 == HB and not final:
                                features_1(b + 1)
                            if i != 2 and r is not None:
                                route_piece(r, i, rst)
                            if i < 3 and q_ is not None:
                                stage_weights(q_, i + 1)
                        output(b, HB - 1)
                        if not final:
                            values_and_queries(b + 1)
                            shift(b + 1, 0, st)
                        projected(b, TPB - 1, st)
                        if not final:
                            row_sums(b + 1, 0, st)
                            st.close()

                    def last():
                        r = NB - 1
                        rst = Steps(dve, route_step, r, ROUTE)
                        for i in range(HB):
                            route_piece(r, i, rst)
                            if i < 3:
                                stage_weights(r - 1, i + 1)
                        for t in range(1, TPB):
                            stage_weights(r, t)
                        dve.tensor_copy(be_i[:], be[:]).then_inc(tables, 1)
                    steps(dve, body, last)

        def slot_experts():
            ph = ExitStack()
            with ph:
                def sb(name, shape, dt=F32):
                    return ph.enter_context(nc.sbuf_tensor("se_" + name, shape, dt))

                def sem(name):
                    return ctx.enter_context(nc.semaphore("se_" + name))

                XR = 2
                TR = 4
                HOLD = (BT * K2 // P + E2) // GB + TR
                HALVES = NT * 2
                assert HOLD == 28 and HOLD % TR == 0
                be_row = sb("be_row", [1, NBLK], I32)
                xs = sb("xs", [P, XR, GB, ROW])
                xsT = sb("xsT", [P, 2, GB, C, P])
                up = sb("up", [P, 2, GB, C, M2])
                hT = sb("hT", [P, 2, GB, P])
                ys = sb("ys", [P, 2, GB, D])
                yidx = sb("yidx", [P, 2, GB], I32)
                tail = sb("tail", [P, TR, GB, 2])
                got = sb("got", [P, 2, K2 // 2, D])
                part = sb("part", [P, D])
                be_in = sem("be_in")
                x_in = [sem(f"x_in{i}") for i in range(XR)]
                here = [sem("here0"), sem("here1")]
                summed, added, stored = sem("summed"), sem("added"), sem("stored")
                y_out = [sem("y_out0"), sem("y_out1")]
                t_ps, t_act, t_dve, up_ready, z_ps, r_ready, h_ready, y_ps, y_act, y_dve = (
                    sem(n) for n in ("t_ps", "t_act", "t_dve", "up_ready", "z_ps", "r_ready", "h_ready",
                                     "y_ps", "y_act", "y_dve"))
                block = ph.enter_context(nc.Block())
                LAG = 2

                def experts_of(eng, regs, g):
                    eng.load(regs, be_row[0:1, bass.ds(g * GB, GB)])
                    return [eng.snap(reg, min_val=0, max_val=E2 - 1) for reg in regs]

                def pipeline(eng, turn):
                    def plain(first, end):
                        for n in range(first, end):
                            turn(n, n % TR, n // TR, lambda lag, n=n: 0 <= n - lag < NG, n - HOLD if n >= HOLD else None)

                    def loop(first, end, sums):
                        with eng.Fori(first // TR, end // TR) as q:
                            for w in range(TR):
                                turn(q * TR + w, w, q, lambda lag: True, q * TR + w - HOLD if sums else None)
                    plain(0, 2 * TR)
                    loop(2 * TR, HOLD, False)
                    plain(HOLD, HOLD + TR)
                    loop(HOLD + TR, NG, True)
                    plain(NG, HOLD + HALVES)

                def half(q, w, lag):
                    return q * 2 + (w - lag) // 2

                @block.sync
                def _(sp):
                    sp.dma_start(be_row[:], block_expert[0:NBLK].rearrange("(o n) -> o n", o=1)).then_inc(be_in, 16)
                    xv = x_slots.rearrange("(g b p) d -> g p b d", p=P, b=GB)

                    def turn(n, w, q, live, u):
                        if live(0):
                            wait(sp, t_dve, n - XR + 1)
                            sp.dma_start(xs[:, w % XR], xv[bass.ds(n, 1)].rearrange("o p b d -> p (o b) d")
                                         ).then_inc(x_in[w % XR], 16)
                            if isinstance(n, int) and n == 0:
                                sp.dma_start(w_dn[:, EARLY:], down2[:, EARLY:]).then_inc(wd_in, 16)
                        if u is not None:
                            sp.nop(nofuse=True)
                            tile = q * 2 + w // 2 - HOLD // 2
                            if w == 0:
                                done = q * 2 - 2 if not isinstance(q, int) else min(q * 2 - 2, NG // 2)
                                for sent in y_out:
                                    sp.wait_ge(sent, done * 16 * GB)
                                    sp.nop(nofuse=True)
                            wait(sp, summed, u - 1)
                            sp.nop(nofuse=True)
                            sp.dma_start(got[:, w % 2], yv[bass.ds(tile, 1)].rearrange("o p h k d -> p (o h) k d")
                                         [:, w % 2]).then_inc(here[w % 2], 16)
                            if w % 2 == 0 and not (isinstance(u, int) and u < 4):
                                store(tile - 2, u - 2)

                    def store(tile, halves_done):
                        sp.wait_ge(added, halves_done)
                        sp.nop(nofuse=True)
                        sp.dma_start(ov[bass.ds(tile, 1)].rearrange("o p d -> p (o d)"),
                                     acc[:, bass.ds(tile, 1), :].rearrange("p o d -> p (o d)")).then_inc(stored, 16)
                    yv = y_rows.rearrange("(t p h k) d -> t p h k d", p=P, h=2, k=K2 // 2)
                    ov = out.rearrange("(t p) d -> t p d", p=P)
                    pipeline(sp, turn)
                    store(NT - 2, HALVES - 2)
                    store(NT - 1, HALVES)
                    sp.wait_ge(stored, NT * 16)

                @block.gpsimd
                def _(pool):
                    def turn(n, w, q, live, u):
                        if live(2):
                            g = n - 2
                            pool.wait_ge(y_act, g + 1)
                            pool.wait_ge(y_dve, g + 1)
                            pool.nop(nofuse=True)
                            for b in range(GB):
                                pool.indirect_dma_start(
                                    out=y_rows, out_offset=bass.IndirectOffsetOnAxis(ap=yidx[:, w % 2, b:b + 1], axis=0),
                                    in_=ys[:, w % 2, b, :], in_offset=None,
                                    bounds_check=T * K2 - 1, oob_is_err=False).then_inc(y_out[w % 2], 16)
                    pipeline(pool, turn)
                    for w in range(2):
                        pool.wait_ge(y_out[w], NG // 2 * 16 * GB)

                @block.tensor
                def _(pe):
                    pe.wait_ge(be_in, 16)
                    regs = [pe.alloc_register(name=f"expert{i}") for i in range(GB)]

                    def turn(n, w, q, live, u):
                        if live(0):
                            pe.wait_ge(x_in[w % XR], (q * 2 + w // 2 + 1) * 16)
                            wait(pe, t_act, n)
                            wait(pe, t_dve, n)
                            for b in range(GB):
                                for c in range(C):
                                    last = pe.transpose(ps[:, b // 2, (b % 2 * C + c) * P:(b % 2 * C + c + 1) * P],
                                                        xs[:, w % XR, b, c * P:(c + 1) * P], ident[:])
                            last.then_inc(t_ps, 1)
                        if live(1):
                            g = n - 1
                            pe.wait_ge(t_act, g + 1)
                            pe.wait_ge(t_dve, g + 1)
                            pe.wait_ge(up_ready, g + 1)
                            wait(pe, h_ready, g)
                            for b in range(GB):
                                for c in range(C):
                                    last = pe.matmul(ps[:, 2, b * P:(b + 1) * P], up[:, (w - 1) % 2, b, c, :],
                                                     xsT[:, (w - 1) % 2, b, c, :], start=(c == 0), stop=(c == C - 1))
                            last.then_inc(z_ps, 1)
                        if live(2):
                            g = n - 2
                            e = experts_of(pe, regs, g)
                            pe.wait_ge(h_ready, g + 1)
                            if isinstance(g, int) and g == 0:
                                pe.wait_ge(wd_in, 32)
                            wait(pe, y_act, g)
                            wait(pe, y_dve, g)
                            for b in range(GB):
                                last = pe.matmul(ps[:, 4 + b // 2, (b % 2) * D:(b % 2 + 1) * D],
                                                 hT[:, w % 2, b, :],
                                                 w_dn[:, bass.ds(e[b], 1), :].rearrange("p o n -> p (o n)"),
                                                 start=True, stop=True)
                            last.then_inc(y_ps, 1)
                    pipeline(pe, turn)

                @block.scalar
                def _(act):
                    act.wait_ge(be_in, 16)
                    act.wait_ge(w_res, 16)
                    regs = [act.alloc_register(name=f"act_expert{i}") for i in range(GB)]

                    def turn(n, w, q, live, u):
                        if live(0):
                            e = experts_of(act, regs, n)
                            wait(act, z_ps, n - 1)
                            act.nop(nofuse=True)
                            for b in range(GB):
                                last = act.copy(up[:, w % 2, b], w_up[:, bass.ds(e[b], 1)].rearrange("p o c m -> p (o c) m"))
                            last.then_inc(up_ready, 1)
                            act.wait_ge(t_ps, n + 1)
                            act.copy(xsT[:, w % 2, 0:2].rearrange("p b c m -> p (b c m)"), ps[:, 0, :]).then_inc(t_act, 1)
                        if live(1):
                            g = n - 1
                            act.wait_ge(z_ps, g + 1)
                            wait(act, y_ps, g - 1)
                            act.activation(hT[:, (w - 1) % 2].rearrange("p b m -> p (b m)"), ps[:, 2, :], ACT.Relu).then_inc(r_ready, 1)
                        if live(2):
                            g = n - 2
                            act.wait_ge(y_ps, g + 1)
                            wait(act, y_out[w % 2], half(q, w, 2) * 16 * GB)
                            for b in range(2):
                                last = act.activation(ys[:, w % 2, b, :], ps[:, 4, b * D:(b + 1) * D], ACT.Copy,
                                                      scale=tail[:, (w - 2) % TR, b, 1:2])
                            last.then_inc(y_act, 1)
                    pipeline(act, turn)

                @block.vector
                def _(dve):
                    def turn(n, w, q, live, u):
                        if live(0):
                            dve.wait_ge(t_ps, n + 1)
                            wait(dve, z_ps, n - 1)
                            wait(dve, y_act, n - TR + 1)
                            wait(dve, y_dve, n - TR + 1)
                            dve.nop(nofuse=True)
                            dve.tensor_copy(tail[:, w], xs[:, w % XR, :, D:D + 2])
                            dve.tensor_copy(xsT[:, w % 2, 2:4].rearrange("p b c m -> p (b c m)"), ps[:, 1, :]
                                            ).then_inc(t_dve, 1)
                        if live(1):
                            g = n - 1
                            dve.wait_ge(r_ready, g + 1)
                            dve.scalar_tensor_tensor(hT[:, (w - 1) % 2].rearrange("p b m -> p (b m)"), ps[:, 2, :], 0.0,
                                                     hT[:, (w - 1) % 2].rearrange("p b m -> p (b m)"), ALU.max, ALU.mult
                                                     ).then_inc(h_ready, 1)
                        if live(2):
                            g = n - 2
                            dve.wait_ge(y_ps, g + 1)
                            wait(dve, y_out[w % 2], half(q, w, 2) * 16 * GB)
                            dve.tensor_scalar(yidx[:, w % 2, :], tail[:, (w - 2) % TR, :, 0], -1.0, float(T * K2),
                                              ALU.mult, ALU.add)
                            for b in range(2, GB):
                                last = dve.tensor_scalar(ys[:, w % 2, b, :], ps[:, 5, (b - 2) * D:(b - 1) * D],
                                                         tail[:, (w - 2) % TR, b, 1:2], None, ALU.mult)
                            last.then_inc(y_dve, 1)
                        if u is not None:
                            tile = q * 2 + w // 2 - HOLD // 2
                            dve.wait_ge(here[w % 2], (tile + 1) * 16)
                            wait(dve, added, u)
                            dve.tensor_reduce(part[:], got[:, w % 2].rearrange("p k d -> p d k"), AX.X, ALU.add
                                              ).then_inc(summed, 1)
                            dve.wait_ge(summed, u + 1)
                            dve.nop(nofuse=True)
                            a_ = acc[:, bass.ds(tile, 1), :].rearrange("p o d -> p (o d)")
                            dve.tensor_tensor(a_, part[:], a_, ALU.add).then_inc(added, 1)
                    pipeline(dve, turn)

        router1()
        experts()
        halves.close()
        attention1()
        deviations("ln1_")
        up_flat = sb("w_up", [P, E2 * C * M2])
        w_up = up_flat[:].rearrange("p (e c m) -> p e c m", e=E2, c=C)
        w_dn = wide[:].rearrange("p (e n) -> p e n", e=E2)
        w_res, wd_in = sem("w_res"), sem("wd_in")
        attention2()
        slot_experts()


def kernel(x, cond_64, fside_16xSxS_0, mask_BxS_bk0, L0_cond_wt, L0_cond_wg, L0_cond_w_gate, L0_cond_w_up,
           L0_cond_w_down, L0_cond_sw_gate, L0_cond_sw_up, L0_cond_sw_down, L0_attn_Wq, L0_attn_Wk, L0_attn_Wv,
           L0_attn_Wo, L0_attn_rel_emb, L0_cond2_g_in, L0_cond2_null_attn_bias, L0_cond2_Wq, L0_cond2_Wkv,
           L0_cond2_Wo, L0_cond2_g_out, L0_ffn_router_w, L0_ffn_correction_bias, L0_ffn_up_w, L0_ffn_down_w,
           L0_ffn_shared_up_w, L0_ffn_shared_down_w):
    import numpy as _np
    import concourse.bacc as _bacc
    from concourse import mybir as _mybir
    from concourse.bass_utils import run_bass_kernel_spmd as _run

    def arr(a):
        return _np.asarray(a)

    def columns(w, n):
        w = arr(w)
        return w.reshape(w.shape[0], n, w.shape[1] // n).transpose(1, 0, 2)

    def rows(w, n):
        w = arr(w)
        return w.reshape(n, w.shape[0] // n, w.shape[1])

    def up_rows(w):
        return w.reshape(w.shape[0], C, P, w.shape[2]).transpose(2, 0, 1, 3)

    flat = arr(x).reshape(T, D)
    laid = {
        "x": flat,
        "xT": flat.T,
        "condT": arr(cond_64).T,
        "cond": arr(cond_64),
        "bias2": arr(fside_16xSxS_0),
        "mask": arr(mask_BxS_bk0),
        "w1gate": _np.concatenate([arr(L0_cond_w_gate), columns(L0_cond_sw_gate, SH1)]),
        "w1up": _np.concatenate([arr(L0_cond_w_up), columns(L0_cond_sw_up, SH1)]),
        "w1down": _np.concatenate([arr(L0_cond_w_down), rows(L0_cond_sw_down, SH1)]),
        "wtT": arr(L0_cond_wt).T,
        "wgT": arr(L0_cond_wg).T,
        "wqT": arr(L0_attn_Wq).T,
        "wkT": arr(L0_attn_Wk).T,
        "wvT": arr(L0_attn_Wv).T,
        "woT": arr(L0_attn_Wo).T,
        "relT": arr(L0_attn_rel_emb).T,
        "g_in": arr(L0_cond2_g_in).reshape(C, P).T,
        "nbias": arr(L0_cond2_null_attn_bias),
        "wq2": arr(L0_cond2_Wq),
        "wkv2": arr(L0_cond2_Wkv),
        "wo2": arr(L0_cond2_Wo),
        "g_row": arr(L0_cond2_g_out).reshape(1, D),
        "rwT": arr(L0_ffn_router_w).T,
        "cbias": arr(L0_ffn_correction_bias),
        "up2": up_rows(arr(L0_ffn_up_w)),
        "down2": arr(L0_ffn_down_w).transpose(1, 0, 2),
        "up2s": up_rows(columns(L0_ffn_shared_up_w, SH2)),
        "down2s": rows(L0_ffn_shared_down_w, SH2).transpose(1, 0, 2),
    }
    nc = _bacc.Bacc("TRN2", target_bir_lowering=False, num_devices=1)
    arrays, args = {}, {}
    for name, a in laid.items():
        a = _np.ascontiguousarray(a)
        arrays[f"in_{name}"] = a
        args[name] = nc.dram_tensor(f"in_{name}", a.shape, _mybir.dt.from_np(a.dtype), kind="ExternalInput").ap()
    args["out"] = nc.dram_tensor("out_x", (T, D), _mybir.dt.float32, kind="ExternalOutput").ap()
    build(nc, **args)
    r = _run(nc, [arrays], core_ids=[0])
    return r.results[0]["out_x"].reshape(SEQS, S, D)
```
